# Optimizing a Trainium2 kernel written in Bass

```python
import numpy as np
import jax
import jax.numpy as jnp

def _softmax(x, axis=-1):
    return jax.nn.softmax(x, axis=axis)

def _gelu(x):
    return jax.nn.gelu(x, approximate=True)

def _silu(x):
    return jax.nn.silu(x)

def _sigmoid(x):
    return jax.nn.sigmoid(x)

def _layernorm(x, axis=-1, eps=1e-05):
    m = jnp.mean(x, axis=axis, keepdims=True)
    v = jnp.var(x, axis=axis, keepdims=True)
    return (x - m) / jnp.sqrt(v + eps)

def _scatter_add(tgt, idx, src, axis=0):
    return tgt.at[idx].add(src)

def _segment_sum(src, seg, n):
    return jax.ops.segment_sum(src, seg, n)
kernel_name = 'mk_seq_postln_d2_jaxref_r4_b23aff'

def setup_inputs(seed: int=0):
    np.random.seed(seed)
    _w = jnp.asarray

    def _L0_attn_setup():
        import jax, jax.numpy as jnp
        import numpy as np
        D = 256
        H = 16
        S = 512
        B = 2
        LN_EPS = 1e-05
        key = jax.random.key(seed)
        ks = jax.random.split(key, 8)
        x = jax.random.normal(ks[0], (B, S, D), dtype=jnp.float32)
        W_w = jax.random.normal(ks[1], (3 * D, D), dtype=jnp.float32) * 0.02
        W_b = jnp.zeros((3 * D,), dtype=jnp.float32)
        proj_w = jax.random.normal(ks[2], (D, D), dtype=jnp.float32) * 0.02
        proj_b = jnp.zeros((D,), dtype=jnp.float32)
        ln_g = jnp.ones((D,), dtype=jnp.float32)
        ln_b = jnp.zeros((D,), dtype=jnp.float32)
        rpb = jax.random.normal(ks[3], (2 * S - 1, H), dtype=jnp.float32)
        return {'x': x, 'W_w': W_w, 'W_b': W_b, 'proj_w': proj_w, 'proj_b': proj_b, 'ln_g': ln_g, 'ln_b': ln_b, 'rpb': rpb}
    _L0_attn_in = _L0_attn_setup()

    def _L0_ffn_setup():
        import jax, jax.numpy as jnp
        import numpy as np
        B, T, D, R, KEXP = (4, 1024, 256, 64, 8)
        RH = max(D, 32)
        SCALE = 0.02

        def _fused_branch(Q_side, K_side, V, W, U, b, router_w1, router_b1, router_w2, router_b2, expert_bias):
            xV = jnp.einsum('btd,kdr->btkr', Q_side, V)
            yW = jnp.einsum('btd,kdr->btkr', K_side, W)
            cum_yW = jnp.cumsum(yW, axis=1)
            prod = xV * cum_yW
            h = jax.nn.gelu(Q_side @ router_w1.T + router_b1, approximate=False)
            logits = h @ router_w2.T + router_b2 + expert_bias
            weights = jax.nn.softmax(logits, axis=-1)
            out = jnp.einsum('btkr,kdr->btd', prod * weights[..., None], U)
            out = out + weights @ b
            n_valid = jnp.arange(1, Q_side.shape[1] + 1, dtype=Q_side.dtype)
            return out / n_valid[None, :, None]
        key = jax.random.key(seed)
        ks = jax.random.split(key, 20)
        x = jax.random.normal(ks[0], (B, T, D), dtype=jnp.float32)
        W_Q = jax.random.normal(ks[1], (D, D), dtype=jnp.float32) * (1.0 / np.sqrt(D))
        W_K = jax.random.normal(ks[2], (D, D), dtype=jnp.float32) * (1.0 / np.sqrt(D))
        W_O = jax.random.normal(ks[3], (D, D), dtype=jnp.float32) * (1.0 / np.sqrt(D))
        W_inv = jnp.eye(D, dtype=jnp.float32) + 0.01 * jax.random.normal(ks[4], (D, D), dtype=jnp.float32)
        V_fwd = jax.random.normal(ks[5], (KEXP, D, R), dtype=jnp.float32) * SCALE
        W_fwd = jax.random.normal(ks[6], (KEXP, D, R), dtype=jnp.float32) * SCALE
        U_fwd = jax.random.normal(ks[7], (KEXP, D, R), dtype=jnp.float32) * SCALE
        b_fwd = jnp.zeros((KEXP, D), dtype=jnp.float32)
        V_inv = jax.random.normal(ks[8], (KEXP, D, R), dtype=jnp.float32) * SCALE
        W_inv_exp = jax.random.normal(ks[9], (KEXP, D, R), dtype=jnp.float32) * SCALE
        U_inv = jax.random.normal(ks[10], (KEXP, D, R), dtype=jnp.float32) * SCALE
        b_inv = jnp.zeros((KEXP, D), dtype=jnp.float32)
        router_w1 = jax.random.normal(ks[11], (RH, D), dtype=jnp.float32) * (1.0 / np.sqrt(D))
        router_b1 = jnp.zeros((RH,), dtype=jnp.float32)
        router_w2 = jax.random.normal(ks[12], (KEXP, RH), dtype=jnp.float32) * (1.0 / np.sqrt(RH))
        router_b2 = jnp.zeros((KEXP,), dtype=jnp.float32)
        alpha_bi = jnp.asarray(0.5, dtype=jnp.float32)
        expert_bias = jnp.zeros((KEXP,), dtype=jnp.float32)
        return dict(x=x, W_Q=W_Q, W_K=W_K, W_O=W_O, W_inv=W_inv, V_fwd=V_fwd, W_fwd=W_fwd, U_fwd=U_fwd, b_fwd=b_fwd, V_inv=V_inv, W_inv_exp=W_inv_exp, U_inv=U_inv, b_inv=b_inv, router_w1=router_w1, router_b1=router_b1, router_w2=router_w2, router_b2=router_b2, alpha_bi=alpha_bi, expert_bias=expert_bias)
    _L0_ffn_in = _L0_ffn_setup()

    def _L1_attn_setup():
        import jax, jax.numpy as jnp
        import numpy as np
        B, L, D, N = (2, 512, 256, 16)
        DT_MIN, DT_MAX = (0.001, 0.1)
        key = jax.random.key(seed)
        ks = jax.random.split(key, 8)
        u = jax.random.normal(ks[0], (B, L, D), dtype=jnp.float32)
        W_dt = jax.random.normal(ks[1], (D, D), dtype=jnp.float32) * 0.02
        b_dt = jnp.zeros((D,), dtype=jnp.float32)
        W_B = jax.random.normal(ks[2], (D * N, D), dtype=jnp.float32) * 0.02
        b_B = jnp.zeros((D * N,), dtype=jnp.float32)
        W_C = jax.random.normal(ks[3], (D * N, D), dtype=jnp.float32) * 0.02
        b_C = jnp.zeros((D * N,), dtype=jnp.float32)
        log_A = jnp.broadcast_to(jnp.log(jnp.arange(1, N + 1, dtype=jnp.float32)), (D, N))
        D_skip = jnp.ones((D,), dtype=jnp.float32)
        lo, hi = (float(np.log(DT_MIN)), float(np.log(DT_MAX)))
        dt_bias = jax.random.uniform(ks[4], (D,), dtype=jnp.float32) * (hi - lo) + lo
        return {'u': u, 'log_A': log_A, 'D_skip': D_skip, 'dt_bias': dt_bias, 'W_dt': W_dt, 'b_dt': b_dt, 'W_B': W_B, 'b_B': b_B, 'W_C': W_C, 'b_C': b_C}
    _L1_attn_in = _L1_attn_setup()

    def _L1_ffn_setup():
        import jax, jax.numpy as jnp
        import numpy as np
        B, S, D, DO = (4, 512, 256, 256)
        E, K = (20, 2)
        key = jax.random.key(seed)
        ks = jax.random.split(key, 6)
        sc_d = 1.0 / np.sqrt(D)
        sc_h = 1.0 / np.sqrt(D // 4)
        return {'x': jax.random.normal(ks[0], (B, S, D), jnp.float32), 'wg1': jax.random.normal(ks[1], (D, D // 4), jnp.float32) * sc_d, 'bg1': jnp.zeros((D // 4,), jnp.float32), 'wg2': jax.random.normal(ks[2], (D // 4, 2 * E), jnp.float32) * sc_h, 'bg2': jnp.zeros((2 * E,), jnp.float32), 'We': jax.random.normal(ks[3], (E, D, DO), jnp.float32) * sc_d, 'be': jnp.zeros((E, DO), jnp.float32)}
    _L1_ffn_in = _L1_ffn_setup()
    _d = {'L0_attn_x': _L0_attn_in['x'], 'L0_attn_W_w': _L0_attn_in['W_w'], 'L0_attn_W_b': _L0_attn_in['W_b'], 'L0_attn_proj_w': _L0_attn_in['proj_w'], 'L0_attn_proj_b': _L0_attn_in['proj_b'], 'L0_attn_ln_g': _L0_attn_in['ln_g'], 'L0_attn_ln_b': _L0_attn_in['ln_b'], 'L0_attn_rpb': _L0_attn_in['rpb'], 'L0_ffn_W_Q': _L0_ffn_in['W_Q'], 'L0_ffn_W_K': _L0_ffn_in['W_K'], 'L0_ffn_W_O': _L0_ffn_in['W_O'], 'L0_ffn_W_inv': _L0_ffn_in['W_inv'], 'L0_ffn_V_fwd': _L0_ffn_in['V_fwd'], 'L0_ffn_W_fwd': _L0_ffn_in['W_fwd'], 'L0_ffn_U_fwd': _L0_ffn_in['U_fwd'], 'L0_ffn_b_fwd': _L0_ffn_in['b_fwd'], 'L0_ffn_V_inv': _L0_ffn_in['V_inv'], 'L0_ffn_W_inv_exp': _L0_ffn_in['W_inv_exp'], 'L0_ffn_U_inv': _L0_ffn_in['U_inv'], 'L0_ffn_b_inv': _L0_ffn_in['b_inv'], 'L0_ffn_router_w1': _L0_ffn_in['router_w1'], 'L0_ffn_router_b1': _L0_ffn_in['router_b1'], 'L0_ffn_router_w2': _L0_ffn_in['router_w2'], 'L0_ffn_router_b2': _L0_ffn_in['router_b2'], 'L0_ffn_alpha_bi': _L0_ffn_in['alpha_bi'], 'L0_ffn_expert_bias': _L0_ffn_in['expert_bias'], 'L1_attn_log_A': _L1_attn_in['log_A'], 'L1_attn_D_skip': _L1_attn_in['D_skip'], 'L1_attn_dt_bias': _L1_attn_in['dt_bias'], 'L1_attn_W_dt': _L1_attn_in['W_dt'], 'L1_attn_b_dt': _L1_attn_in['b_dt'], 'L1_attn_W_B': _L1_attn_in['W_B'], 'L1_attn_b_B': _L1_attn_in['b_B'], 'L1_attn_W_C': _L1_attn_in['W_C'], 'L1_attn_b_C': _L1_attn_in['b_C'], 'L1_ffn_wg1': _L1_ffn_in['wg1'], 'L1_ffn_bg1': _L1_ffn_in['bg1'], 'L1_ffn_wg2': _L1_ffn_in['wg2'], 'L1_ffn_bg2': _L1_ffn_in['bg2'], 'L1_ffn_We': _L1_ffn_in['We'], 'L1_ffn_be': _L1_ffn_in['be']}
    _x0 = _d['L0_attn_x']
    _d['L0_attn_x'] = jax.random.normal(jax.random.fold_in(jax.random.key(seed), 1), (2, 2048, 256), dtype=_x0.dtype)
    del _x0
    return _d

def reference(L0_attn_x, L0_attn_W_w, L0_attn_W_b, L0_attn_proj_w, L0_attn_proj_b, L0_attn_ln_g, L0_attn_ln_b, L0_attn_rpb, L0_ffn_W_Q, L0_ffn_W_K, L0_ffn_W_O, L0_ffn_W_inv, L0_ffn_V_fwd, L0_ffn_W_fwd, L0_ffn_U_fwd, L0_ffn_b_fwd, L0_ffn_V_inv, L0_ffn_W_inv_exp, L0_ffn_U_inv, L0_ffn_b_inv, L0_ffn_router_w1, L0_ffn_router_b1, L0_ffn_router_w2, L0_ffn_router_b2, L0_ffn_alpha_bi, L0_ffn_expert_bias, L1_attn_log_A, L1_attn_D_skip, L1_attn_dt_bias, L1_attn_W_dt, L1_attn_b_dt, L1_attn_W_B, L1_attn_b_B, L1_attn_W_C, L1_attn_b_C, L1_ffn_wg1, L1_ffn_bg1, L1_ffn_wg2, L1_ffn_bg2, L1_ffn_We, L1_ffn_be):

    def _L0_attn_ref(x, W_w, W_b, proj_w, proj_b, ln_g, ln_b, rpb):
        import jax, jax.numpy as jnp
        import numpy as np
        D = 256
        H = 16
        S = 512
        B = 2
        LN_EPS = 1e-05
        b, s, d = x.shape
        hd = d // H
        qkv = x @ W_w.T + W_b
        q, k, v = jnp.split(qkv, 3, axis=-1)
        q, k, v = (z.reshape(b, s, H, hd).transpose(0, 2, 1, 3) for z in (q, k, v))
        attn = jnp.einsum('bhqd,bhkd->bhqk', q, k) / jnp.sqrt(jnp.float32(d))
        causal = jnp.triu(jnp.ones((s, s), dtype=bool), k=1)
        attn = jnp.where(causal[None, None], -jnp.inf, attn)
        rel_idx = jnp.arange(s)[None, :] - jnp.arange(s)[:, None] + (s - 1)
        bias = rpb[rel_idx].transpose(2, 0, 1)
        attn = attn + bias[None]
        w = jax.nn.softmax(attn, axis=-1)
        o = jnp.einsum('bhqk,bhkd->bhqd', w, v)
        o = o.transpose(0, 2, 1, 3).reshape(b, s, d)
        out = o @ proj_w.T + proj_b
        y = x + out
        mu = jnp.mean(y, axis=-1, keepdims=True)
        var = jnp.var(y, axis=-1, keepdims=True)
        return (y - mu) / jnp.sqrt(var + LN_EPS) * ln_g + ln_b

    def _L0_ffn_ref(x, W_Q, W_K, W_O, W_inv, V_fwd, W_fwd, U_fwd, b_fwd, V_inv, W_inv_exp, U_inv, b_inv, router_w1, router_b1, router_w2, router_b2, alpha_bi, expert_bias):
        import jax, jax.numpy as jnp
        import numpy as np
        B, T, D, R, KEXP = (4, 1024, 256, 64, 8)
        RH = max(D, 32)
        SCALE = 0.02

        def _fused_branch(Q_side, K_side, V, W, U, b, router_w1, router_b1, router_w2, router_b2, expert_bias):
            xV = jnp.einsum('btd,kdr->btkr', Q_side, V)
            yW = jnp.einsum('btd,kdr->btkr', K_side, W)
            cum_yW = jnp.cumsum(yW, axis=1)
            prod = xV * cum_yW
            h = jax.nn.gelu(Q_side @ router_w1.T + router_b1, approximate=False)
            logits = h @ router_w2.T + router_b2 + expert_bias
            weights = jax.nn.softmax(logits, axis=-1)
            out = jnp.einsum('btkr,kdr->btd', prod * weights[..., None], U)
            out = out + weights @ b
            n_valid = jnp.arange(1, Q_side.shape[1] + 1, dtype=Q_side.dtype)
            return out / n_valid[None, :, None]
        Q = x @ W_Q.T
        K = x @ W_K.T
        invQ = Q @ W_inv.T
        invK = K @ W_inv.T
        fwd = _fused_branch(Q, K, V_fwd, W_fwd, U_fwd, b_fwd, router_w1, router_b1, router_w2, router_b2, expert_bias)
        inv = _fused_branch(invQ, invK, W_inv_exp, V_inv, U_inv, b_inv, router_w1, router_b1, router_w2, router_b2, expert_bias)
        out = fwd + alpha_bi * inv
        return out @ W_O.T

    def _L1_attn_ref(u, log_A, D_skip, dt_bias, W_dt, b_dt, W_B, b_B, W_C, b_C):
        import jax, jax.numpy as jnp
        import numpy as np
        B, L, D, N = (2, 512, 256, 16)
        DT_MIN, DT_MAX = (0.001, 0.1)
        b, l, d = u.shape
        n = log_A.shape[1]
        A = -jnp.exp(log_A)
        dt = jax.nn.softplus(u @ W_dt.T + b_dt + dt_bias)
        Bt = (u @ W_B.T + b_B).reshape(b, l, d, n)
        Ct = (u @ W_C.T + b_C).reshape(b, l, d, n)
        A_bar = jnp.exp(dt[..., None] * A)
        B_bar = (A_bar - 1.0) / A * Bt
        x_in = B_bar * u[..., None]

        def step(h, inp):
            a_t, x_t, c_t = inp
            h = a_t * h + x_t
            y_t = jnp.sum(c_t * h, axis=-1)
            return (h, y_t)
        h0 = jnp.zeros((b, d, n), dtype=u.dtype)
        xs = (jnp.moveaxis(A_bar, 1, 0), jnp.moveaxis(x_in, 1, 0), jnp.moveaxis(Ct, 1, 0))
        _, ys = jax.lax.scan(step, h0, xs)
        y = jnp.moveaxis(ys, 0, 1) + D_skip * u
        return y

    def _L1_ffn_ref(x, wg1, bg1, wg2, bg2, We, be):
        import jax, jax.numpy as jnp
        import numpy as np
        B, S, D, DO = (4, 512, 256, 256)
        E, K = (20, 2)
        Bv, Sv, Dv = x.shape
        xf = x.reshape(-1, Dv)
        h = jax.nn.gelu(xf @ wg1 + bg1, approximate=False)
        logits = (xf @ 0.0 + (h @ wg2 + bg2))[:, :E] if False else (h @ wg2 + bg2)[:, :E]
        probs = jax.nn.softmax(logits, axis=-1)
        top_vals, top_idx = jax.lax.top_k(probs, K)
        N = xf.shape[0]
        gates = jnp.zeros((N, E), xf.dtype).at[jnp.arange(N)[:, None], top_idx].set(top_vals)

        def body(y, eb):
            We_e, be_e, g_e = eb
            return (y + g_e[:, None] * (xf @ We_e + be_e), None)
        y0 = jnp.zeros((N, be.shape[-1]), xf.dtype)
        y, _ = jax.lax.scan(body, y0, (We, be, gates.T))
        return y.reshape(Bv, Sv, -1)
    x = L0_attn_x
    x = _layernorm(x + _L0_attn_ref(x, L0_attn_W_w, L0_attn_W_b, L0_attn_proj_w, L0_attn_proj_b, L0_attn_ln_g, L0_attn_ln_b, L0_attn_rpb), axis=-1)
    x = _layernorm(x + _L0_ffn_ref(x, L0_ffn_W_Q, L0_ffn_W_K, L0_ffn_W_O, L0_ffn_W_inv, L0_ffn_V_fwd, L0_ffn_W_fwd, L0_ffn_U_fwd, L0_ffn_b_fwd, L0_ffn_V_inv, L0_ffn_W_inv_exp, L0_ffn_U_inv, L0_ffn_b_inv, L0_ffn_router_w1, L0_ffn_router_b1, L0_ffn_router_w2, L0_ffn_router_b2, L0_ffn_alpha_bi, L0_ffn_expert_bias), axis=-1)
    x = _layernorm(x + _L1_attn_ref(x, L1_attn_log_A, L1_attn_D_skip, L1_attn_dt_bias, L1_attn_W_dt, L1_attn_b_dt, L1_attn_W_B, L1_attn_b_B, L1_attn_W_C, L1_attn_b_C), axis=-1)
    x = _layernorm(x + _L1_ffn_ref(x, L1_ffn_wg1, L1_ffn_bg1, L1_ffn_wg2, L1_ffn_bg2, L1_ffn_We, L1_ffn_be), axis=-1)
    return x

_drawn_inputs = setup_inputs


def setup_inputs(seed=0):
    import zlib

    import numpy as np

    out = dict(_drawn_inputs(seed))
    spreads = {'L0_attn_W_b': (0.0, 0.293),
     'L0_attn_proj_b': (0.0, 0.1),
     'L0_attn_ln_g': (1.0, 0.2),
     'L0_attn_ln_b': (0.0, 0.1),
     'L0_ffn_b_fwd': (0.0, 2.0),
     'L0_ffn_b_inv': (0.0, 2.0),
     'L0_ffn_router_b1': (0.0, 0.8),
     'L0_ffn_router_b2': (0.0, 2.0),
     'L0_ffn_expert_bias': (0.0, 2.0),
     'L1_attn_D_skip': (1.0, 0.2),
     'L1_attn_b_dt': (0.0, 2.0),
     'L1_attn_b_B': (0.0, 0.8),
     'L1_attn_b_C': (0.0, 2.0),
     'L1_ffn_bg1': (0.0, 0.1),
     'L1_ffn_bg2': (0.0, 0.1),
     'L1_ffn_be': (0.0, 0.431)}
    factors = {'L0_attn_W_w': 7.127,
     'L0_attn_rpb': 8.0,
     'L0_ffn_W_Q': 8.0,
     'L0_ffn_W_K': 8.0,
     'L0_ffn_W_O': 8.0,
     'L0_ffn_W_inv': 8.0,
     'L0_ffn_V_fwd': 8.0,
     'L0_ffn_W_fwd': 8.0,
     'L0_ffn_U_fwd': 8.0,
     'L0_ffn_V_inv': 8.0,
     'L0_ffn_W_inv_exp': 8.0,
     'L0_ffn_U_inv': 8.0,
     'L0_ffn_router_w1': 8.0,
     'L0_ffn_router_w2': 8.0,
     'L1_attn_log_A': 3.831,
     'L1_attn_dt_bias': 3.786,
     'L1_attn_W_dt': 5.698,
     'L1_attn_W_B': 2.934,
     'L1_attn_W_C': 2.84}
    for name, (base, spread) in spreads.items():
        noise = np.random.default_rng([zlib.crc32(name.encode()), seed]).standard_normal(out[name].shape)
        drawn = base * np.exp(spread * noise) if base else spread * noise
        out[name] = jnp.asarray(drawn.astype(out[name].dtype))
    for name, factor in factors.items():
        out[name] = (out[name] * factor).astype(out[name].dtype)
    return out
```

```python
from contextlib import ExitStack

import concourse.bass as bass
import concourse.mybir as mybir

ALU = mybir.AluOpType
ACT = mybir.ActivationFunctionType
AX = mybir.AxisListType.X
F32 = mybir.dt.float32
BF16 = mybir.dt.bfloat16
F32R = mybir.dt.float32r
U32 = mybir.dt.uint32

P = 128
B, S, D = 2, 2048, 256
NTOK = B * S
KT = D // P
CH = 512
NCH = NTOK // CH
TPC = CH // P
NT = NTOK // P
TB = S // P
H = 16
HD = D // H
RPB = 1023
EW = 1152
EPS = 1e-5
START = 1


def ds(start, size):
    return bass.ds(start, size)


class Steps:

    def __init__(self, eng, sem):
        self.eng, self.sem, self.base, self.n = eng, sem, 0, 0

    def __call__(self, ins):
        ins.then_inc(self.sem, 1)
        self.n += 1
        self.eng.wait_ge(self.sem, self.base + self.n)

    def go(self, ins):
        ins.then_inc(self.sem, 1)
        self.n += 1

    def wait(self):
        self.eng.wait_ge(self.sem, self.base + self.n)

    def enter(self, i, per):
        self.start, self.per = self.base + self.n, per
        self.base, self.n = i * per + self.start, 0

    def leave(self, times):
        assert self.n == self.per, f"{self.n} steps in the body, {self.per} stated"
        self.base, self.n = self.start + times * self.per, 0


def after(eng, sem, value):
    if not isinstance(value, int) or value > 0:
        eng.wait_ge(sem, value)


class Space:

    def __init__(self, nc, ctx, prefix):
        self.nc, self.ctx, self.prefix = nc, ctx, prefix

    def sb(self, name, shape, dt=F32):
        return self.ctx.enter_context(self.nc.sbuf_tensor(f"{self.prefix}_{name}", shape, dt))

    def psum(self, name, shape, dt=F32):
        return self.ctx.enter_context(self.nc.psum_tensor(f"{self.prefix}_{name}", shape, dt))

    def sem(self, name):
        return self.nc.alloc_semaphore(f"{self.prefix}_{name}")


def phase_qkv(nc, t):
    with nc.cleanup_on_exit(), ExitStack() as ctx:
        sp = Space(nc, ctx, "qkv")
        w = sp.sb("w", [P, KT, 3 * D])
        bqk = sp.sb("bqk", [P, 4])
        bqs = sp.sb("bqs", [P, 2])
        bv = sp.sb("bv", [P, D])
        x = [sp.sb(f"x{s}", [P, KT, CH]) for s in range(2)]
        whole = sp.sb("whole", [P, 4, CH])
        rest = sp.sb("rest", [P, 2, CH])
        parts = [sp.sb(f"parts{s}", [P, 4, 3, CH], BF16) for s in range(2)]
        tab = sp.sb("tab", [H, 2, EW])
        clamped = sp.sb("clamped", [H, 1])
        tabrest = sp.sb("tabrest", [H, EW])
        tabparts = sp.sb("tabparts", [H, 4, EW], BF16)
        qk_ps = sp.psum("qk_ps", [P, 4, CH])
        v_ps = sp.psum("v_ps", [P, 4, CH])

        w_loaded, tab_loaded = sp.sem("w_loaded"), sp.sem("tab_loaded")
        x_loaded = [sp.sem(f"x_loaded{s}") for s in range(2)]
        qk_ready, qk_turns = sp.sem("qk_ready"), sp.sem("qk_turns")
        v_ready, v_turns = sp.sem("v_ready"), sp.sem("v_turns")
        whole_turns = sp.sem("whole_turns")
        whole_ready = sp.sem("whole_ready")
        parts_ready = sp.sem("parts_ready")
        stored = [sp.sem(f"stored{s}") for s in range(2)]
        tab_ready, tab_stored = sp.sem("tab_ready"), sp.sem("tab_stored")
        dve_step, act_step, tab_zeroed = sp.sem("dve_step"), sp.sem("act_step"), sp.sem("tab_zeroed")
        block = ctx.enter_context(nc.Block())

        @block.sync
        def _(eng):
            eng.sem_inc(stored[0], START)
            eng.sem_inc(stored[1], START)
            for dst, src in ((w, t.wqkv), (bqk, t.bqk), (bv, t.bv)):
                eng.dma_start(dst[:], src).then_inc(w_loaded, 16)
            eng.wait_ge(tab_zeroed, 1)
            eng.dma_start(tab[:, 0, 0:RPB], t.rpb).then_inc(tab_loaded, 16)
            eng.dma_start(tab[:, 1, P:P + RPB], t.rpb_back).then_inc(tab_loaded, 16)

            def load(c, s):
                eng.dma_start(x[s][:], t.xT[:, :, ds(c * CH, CH)]).then_inc(x_loaded[s], 16)

            def store(c, s):
                for m in range(4):
                    eng.wait_ge(parts_ready, 4 * c + m + 1)
                    eng.dma_start(t.qk[m // 2, :, (m % 2) * P:(m % 2 + 1) * P, ds(c * CH, CH)].rearrange("a p n -> p a n"),
                                  parts[s][:, m]).then_inc(stored[s], 16)

            for s in range(2):
                load(s, s)
            eng.wait_ge(tab_ready, 1)
            eng.dma_start(t.tables.rearrange("a h e -> h a e"), tabparts[:]).then_inc(tab_stored, 16)
            with eng.Fori(0, NCH // 2 - 1) as i:
                for s in range(2):
                    eng.wait_ge(v_ready, 4 * (2 * i + s) + 4)
                    load(2 * i + s + 2, s)
                for s in range(2):
                    store(2 * i + s, s)
            for s in range(2):
                store(NCH - 2 + s, s)
            for s in range(2):
                eng.wait_ge(stored[s], 64 * (NCH // 2) + START)
            eng.wait_ge(tab_stored, 16)

        @block.gpsimd
        def _(eng):
            nc.gpsimd.memset(tab[:], 0.0).then_inc(tab_zeroed, 1)

        @block.tensor
        def _(eng):
            eng.wait_ge(w_loaded, 48)
            with eng.Fori(0, NCH // 2) as i:
                for s in range(2):
                    c = 2 * i + s
                    eng.wait_ge(x_loaded[s], 16 * i + 16)
                    for m in range(4):
                        eng.wait_ge(qk_turns, 4 * c + m + 1)
                        for k in range(KT):
                            mm = nc.tensor.matmul(qk_ps[:, m], w[:, k, m * P:(m + 1) * P], x[s][:, k],
                                                  start=k == 0, stop=k == KT - 1)
                        mm.then_inc(qk_ready, 1)
                    for j in range(TPC):
                        eng.wait_ge(v_turns, 4 * c + j + 1)
                        for k in range(KT):
                            mm = nc.tensor.matmul(v_ps[:, j, 0:D], x[s][:, k, j * P:(j + 1) * P],
                                                  w[:, k, 2 * D:], start=k == 0, stop=k == KT - 1)
                        mm.then_inc(v_ready, 1)

        @block.scalar
        def _(eng):
            eng.sem_inc(qk_turns, 4)
            eng.wait_ge(w_loaded, 48)
            nc.scalar.mul(bqs[:], bqk[:, 0:2], 1.0 / HD).then_inc(act_step, 1)
            eng.wait_ge(act_step, 1)
            with eng.Fori(0, NCH // 2) as i:
                for s in range(2):
                    c = 2 * i + s
                    for m in range(4):
                        eng.wait_ge(qk_ready, 4 * c + m + 1)
                        eng.wait_ge(whole_turns, 4 * c + m + 1)
                        nc.scalar.activation(whole[:, m], qk_ps[:, m], ACT.Identity,
                                             bias=bqs[:, m:m + 1] if m < 2 else bqk[:, m:m + 1],
                                             scale=1.0 / HD if m < 2 else 1.0).then_inc(qk_turns, 1)

        @block.vector
        def _(eng):
            step = Steps(eng, dve_step)
            eng.sem_inc(whole_turns, 4)
            eng.sem_inc(v_turns, 4)
            eng.wait_ge(w_loaded, 48)
            eng.wait_ge(tab_loaded, 32)
            step(nc.vector.tensor_copy(clamped[:], tab[:, 0, RPB - 1:RPB]))
            step(nc.vector.tensor_scalar(tab[:, 0, 0:RPB], tab[:, 0, 0:RPB], clamped[:, 0:1], None, ALU.subtract))
            step(nc.vector.tensor_scalar(tab[:, 1, P:P + RPB], tab[:, 1, P:P + RPB], clamped[:, 0:1], None, ALU.subtract))
            step(nc.vector.tensor_copy(tabparts[:, 0], tab[:, 0]))
            step(nc.vector.tensor_copy(tabparts[:, 1], tab[:, 1]))
            step(nc.vector.tensor_tensor(tabrest[:], tab[:, 1], tabparts[:, 1], ALU.subtract))
            step(nc.vector.tensor_copy(tabparts[:, 2], tabrest[:]))
            nc.vector.tensor_tensor(tabparts[:, 3], tabrest[:], tabparts[:, 2], ALU.subtract).then_inc(tab_ready, 1)
            with eng.Fori(0, NCH // 2) as i:
                step.enter(i, 2 * 4 * 3)
                for s in range(2):
                    c = 2 * i + s
                    eng.wait_ge(stored[s], 64 * i + START)
                    for m in range(4):
                        p = parts[s]
                        eng.wait_ge(qk_turns, 4 * c + m + 5)
                        step(nc.vector.tensor_copy(p[:, m, 0], whole[:, m]))
                        step(nc.vector.tensor_tensor(rest[:, m % 2], whole[:, m], p[:, m, 0], ALU.subtract))
                        eng.sem_inc(whole_turns, 1)
                        step(nc.vector.tensor_copy(p[:, m, 1], rest[:, m % 2]))
                        nc.vector.tensor_tensor(p[:, m, 2], rest[:, m % 2], p[:, m, 1],
                                                ALU.subtract).then_inc(parts_ready, 1)
                        eng.wait_ge(parts_ready, 4 * c + m + 1)
                    for j in range(TPC):
                        eng.wait_ge(v_ready, 4 * c + j + 1)
                        nc.vector.tensor_tensor(t.v_sb[:, ds(c * TPC + j, 1), :], v_ps[:, j, 0:D].unsqueeze(1),
                                                bv[:].unsqueeze(1), ALU.add).then_inc(v_turns, 1)
                step.leave(NCH // 2)


def attention_pieces(J):
    return [(q, min(q + 2 * CH, S)) for q in range(J * P, S, 2 * CH)]


PIECES = [len(attention_pieces(J)) for J in range(TB)]
GROUPS = [(I * P + P + CH - 1) // CH for I in range(TB)]
NP2, NG1 = sum(PIECES), sum(GROUPS)
FAR = 8
QUAD = 4
ROWS = 6 * HD


def phase_attention(nc, t):
    with nc.cleanup_on_exit(), ExitStack() as ctx:
        sp = Space(nc, ctx, "att")
        qs = [sp.sb(f"qs{s}", [P, S], BF16) for s in range(QUAD)]
        ks = [sp.sb(f"ks{s}", [P, S], BF16) for s in range(QUAD)]
        near = [sp.sb(f"near{s}", [P, 8 * P], BF16) for s in range(2)]
        far = [sp.sb(f"far{s}", [P, 3, 8 * P], BF16) for s in range(2)]
        prob = sp.sb("prob", [P, 4, S])
        vst = [sp.sb(f"vst{s}", [P, TB, 32]) for s in range(2)]
        partmax = sp.sb("partmax", [P, TB, 4])
        mx = sp.sb("mx", [P, TB])
        negmax = sp.sb("negmax", [P, 2, TB], BF16)
        negmaxT = [sp.sb(f"negmaxT{s}", [2 * TB, P], BF16) for s in range(2)]
        oT = sp.sb("oT", [P, CH])
        rsum = sp.sb("rsum", [P, 4, 4])
        squares = sp.sb("squares", [P, 4, P])
        squares_b = sp.sb("squares_b", [P, 4, P], BF16)
        ident = squares[:, 0]
        idb, flip, maskq, maskk = (squares_b[:, n] for n in range(4))
        s1 = sp.psum("s1", [P, 2, CH])
        s2 = sp.psum("s2", [P, 2, 2 * CH])
        o_ps = sp.psum("o_ps", [P, CH])
        turn = sp.psum("turn", [P, CH])

        const_loaded, const_cast = sp.sem("const_loaded"), sp.sem("const_cast")
        stack_loaded = [sp.sem(f"stack_loaded{s}") for s in range(QUAD)]
        near_loaded = [sp.sem(f"near_loaded{s}") for s in range(2)]
        far_loaded = [sp.sem(f"far_loaded{s}") for s in range(2)]
        max_loaded = [sp.sem(f"max_loaded{s}") for s in range(QUAD)]
        s1_ready = sp.sem("s1_ready")
        s1_turns = sp.sem("s1_turns")
        s2_ready = sp.sem("s2_ready")
        s2_turns = sp.sem("s2_turns")
        prob_turns = sp.sem("prob_turns")
        vst_turns = sp.sem("vst_turns")
        vst_ready = sp.sem("vst_ready")
        negmax_ready = sp.sem("negmax_ready")
        negmaxT_ready = sp.sem("negmaxT_ready")
        turn_ready = sp.sem("turn_ready")
        turn_free = sp.sem("turn_free")
        oT_ready = sp.sem("oT_ready")
        pool_set = sp.sem("pool_set")
        dve_step = sp.sem("dve_step")
        block = ctx.enter_context(nc.Block())
        NQ = B * H // QUAD

        def window(part, h):
            at = t.tables[part, ds(h, 1), 0:1]
            return bass.AP(tensor=at.tensor, offset=at.offset, ap=[[1, P], [1, 8 * P]])

        @block.sync
        def _(eng):
            eng.sem_inc(max_loaded[0], START)
            eng.sem_inc(max_loaded[1], START)
            eng.sem_inc(max_loaded[2], START)
            eng.sem_inc(max_loaded[3], START)
            eng.dma_start(squares[:], t.squares).then_inc(const_loaded, 16)

            def load_stack(h, b, s):
                tok = slice(b * S, (b + 1) * S)
                for n, (lo, parts) in enumerate(((0, "111"), (3, "22"), (5, "3"))):
                    for r, part in enumerate(parts):
                        eng.dma_start(qs[s][(lo + r) * HD:(lo + r + 1) * HD, :],
                                      t.qk4[0, int(part) - 1, ds(h, 1), :, tok].rearrange("a r n -> (a r) n")).then_inc(stack_loaded[s], 16)
                for lo, num in ((0, 3), (3, 2), (5, 1)):
                    eng.dma_start(ks[s][lo * HD:(lo + num) * HD, :],
                                  t.qk4[1, 0:num, ds(h, 1), :, tok].rearrange("c a r n -> c (a r) n")).then_inc(stack_loaded[s], 16)

            def load_near(h, s):
                eng.dma_start(near[s][:], window(0, h)).then_inc(near_loaded[s], 16)

            def load_far(h, s):
                for part in range(3):
                    eng.dma_start(far[s][:, part], window(1 + part, h)).then_inc(far_loaded[s], 16)

            def store_max(v, i, k):
                eng.wait_ge(negmaxT_ready, v + 1)
                for a in range(2):
                    eng.dma_start(qs[k][ROWS + a:ROWS + a + 1, :],
                                  negmaxT[k % 2][a * TB:(a + 1) * TB, :]).then_inc(max_loaded[k], 16)

            load_near(0, 0)
            load_stack(0, 0, 0)
            load_stack(0, 1, 1)
            load_far(0, 0)
            load_stack(1, 0, 2)
            load_near(1, 1)
            store_max(0, 0, 0)

            def units(i, last):
                for k in range(QUAD):
                    u = QUAD * i + k
                    eng.wait_ge(s2_ready, NP2 * u + START)
                    if k % 2 == 0:
                        h = 2 * i + k // 2
                        if not (last and k == 2):
                            load_far(h + 1, (k // 2 + 1) % 2)
                        if not last:
                            eng.wait_ge(s1_ready, NG1 * (u + 2))
                            load_near(h + 2, k // 2)
                    if not last or k == 0:
                        load_stack(2 * i + (k + 3) // 2, (k + 3) % 2, (k + 3) % QUAD)
                    if not last or k < 3:
                        store_max(u + 1, i, (k + 1) % QUAD)

            with eng.Fori(0, NQ - 1) as i:
                units(i, False)
            units(NQ - 1, True)

        @block.gpsimd
        def _(eng):
            step = Steps(eng, pool_set)
            for s in range(QUAD):
                step(nc.gpsimd.memset(ks[s][ROWS:ROWS + 2, :], 1.0))
            for s in range(2):
                step(nc.gpsimd.memset(vst[s][:, :, 16:17], 1.0))
                step(nc.gpsimd.memset(vst[s][:, :, 17:32], 0.0))
            with eng.Fori(0, NQ) as i:
                for k in range(QUAD):
                    u = QUAD * i + k
                    b = k % 2
                    eng.wait_ge(vst_turns, u + 1)
                    nc.gpsimd.tensor_copy(vst[b][:, :, 0:HD],
                                          t.v_sb[:, b * TB:(b + 1) * TB, ds((2 * i + k // 2) * HD, HD)]).then_inc(vst_ready, 1)

        @block.tensor
        def _(eng):
            eng.sem_inc(s2_ready, START)
            eng.sem_inc(vst_turns, 2)
            eng.sem_inc(prob_turns, 4)
            eng.wait_ge(const_loaded, 16)
            eng.wait_ge(const_cast, 1)
            eng.wait_ge(pool_set, 8)

            def maxima(v, s, hs, I, banks=None):
                before = sum(GROUPS[I + 1:])
                for g in range(GROUPS[I]) if banks is None else banks:
                    n = NG1 * v + before + g
                    lo, hi = g * CH, min(g * CH + CH, (I + 1) * P)
                    bank = s1[:, (before + g) % 2]
                    eng.wait_ge(s1_turns, n + 1)
                    last = hi == (I + 1) * P
                    near_hi = min(hi, (I - FAR + 1) * P)
                    mm = nc.tensor.matmul(bank[:, 0:hi - lo], qs[s][0:ROWS, I * P:(I + 1) * P],
                                          ks[s][0:ROWS, lo:hi], start=True,
                                          stop=not last and near_hi <= lo)
                    if near_hi > lo:
                        at = 15 * P - I * P + lo
                        mm = nc.tensor.matmul(bank[:, 0:near_hi - lo], flip, near[hs][:, at:at + near_hi - lo],
                                              start=False, stop=not last)
                    if last:
                        mm = nc.tensor.matmul(bank[:, I * P - lo:hi - lo], idb, maskq, start=False, stop=True)
                    mm.then_inc(s1_ready, 1)

            def scores(u, s, hs, J, n):
                before = sum(PIECES[:J])
                if n < PIECES[J]:
                    q0, q1 = attention_pieces(J)[n]
                    slot = s2[:, (before + n) % 2]
                    eng.wait_ge(s2_turns, NP2 * u + before + n + 1)
                    for lo in range(q0, q1, CH):
                        hi = min(lo + CH, q1)
                        col = lo - q0
                        far_lo = max(lo, (J + FAR) * P)
                        has_far, has_mask = far_lo < hi, lo == J * P
                        mm = nc.tensor.matmul(slot[:, col:col + hi - lo], ks[s][0:ROWS + 2, J * P:(J + 1) * P],
                                              qs[s][0:ROWS + 2, lo:hi], start=True, stop=not (has_far or has_mask))
                        if has_far:
                            at = far_lo - (J + FAR) * P
                            for part in range(3):
                                mm = nc.tensor.matmul(slot[:, far_lo - q0:hi - q0], flip,
                                                      far[hs][:, part, at:at + hi - far_lo], start=False,
                                                      stop=part == 2 and not has_mask)
                        if has_mask:
                            mm = nc.tensor.matmul(slot[:, 0:P], idb, maskk, start=False, stop=True)
                    mm.then_inc(s2_ready, 1)

            def values(u, s, J):
                eng.wait_ge(s2_turns, NP2 * u + sum(PIECES[:J + 1]) + 2)
                for c in range(J // TPC, S // CH):
                    lo = max(J * P, c * CH)
                    mm = nc.tensor.matmul(o_ps[32 * c:32 * c + 32, lo - c * CH:CH], vst[s % 2][:, J, :],
                                          prob[:, J % 4, lo:(c + 1) * CH], start=J == 0, stop=J == TPC * c + TPC - 1)
                mm.then_inc(prob_turns, 1)

            def turn_max(v, uses):
                eng.wait_ge(negmax_ready, v + 1)
                eng.wait_ge(turn_free, uses)
                nc.tensor.transpose(turn[0:2 * TB, 0:P // 2].bitcast(BF16), negmax[:].rearrange("p a n -> p (a n)"),
                                    idb).then_inc(turn_ready, 1)

            eng.wait_ge(near_loaded[0], 16)
            for v in range(2):
                eng.wait_ge(stack_loaded[v], 144)
                for I in reversed(range(TB)):
                    maxima(v, v, 0, I)
            turn_max(0, 1)

            def stack_ready(i, k):
                eng.wait_ge(max_loaded[k], 32 * i + 32 + START)
                if k % 2 == 0:
                    eng.wait_ge(far_loaded[k // 2], 48 * i + 48)

            def units(i, last):
                for k in range(QUAD):
                    u = QUAD * i + k
                    k2 = (k + 2) % QUAD
                    hs2 = (k // 2 + 1) % 2
                    ahead = not (last and k >= 2)
                    if ahead:
                        again = 1 if k < 2 else 2
                        eng.wait_ge(stack_loaded[k2], 144 * (i + again))
                        if k % 2 == 0:
                            eng.wait_ge(near_loaded[hs2], 16 * (i + again))
                    for j in range(TB):
                        I = TB - 1 - j
                        banks = range(GROUPS[I]) if ahead else ()
                        if j < TB - 1:
                            ahead_tile = (u, k, k // 2, j + 1)
                        elif not (last and k == QUAD - 1):
                            k1 = (k + 1) % QUAD
                            stack_ready(i + (k + 1) // QUAD, k1)
                            ahead_tile = (u + 1, k1, k1 // 2, 0)
                        else:
                            ahead_tile = None
                        if ahead_tile:
                            scores(*ahead_tile, 0)
                        maxima(u + 2, k2, hs2, I, banks[:1])
                        if j == 0:
                            eng.wait_ge(vst_ready, u + 1)
                            eng.wait_ge(oT_ready, u + START)
                        values(u, k, j)
                        maxima(u + 2, k2, hs2, I, banks[1:2])
                        if ahead_tile:
                            scores(*ahead_tile, 1)
                        maxima(u + 2, k2, hs2, I, banks[2:])
                        if j == 5 and not (last and k == 3):
                            turn_max(u + 1, 2 * u + 2)
                    eng.wait_ge(oT_ready, u + 1 + START)
                    eng.wait_ge(turn_free, 2 * u + (2 if last and k == 3 else 3) )
                    for n in range(TPC):
                        mm = nc.tensor.transpose(turn[:, n * P:(n + 1) * P], oT[:, n * P:(n + 1) * P], ident)
                        if n == 0:
                            mm.then_inc(vst_turns, 1)
                    mm.then_inc(turn_ready, 1)

            stack_ready(0, 0)
            for n in range(2):
                scores(0, 0, 0, 0, n)
            with eng.Fori(0, NQ - 1) as i:
                units(i, False)
            units(NQ - 1, True)

        @block.scalar
        def _(eng):
            eng.sem_inc(oT_ready, START)
            eng.sem_inc(s2_turns, 2)

            def exponentials(u, J, n):
                if n < PIECES[J]:
                    q0, q1 = attention_pieces(J)[n]
                    if n == 0:
                        eng.wait_ge(prob_turns, TB * u + J + 1)
                    before = sum(PIECES[:J])
                    eng.wait_ge(s2_ready, NP2 * u + before + n + 1 + START)
                    nc.scalar.activation(prob[:, J % 4, q0:q1], s2[:, (before + n) % 2, 0:q1 - q0],
                                         ACT.Exp).then_inc(s2_turns, 1)

            def units(i, last):
                for k in range(QUAD):
                    u = QUAD * i + k
                    more = not (last and k == QUAD - 1)
                    for J in range(1, TB):
                        for n in range(2):
                            exponentials(u, J, n)
                    if more:
                        exponentials(u + 1, 0, 0)
                    eng.wait_ge(prob_turns, TB * (u + 1) + 4)
                    eng.wait_ge(turn_ready, 2 * u + 1)
                    nc.scalar.copy(oT[:], o_ps[:]).then_inc(oT_ready, 1)
                    if more:
                        exponentials(u + 1, 0, 1)

            for n in range(2):
                exponentials(0, 0, n)
            with eng.Fori(0, NQ - 1) as i:
                units(i, False)
            units(NQ - 1, True)

        @block.vector
        def _(eng):
            step = Steps(eng, dve_step)
            eng.sem_inc(s1_turns, 2)
            eng.sem_inc(turn_free, 1)
            step(nc.vector.memset(partmax[:], -3.0e38))
            eng.wait_ge(const_loaded, 16)
            nc.vector.tensor_copy(squares_b[:], squares[:]).then_inc(const_cast, 1)

            def maxima(v, I):
                before = sum(GROUPS[I + 1:])
                for g in range(GROUPS[I]):
                    eng.wait_ge(s1_ready, NG1 * v + before + g + 1)
                    width = min(CH, (I + 1) * P - g * CH)
                    nc.vector.tensor_reduce(partmax[:, I, g:g + 1], s1[:, (before + g) % 2, 0:width],
                                            AX, ALU.max).then_inc(s1_turns, 1)

            def negate(v):
                eng.wait_ge(s1_turns, NG1 * (v + 1) + 2)
                step(nc.vector.tensor_reduce(mx[:], partmax[:], AX, ALU.max))
                step(nc.vector.tensor_scalar(negmax[:, 0], mx[:], -1.0, None, ALU.mult))
                nc.vector.scalar_tensor_tensor(out=negmax[:, 1], in0=mx[:], scalar=-1.0, in1=negmax[:, 0],
                                               op0=ALU.mult, op1=ALU.subtract).then_inc(negmax_ready, 1)

            def turned_max(v, i, k, uses):
                eng.wait_ge(turn_ready, uses)
                if k < 2:
                    eng.wait_ge(max_loaded[(k + 2) % QUAD], 32 * i + START)
                else:
                    eng.wait_ge(max_loaded[(k + 2) % QUAD], 32 * i + 32 + START)
                nc.vector.tensor_copy(negmaxT[k % 2][:], turn[0:2 * TB, 0:P // 2].bitcast(BF16)).then_inc(negmaxT_ready, 1)
                eng.wait_ge(negmaxT_ready, v + 1)
                eng.sem_inc(turn_free, 1)

            def normalise(u, i, k, uses):
                eng.wait_ge(turn_ready, uses)
                view = turn[:].rearrange("p (n c d) -> p c n d", n=TPC, c=4)
                step(nc.vector.reciprocal(rsum[:], view[:, :, :, HD]))
                b = k % 2
                out = t.o_sb[:, b * TB:(b + 1) * TB, ds((2 * i + k // 2) * HD, HD)]
                step(nc.vector.tensor_tensor(out.rearrange("p (c n) d -> p c n d", c=4), view[:, :, :, 0:HD],
                                             rsum[:].unsqueeze(3).to_broadcast([P, 4, TPC, HD]), ALU.mult))
                eng.sem_inc(turn_free, 1)

            for I in reversed(range(TB)):
                maxima(0, I)
            negate(0)
            for I in reversed(range(TB)):
                maxima(1, I)
            turned_max(0, 0, 0, 1)
            negate(1)

            def units(i, last):
                for k in range(QUAD):
                    u = QUAD * i + k
                    ahead = not (last and k >= 2)
                    for j in range(TB):
                        if ahead:
                            maxima(u + 2, TB - 1 - j)
                        if j == 6 and not (last and k == 3):
                            turned_max(u + 1, i + (k + 1) // QUAD, (k + 1) % QUAD, 2 * u + 2)
                    normalise(u, i, k, 2 * u + (2 if last and k == 3 else 3))
                    if ahead:
                        negate(u + 2)

            with eng.Fori(0, NQ - 1) as i:
                step.enter(i, QUAD * 4)
                units(i, False)
                step.leave(NQ - 1)
            units(NQ - 1, True)



def phase_project(nc, t):
    with nc.cleanup_on_exit(), ExitStack() as ctx:
        sp = Space(nc, ctx, "prj")
        wp = sp.sb("wp", [P, KT, D])
        pb, gain, shift = sp.sb("pb", [P, D]), sp.sb("gain", [P, D]), sp.sb("shift", [P, D])
        ident = sp.sb("ident", [P, P])
        keep = sp.sb("keep", [P, NCH])
        eps = sp.sb("eps", [P, 1])
        ones = sp.sb("ones", [P, CH])
        o = sp.sb("o", [P, TPC, D])
        x = sp.sb("x", [P, TPC, D])
        xp = sp.sb("xp", [P, TPC, D])
        xl = sp.sb("xl", [P, TPC, D])
        oT = sp.sb("oT", [P, 2, KT, P])
        y = sp.sb("y", [P, TPC, D])
        x1 = sp.sb("x1", [P, TPC, D])
        stats = sp.sb("stats", [P, TPC, 6])
        mv = sp.sb("mv", [P, 2, TPC, 2])
        std = sp.sb("std", [P, 2, TPC])
        rstd = sp.sb("rstd", [P, 2, TPC])
        xT = sp.sb("xT", [P, KT, CH])
        cum = sp.sb("cum", [P, KT, CH])
        carry = sp.sb("carry", [P, KT])
        oT_ps = sp.psum("oT_ps", [P, 2, CH])
        y_ps = sp.psum("y_ps", [P, TPC, CH])
        xT_ps = sp.psum("xT_ps", [P, KT, CH])

        const_loaded, pool_set = sp.sem("const_loaded"), sp.sem("pool_set")
        o_loaded, x_loaded = sp.sem("o_loaded"), sp.sem("x_loaded")
        o_used = sp.sem("o_used")
        biased = sp.sem("biased")
        oT_ps_ready, oT_ready = sp.sem("oT_ps_ready"), sp.sem("oT_ready")
        y_ready, y_used = sp.sem("y_ready"), sp.sem("y_used")
        xl_used = sp.sem("xl_used")
        var_ready, std_ready = sp.sem("var_ready"), sp.sem("std_ready")
        x1_ready, xT_ps_ready = sp.sem("x1_ready"), sp.sem("xT_ps_ready")
        xT_ready, cum_ready = sp.sem("xT_ready"), sp.sem("cum_ready")
        x1_stored, xT_stored, cum_stored = sp.sem("x1_stored"), sp.sem("xT_stored"), sp.sem("cum_stored")
        dve_step = sp.sem("dve_step")
        block = ctx.enter_context(nc.Block())

        @block.sync
        def _(eng):
            eng.sem_inc(x1_stored, START)
            eng.sem_inc(xT_stored, START)
            eng.sem_inc(cum_stored, START)
            for dst, src in ((wp, t.wproj), (pb, t.bproj), (gain, t.ln_g), (shift, t.ln_b), (ident, t.ident), (keep, t.keep)):
                eng.dma_start(dst[:], src).then_inc(const_loaded, 16)

            def load(c):
                after(eng, o_used, c)
                eng.dma_start(o[:], t.o_sb[:, ds(c * TPC, TPC), :]).then_inc(o_loaded, 16)
                after(eng, biased, 2 * c)
                eng.dma_start(x[:], t.x.rearrange("(n p) d -> p n d", p=P)[:, ds(c * TPC, TPC), :]).then_inc(x_loaded, 16)

            def store(c):
                eng.wait_ge(x1_ready, c + 1)
                eng.dma_start(t.x1.rearrange("(n p) d -> p n d", p=P)[:, ds(c * TPC, TPC), :], x1[:]).then_inc(x1_stored, 16)
                eng.wait_ge(xT_ready, KT * (c + 1) + START)
                eng.dma_start(t.x1T[:, :, ds(c * CH, CH)], xT[:]).then_inc(xT_stored, 16)
                eng.wait_ge(cum_ready, c + 1 + START)
                eng.dma_start(t.cumT[:, :, ds(c * CH, CH)], cum[:]).then_inc(cum_stored, 16)

            load(0)
            load(1)
            with eng.Fori(0, NCH - 2) as i:
                store(i)
                load(i + 2)
            store(NCH - 2)
            store(NCH - 1)
            for sem in (x1_stored, xT_stored, cum_stored):
                eng.wait_ge(sem, 16 * NCH + START)

        @block.gpsimd
        def _(eng):
            step = Steps(eng, pool_set)
            step(nc.gpsimd.memset(eps[:], EPS))
            step(nc.gpsimd.memset(ones[:], 1.0))
            step(nc.gpsimd.memset(carry[:], 0.0))
            eng.wait_ge(const_loaded, 96)

            with eng.Fori(0, NCH) as c:
                eng.wait_ge(x_loaded, 16 * c + 16)
                eng.wait_ge(y_used, TPC * c + START)
                nc.gpsimd.tensor_tensor(xp[:], x[:], pb[:].unsqueeze(1).to_broadcast([P, TPC, D]), ALU.add).then_inc(biased, 1)
                eng.wait_ge(biased, 2 * c + 1)
                eng.wait_ge(xl_used, c + START)
                nc.gpsimd.tensor_tensor(xl[:], x[:], shift[:].unsqueeze(1).to_broadcast([P, TPC, D]), ALU.add).then_inc(biased, 1)
                eng.wait_ge(biased, 2 * c + 2)

        @block.tensor
        def _(eng):
            eng.wait_ge(const_loaded, 96)

            def project(c):
                eng.wait_ge(o_loaded, 16 * c + 16)
                for j in range(TPC + 1):
                    if j < TPC:
                        after(eng, oT_ready, TPC * c + j - 1)
                        for k in range(KT):
                            mm = nc.tensor.transpose(oT_ps[:, j % 2, k * P:(k + 1) * P], o[:, j, k * P:(k + 1) * P], ident[:])
                        mm.then_inc(oT_ps_ready, 1)
                        if j == TPC - 1:
                            eng.wait_ge(oT_ps_ready, TPC * c + TPC)
                            eng.sem_inc(o_used, 1)
                    if j > 0:
                        eng.wait_ge(oT_ready, TPC * c + j)
                        after(eng, y_used, TPC * (c - 1) + j + START)
                        for k in range(KT):
                            mm = nc.tensor.matmul(y_ps[:, j - 1, 0:D], oT[:, (j - 1) % 2, k], wp[:, k],
                                                  start=k == 0, stop=k == KT - 1)
                        mm.then_inc(y_ready, 1)

            def turn(c):
                eng.wait_ge(x1_ready, c + 1)
                for k in range(KT):
                    eng.wait_ge(xT_ready, KT * c + START)
                    for j in range(TPC):
                        mm = nc.tensor.transpose(xT_ps[:, k, j * P:(j + 1) * P], x1[:, j, k * P:(k + 1) * P], ident[:])
                    mm.then_inc(xT_ps_ready, 1)

            project(0)
            with eng.Fori(0, NCH - 1) as i:
                project(i + 1)
                turn(i)
            turn(NCH - 1)

        @block.scalar
        def _(eng):
            eng.sem_inc(xT_ready, START)
            eng.wait_ge(pool_set, 3)

            def front(c):
                for j in range(TPC):
                    eng.wait_ge(oT_ps_ready, TPC * c + j + 1)
                    after(eng, y_ready, TPC * c + j - 1)
                    nc.scalar.copy(oT[:, j % 2], oT_ps[:, j % 2, 0:D].rearrange("p (k q) -> p k q", k=KT)).then_inc(oT_ready, 1)
                for n in range(2):
                    eng.wait_ge(var_ready, 2 * c + n + 1)
                    nc.scalar.activation(std[:, n], mv[:, n, :, 1], ACT.Sqrt, bias=eps[:]).then_inc(std_ready, 1)

            def back(c):
                for k in range(KT):
                    eng.wait_ge(xT_ps_ready, KT * c + k + 1)
                    if k == 0:
                        eng.wait_ge(xT_stored, 16 * c + START)
                        eng.wait_ge(cum_ready, c + START)
                    nc.scalar.copy(xT[:, k], xT_ps[:, k]).then_inc(xT_ready, 1)

            front(0)
            with eng.Fori(0, NCH - 1) as i:
                front(i + 1)
                back(i)
            back(NCH - 1)

        @block.vector
        def _(eng):
            eng.sem_inc(y_used, START)
            eng.sem_inc(xl_used, START)
            eng.sem_inc(cum_ready, START)
            step = Steps(eng, dve_step)
            eng.wait_ge(const_loaded, 96)
            eng.wait_ge(pool_set, 3)

            def moments(n):
                for j in range(TPC):
                    step.go(nc.vector.bn_stats(stats[:, j], y[:, j]))
                eng.drain()
                for j in range(TPC):
                    ins = nc.vector.bn_aggr(mv[:, n, j], stats[:, j])
                    if j < TPC - 1:
                        step.go(ins)
                    else:
                        ins.then_inc(var_ready, 1)

            def front(c):
                eng.wait_ge(biased, 2 * c + 1)
                for j in range(TPC):
                    eng.wait_ge(y_ready, TPC * c + j + 1)
                    nc.vector.tensor_tensor(y[:, j], y_ps[:, j, 0:D], xp[:, j], ALU.add).then_inc(y_used, 1)
                eng.wait_ge(y_used, TPC * c + TPC + START)
                moments(0)
                eng.wait_ge(std_ready, 2 * c + 1)
                step(nc.vector.reciprocal(rstd[:, 0], std[:, 0]))
                for j in range(TPC):
                    step.go(nc.vector.scalar_tensor_tensor(out=y[:, j], in0=y[:, j], scalar=mv[:, 0, j, 0:1], in1=gain[:],
                                                           op0=ALU.subtract, op1=ALU.mult))
                step.wait()
                eng.wait_ge(biased, 2 * c + 2)
                for j in range(TPC):
                    step.go(nc.vector.scalar_tensor_tensor(out=y[:, j], in0=y[:, j], scalar=rstd[:, 0, j:j + 1], in1=xl[:, j],
                                                           op0=ALU.mult, op1=ALU.add))
                step.wait()
                eng.sem_inc(xl_used, 1)
                moments(1)
                eng.wait_ge(std_ready, 2 * c + 2)
                step(nc.vector.reciprocal(rstd[:, 1], std[:, 1]))
                after(eng, x1_stored, 16 * c + START)
                after(eng, xT_ps_ready, KT * c)
                for j in range(TPC):
                    ins = nc.vector.tensor_scalar(x1[:, j], y[:, j], mv[:, 1, j, 0:1], rstd[:, 1, j:j + 1],
                                                  ALU.subtract, ALU.mult)
                    if j < TPC - 1:
                        step.go(ins)
                    else:
                        ins.then_inc(x1_ready, 1)
                eng.wait_ge(x1_ready, c + 1)

            def back(c):
                eng.wait_ge(xT_ready, KT * c + KT + START)
                eng.wait_ge(cum_stored, 16 * c + START)
                for k in range(KT):
                    step.go(nc.vector.tensor_tensor_scan(cum[:, k], ones[:], xT[:, k], carry[:, k:k + 1], ALU.mult, ALU.add))
                step.wait()
                nc.vector.tensor_scalar(carry[:].unsqueeze(2), cum[:, :, CH - 1:CH], keep[:, ds(c, 1)], None,
                                        ALU.mult).then_inc(cum_ready, 1)
                eng.wait_ge(cum_ready, c + 1 + START)

            front(0)
            with eng.Fori(0, NCH - 1) as i:
                step.enter(i, 7 + 1 + 8 + 7 + 1 + 3 + 2)
                front(i + 1)
                back(i)
                step.leave(NCH - 1)
            back(NCH - 1)



KE, R = 8, 64
KR = KE * R
GB = KR // P
NG = 2 * GB
RH = 256
WF = KR + RH
NW = 2 * KE
NSP = 6


def phase_combine(nc, t):
    with nc.cleanup_on_exit(), ExitStack() as ctx:
        sp = Space(nc, ctx, "cmb")
        wq, wk, wi = sp.sb("wq", [P, KT, D]), sp.sb("wk", [P, KT, D]), sp.sb("wi", [P, KT, D])
        vq = sp.sb("vq", [P, 2, KT, WF])
        vk = sp.sb("vk", [P, 2, KT, KR])
        iq = sp.sb("iq", [P, KT, WF])
        ik = sp.sb("ik", [P, KT, KR])
        u = sp.sb("u", [P, 2, KT, KR])
        wo = sp.sb("wo", [P, KT, D])
        bias = sp.sb("bias", [P, KT, NSP * NW])
        alpha = sp.sb("alpha", [P, 1])
        b2, be = sp.sb("b2", [P, KE]), sp.sb("be", [P, KE])
        alphas = sp.sb("alphas", [NSP * NW, 1])
        pick = sp.sb("pick", [NSP * NW, 3])
        sel = sp.sb("sel", [NSP * NW, NG, P])
        bo = sp.sb("bo", [NSP * NW, D])
        bopart = sp.sb("bopart", [NSP * NW, 3, D], BF16)
        borest = sp.sb("borest", [NSP * NW, D])
        bosum = sp.sb("bosum", [NSP * NW, D])
        whole = sp.sb("whole", [P, 2, CH])
        ps = sp.psum("ps", [P, 4, CH])
        loaded = sp.sem("loaded")
        ready = sp.sem("ready")
        evac = sp.sem("evac")
        split = sp.sem("split")
        dve_step = sp.sem("dve_step")
        block = ctx.enter_context(nc.Block())

        jobs = []
        for m in range(KT):
            col = slice(m * P, (m + 1) * P)
            for c0, c1 in ((0, CH), (CH, WF)):
                jobs.append((iq[:, m, c0:c1], P, [wi[:, k, col] for k in range(KT)], [vq[:, 1, k, c0:c1] for k in range(KT)], 1.0, None))
            jobs.append((ik[:, m, :], P, [wi[:, k, col] for k in range(KT)], [vk[:, 1, k, :] for k in range(KT)], 1.0, None))
        n_inner = len(jobs)
        for br in range(2):
            for m in range(KT):
                col = slice(m * P, (m + 1) * P)
                right = (lambda k: vq[:, 0, k]) if br == 0 else (lambda k: iq[:, k])
                for c0, c1 in ((0, CH), (CH, WF)):
                    jobs.append((None, P, [wq[:, k, col] for k in range(KT)], [right(k)[:, c0:c1] for k in range(KT)], 1.0,
                                 (t.aq_hi[:, br, m, c0:c1], t.aq_lo[:, br, m, c0:c1])))
                right = (lambda k: vk[:, 0, k]) if br == 0 else (lambda k: ik[:, k])
                jobs.append((None, P, [wk[:, k, col] for k in range(KT)], [right(k) for k in range(KT)], 1.0,
                             (t.ak_hi[:, br, m], t.ak_lo[:, br, m])))
            for g in range(GB):
                jobs.append((t.uo[:, br * GB + g], P, [u[:, br, k, g * P:(g + 1) * P] for k in range(KT)],
                             [wo[:, k] for k in range(KT)], alpha[:, 0:1] if br else 1.0, None))
        jobs.append((bo[:], NSP * NW, [bias[:, k] for k in range(KT)], [wo[:, k] for k in range(KT)], alphas[:, 0:1], None))
        splits = [n for n, j in enumerate(jobs) if j[5]]

        @block.sync
        def _(eng):
            loads = ((wq, t.wq), (wk, t.wk), (wi, t.winv), (vq, t.vq), (vk, t.vk), (u, t.u), (wo, t.wo), (bias, t.bffn),
                     (alpha, t.alpha), (alphas, t.alphas), (pick, t.pick))
            for dst, src in loads:
                eng.dma_start(dst[:], src).then_inc(loaded, 16)
            for dst, src in ((t.router2, t.w2), (t.routerb, t.b1), (b2, t.b2), (be, t.be), (sel, t.sel), (t.count_sb, t.count)):
                eng.dma_start(dst[:], src).then_inc(loaded, 16)
            eng.wait_ge(loaded, 16 * 17)

        @block.tensor
        def _(eng):
            eng.wait_ge(loaded, 16 * 17)
            for n, (_, rows, left, right, _, _) in enumerate(jobs):
                if n >= 4:
                    eng.wait_ge(evac, n - 3)
                if n == n_inner:
                    eng.wait_ge(evac, n)
                width = right[0].shape[-1]
                for k in range(KT):
                    mm = nc.tensor.matmul(ps[0:rows, n % 4, 0:width], left[k], right[k], start=k == 0, stop=k == KT - 1)
                mm.then_inc(ready, 1)

        @block.scalar
        def _(eng):
            for n, (dst, rows, _, right, scale, parts) in enumerate(jobs):
                width = right[0].shape[-1]
                eng.wait_ge(ready, n + 1)
                if parts:
                    s = splits.index(n)
                    if s >= 2:
                        eng.wait_ge(split, s - 1)
                    dst = whole[:, s % 2, 0:width]
                nc.scalar.activation(dst, ps[0:rows, n % 4, 0:width], ACT.Identity, scale=scale).then_inc(evac, 1)

        @block.vector
        def _(eng):
            step = Steps(eng, dve_step)
            eng.wait_ge(loaded, 16 * 17)
            step(nc.vector.tensor_tensor(t.logitb[:], b2[:], be[:], ALU.add))
            step(nc.vector.tensor_copy(t.sel_sb[:], sel[:]))
            for s, n in enumerate(splits):
                hi, lo = jobs[n][5]
                src = whole[:, s % 2, 0:hi.shape[-1]]
                eng.wait_ge(evac, n + 1)
                step(nc.vector.tensor_copy(hi, src))
                nc.vector.tensor_tensor(lo, src, hi.bitcast(F32), ALU.subtract).then_inc(split, 1)
            eng.wait_ge(evac, len(jobs))
            step(nc.vector.tensor_copy(bopart[:, 0], bo[:]))
            step(nc.vector.tensor_tensor(borest[:], bo[:], bopart[:, 0], ALU.subtract))
            step(nc.vector.tensor_copy(bopart[:, 1], borest[:]))
            step(nc.vector.tensor_tensor(bopart[:, 2], borest[:], bopart[:, 1], ALU.subtract))
            step(nc.vector.tensor_scalar(bosum[:], bopart[:, 0], pick[:, 0:1], None, ALU.mult))
            step(nc.vector.scalar_tensor_tensor(out=bosum[:], in0=bopart[:, 1], scalar=pick[:, 1:2], in1=bosum[:],
                                                op0=ALU.mult, op1=ALU.add))
            step(nc.vector.scalar_tensor_tensor(out=t.bo_stack[:], in0=bopart[:, 2], scalar=pick[:, 2:3], in1=bosum[:],
                                                op0=ALU.mult, op1=ALU.add))


def phase_fused(nc, t):
    with nc.cleanup_on_exit(), ExitStack() as ctx:
        sp = Space(nc, ctx, "ffn")
        ident, idb = sp.sb("ident", [P, P]), sp.sb("idb", [P, P], BF16)
        eps = sp.sb("eps", [P, 1])
        raw = sp.sb("raw", [P, 2, KT, CH])
        hi = sp.sb("hi", [P, 2, KT, CH], F32R)
        lo = sp.sb("lo", [P, 2, KT, CH], F32R)
        res = sp.sb("res", [P, TPC, D])
        hT = sp.sb("hT", [P, 2, KT, CH])
        ky = sp.sb("ky", [P, 2, CH])
        prod = sp.sb("prod", [P, NG, CH])
        lg = sp.sb("lg", [P, TPC * 2, KE])
        red = sp.sb("red", [P, TPC * 2])
        den = sp.sb("den", [P, TPC, 2])
        inv = sp.sb("inv", [P, TPC * 2])
        wts = sp.sb("wts", [P, TPC, NW])
        wrest = sp.sb("wrest", [P, TPC, NW])
        wst = sp.sb("wst", [P, TPC, NSP, NW], BF16)
        wT = sp.sb("wT", [NSP * NW, CH], BF16)
        y = sp.sb("y", [P, TPC, D])
        x2 = sp.sb("x2", [P, TPC, D])
        stats = sp.sb("stats", [P, TPC, 6])
        mv = sp.sb("mv", [P, TPC, 2])
        std = sp.sb("std", [P, TPC])
        rstd = sp.sb("rstd", [P, TPC])
        xT = sp.sb("xT", [P, KT, CH])
        work = sp.psum("work", [P, 4, CH])
        o_ps = sp.psum("o_ps", [P, 2, CH])
        lg_ps = sp.psum("lg_ps", [P, CH])
        xT_ps = sp.psum("xT_ps", [P, CH])

        const_loaded, pool_set = sp.sem("const_loaded"), sp.sem("pool_set")
        raw_loaded, res_loaded = sp.sem("raw_loaded"), sp.sem("res_loaded")
        hi_ready, lo_ready = sp.sem("hi_ready"), sp.sem("lo_ready")
        work_ready = sp.sem("work_ready")
        act_read, dve_read = sp.sem("act_read"), sp.sem("dve_read")
        products_done = sp.sem("products_done")
        lg_ready, exp_ready, lg_read = sp.sem("lg_ready"), sp.sem("exp_ready"), sp.sem("lg_read")
        shifted = sp.sem("shifted")
        wst_ready, wT_ps_ready, wT_ready = sp.sem("wst_ready"), sp.sem("wT_ps_ready"), sp.sem("wT_ready")
        ky_used = sp.sem("ky_used")
        o_ready, o_read = sp.sem("o_ready"), sp.sem("o_read")
        var_ready, std_ready = sp.sem("var_ready"), sp.sem("std_ready")
        x2_ready, xT_ps_ready, xT_ready, xT_stored = (sp.sem("x2_ready"), sp.sem("xT_ps_ready"), sp.sem("xT_ready"),
                                                      sp.sem("xT_stored"))
        idb_ready, dve_step = sp.sem("idb_ready"), sp.sem("dve_step")
        block = ctx.enter_context(nc.Block())

        USES = 4 + 2 * NG + NG
        reader = ["act"] * 4 + ["dve", "act"] * NG + ["dve"] * NG
        READS = {who: reader.count(who) for who in ("act", "dve")}

        def bank_free(eng, c, n):
            m = n - 4
            chunk = c if m >= 0 else c - 1
            who = reader[m]
            count = READS[who] * chunk + reader[:m % USES + 1].count(who)
            after(eng, act_read if who == "act" else dve_read, count)

        @block.sync
        def _(eng):
            eng.sem_inc(xT_stored, START)
            eng.dma_start(ident[:], t.ident).then_inc(const_loaded, 16)

            def load(c):
                after(eng, lo_ready, 2 * c)
                eng.dma_start(raw[:, 0], t.x1T[:, :, ds(c * CH, CH)]).then_inc(raw_loaded, 16)
                eng.dma_start(raw[:, 1], t.cumT[:, :, ds(c * CH, CH)]).then_inc(raw_loaded, 16)

            def load_res(c):
                after(eng, o_read, TPC * c)
                eng.dma_start(res[:], t.x1.rearrange("(n p) d -> p n d", p=P)[:, ds(c * TPC, TPC), :]).then_inc(res_loaded, 16)

            def store(c):
                eng.wait_ge(xT_ready, KT * (c + 1) + START)
                eng.dma_start(t.x2T[:, :, ds(c * CH, CH)], xT[:]).then_inc(xT_stored, 16)

            load(0)
            load_res(0)
            load(1)
            load_res(1)
            with eng.Fori(0, NCH - 2) as i:
                load(i + 2)
                store(i)
                load_res(i + 2)
            store(NCH - 2)
            store(NCH - 1)
            eng.wait_ge(xT_stored, 16 * NCH + START)

        @block.gpsimd
        def _(eng):
            nc.gpsimd.memset(eps[:], EPS).then_inc(pool_set, 1)

        @block.tensor
        def _(eng):
            eng.sem_inc(xT_ps_ready, START)
            eng.wait_ge(const_loaded, 16)
            eng.wait_ge(idb_ready, 1)

            def exact(out, w_hi, w_lo, x, first, last):
                nc.tensor.matmul(out, w_hi, hi[:, x[0], x[1]], start=first, stop=False)
                nc.tensor.matmul(out, w_hi, lo[:, x[0], x[1]], start=False, stop=False)
                return nc.tensor.matmul(out, w_lo, hi[:, x[0], x[1]], start=False, stop=last)

            def product(c, n, a_hi, a_lo, br, src, col):
                bank_free(eng, c, n)
                for k in range(KT):
                    mm = exact(work[:, n % 4], a_hi[:, br, k, col], a_lo[:, br, k, col], (src, k), k == 0, k == KT - 1)
                mm.then_inc(work_ready, 1)

            def logits(c):
                eng.wait_ge(act_read, READS["act"] * c + 4)
                after(eng, wT_ready, c)
                for j in range(TPC):
                    for br in range(2):
                        at = (j * 2 + br) * KE
                        for k in range(KT):
                            mm = nc.tensor.matmul(lg_ps[:, at:at + KE], hT[:, br, k, j * P:(j + 1) * P], t.router2[:, k],
                                                  start=k == 0, stop=k == KT - 1)
                mm.then_inc(lg_ready, 1)

            def front(c):
                eng.wait_ge(lo_ready, 2 * c + 2)
                eng.wait_ge(hi_ready, 2 * c + 2)
                for n in range(4):
                    br, m = n // 2, n % 2
                    product(c, n, t.aq_hi, t.aq_lo, br, 0, slice(KR + m * P, KR + (m + 1) * P))
                for g in range(NG):
                    br, col = g // GB, slice(g % GB * P, (g % GB + 1) * P)
                    product(c, 4 + 2 * g, t.aq_hi, t.aq_lo, br, 0, col)
                    product(c, 5 + 2 * g, t.ak_hi, t.ak_lo, br, 1, col)
                    if g == 2:
                        logits(c)

            def back(c):
                eng.wait_ge(x2_ready, c + 1)
                for k in range(KT):
                    eng.wait_ge(xT_ready, KT * c + k + START)
                    for j in range(TPC):
                        mm = nc.tensor.transpose(xT_ps[:, j * P:(j + 1) * P], x2[:, j, k * P:(k + 1) * P], ident[:])
                    mm.then_inc(xT_ps_ready, 1)

            def middle(c):
                eng.wait_ge(wst_ready, c + 1)
                for j in range(TPC):
                    mm = nc.tensor.transpose(lg_ps[0:NSP * NW, j * P // 2:(j + 1) * P // 2].bitcast(BF16),
                                             wst[:, j].rearrange("p a w -> p (a w)"), idb[:])
                mm.then_inc(wT_ps_ready, 1)
                eng.wait_ge(wT_ready, c + 1)
                for g in range(NG):
                    n = 4 + 2 * NG + g
                    bank_free(eng, c, n)
                    nc.tensor.matmul(work[:, n % 4], t.sel_sb[:, g], wT[:], start=True, stop=True).then_inc(work_ready, 1)
                eng.wait_ge(dve_read, READS["dve"] * (c + 1))
                for j in range(TPC):
                    after(eng, o_read, TPC * c + j - 1)
                    tok = slice(j * P, (j + 1) * P)
                    nc.tensor.matmul(o_ps[:, j % 2, 0:D], wT[:, tok], t.bo_stack[:], start=True, stop=False)
                    for g in range(NG):
                        mm = nc.tensor.matmul(o_ps[:, j % 2, 0:D], prod[:, g, tok], t.uo[:, g], start=False, stop=g == NG - 1)
                    mm.then_inc(o_ready, 1)

            front(0)
            middle(0)
            with eng.Fori(0, NCH - 1) as i:
                front(i + 1)
                back(i)
                middle(i + 1)
            back(NCH - 1)

        @block.scalar
        def _(eng):
            eng.sem_inc(xT_ready, START)
            eng.wait_ge(pool_set, 1)

            def round_hi(c):
                for a in range(2):
                    eng.wait_ge(raw_loaded, 32 * c + 32)
                    if a == 0:
                        after(eng, work_ready, USES * (c - 1) + 4 + 2 * NG)
                    nc.scalar.copy(hi[:, a], raw[:, a]).then_inc(hi_ready, 1)

            def hidden(c):
                for n in range(4):
                    br, m = n // 2, n % 2
                    eng.wait_ge(work_ready, USES * c + n + 1)
                    if n == 0:
                        after(eng, lg_ready, c)
                    nc.scalar.activation(hT[:, br, m], work[:, n % 4], ACT.Gelu, bias=t.routerb[:, m:m + 1]).then_inc(act_read, 1)

            def sums(c, groups):
                for g in groups:
                    n = 5 + 2 * g
                    eng.wait_ge(work_ready, USES * c + n + 1)
                    after(eng, ky_used, NG * c + g - 1)
                    nc.scalar.copy(ky[:, g % 2], work[:, n % 4]).then_inc(act_read, 1)

            def exponentials(c):
                eng.wait_ge(shifted, c + 1)
                nc.scalar.activation(lg[:], lg[:], ACT.Exp).then_inc(exp_ready, 1)

            def turned(c):
                eng.wait_ge(wT_ps_ready, c + 1)
                after(eng, o_ready, TPC * c)
                nc.scalar.copy(wT[:], lg_ps[0:NSP * NW, 0:CH // 2].bitcast(BF16)).then_inc(wT_ready, 1)

            def deviation(c):
                eng.wait_ge(var_ready, c + 1)
                nc.scalar.activation(std[:], mv[:, :, 1], ACT.Sqrt, bias=eps[:]).then_inc(std_ready, 1)

            def back(c):
                for k in range(KT):
                    eng.wait_ge(xT_ps_ready, KT * c + k + 1 + START)
                    if k == 0:
                        eng.wait_ge(xT_stored, 16 * c + START)
                    nc.scalar.copy(xT[:, k], xT_ps[:]).then_inc(xT_ready, 1)

            def rest(c, more):
                sums(c, range(4))
                exponentials(c)
                sums(c, range(4, NG))
                if more:
                    round_hi(c + 1)

            round_hi(0)
            hidden(0)
            rest(0, True)
            turned(0)

            def body(i, more):
                hidden(i + 1)
                deviation(i)
                rest(i + 1, more)
                back(i)
                turned(i + 1)

            with eng.Fori(0, NCH - 2) as i:
                body(i, True)
            body(NCH - 2, False)
            deviation(NCH - 1)
            back(NCH - 1)

        @block.vector
        def _(eng):
            step = Steps(eng, dve_step)
            eng.wait_ge(pool_set, 1)
            eng.wait_ge(const_loaded, 16)
            nc.vector.tensor_copy(idb[:], ident[:]).then_inc(idb_ready, 1)

            def round_lo(c):
                for a in range(2):
                    eng.wait_ge(hi_ready, 2 * c + a + 1)
                    nc.vector.tensor_tensor(lo[:, a], raw[:, a], hi[:, a].bitcast(F32), ALU.subtract).then_inc(lo_ready, 1)

            def multiply(c, groups):
                for g in groups:
                    n = 4 + 2 * g
                    eng.wait_ge(act_read, READS["act"] * c + 4 + g + 1)
                    if g == 0:
                        after(eng, o_ready, TPC * c)
                    nc.vector.tensor_tensor(prod[:, g], work[:, n % 4], ky[:, g % 2], ALU.mult).then_inc(dve_read, 1)
                    eng.wait_ge(dve_read, READS["dve"] * c + g + 1)
                    eng.sem_inc(ky_used, 1)

            def weights(c):
                eng.wait_ge(lg_ready, c + 1)
                flat = lambda x: x.unsqueeze(2).to_broadcast([P, TPC * 2, KE])
                step(nc.vector.tensor_tensor(lg[:], lg_ps[:, 0:TPC * NW].rearrange("p (a k) -> p a k", k=KE),
                                             t.logitb[:].unsqueeze(1).to_broadcast([P, TPC * 2, KE]), ALU.add))
                step(nc.vector.tensor_reduce(red[:], lg[:], AX, ALU.max))
                nc.vector.tensor_tensor(lg[:], lg[:], flat(red[:]), ALU.subtract).then_inc(shifted, 1)
                eng.wait_ge(exp_ready, c + 1)
                step(nc.vector.tensor_reduce(red[:], lg[:], AX, ALU.add))
                step(nc.vector.tensor_tensor(den[:], red[:].rearrange("p (n b) -> p n b", b=2),
                                             t.count_sb[:, ds(c * TPC, TPC)].unsqueeze(2).to_broadcast([P, TPC, 2]), ALU.mult))
                step(nc.vector.reciprocal(inv[:], den[:].rearrange("p n b -> p (n b)")))
                step(nc.vector.tensor_tensor(wts[:].rearrange("p n (b k) -> p (n b) k", b=2), lg[:], flat(inv[:]), ALU.mult))
                after(eng, wT_ps_ready, c)
                thrice = lambda x, n: x.unsqueeze(2).to_broadcast([P, TPC, n, NW])
                step(nc.vector.tensor_copy(wst[:, :, 0:3], thrice(wts[:], 3)))
                step(nc.vector.tensor_tensor(wrest[:], wts[:], wst[:, :, 0], ALU.subtract))
                step(nc.vector.tensor_copy(wst[:, :, 3:5], thrice(wrest[:], 2)))
                nc.vector.tensor_tensor(wst[:, :, 5], wrest[:], wst[:, :, 3], ALU.subtract).then_inc(wst_ready, 1)

            def weigh(c):
                for g in range(NG):
                    n = 4 + 2 * NG + g
                    eng.wait_ge(work_ready, USES * c + n + 1)
                    nc.vector.tensor_tensor(prod[:, g], work[:, n % 4], prod[:, g], ALU.mult).then_inc(dve_read, 1)

            def norm(c):
                eng.wait_ge(res_loaded, 16 * c + 16)
                for j in range(TPC):
                    eng.wait_ge(o_ready, TPC * c + j + 1)
                    nc.vector.tensor_tensor(y[:, j], o_ps[:, j % 2, 0:D], res[:, j], ALU.add).then_inc(o_read, 1)
                eng.wait_ge(o_read, TPC * c + TPC)
                for j in range(TPC):
                    nc.vector.bn_stats(stats[:, j], y[:, j])
                eng.drain()
                for j in range(TPC):
                    ins = nc.vector.bn_aggr(mv[:, j], stats[:, j])
                ins.then_inc(var_ready, 1)
                eng.wait_ge(std_ready, c + 1)
                step(nc.vector.reciprocal(rstd[:], std[:]))
                eng.wait_ge(xT_ps_ready, KT * c + START)
                for j in range(TPC):
                    ins = nc.vector.tensor_scalar(x2[:, j], y[:, j], mv[:, j, 0:1], rstd[:, j:j + 1], ALU.subtract, ALU.mult)
                ins.then_inc(x2_ready, 1)
                eng.wait_ge(x2_ready, c + 1)

            def chunk(c, more):
                multiply(c, range(4))
                weights(c)
                multiply(c, range(4, NG))
                if more:
                    round_lo(c + 1)
                weigh(c)

            round_lo(0)
            chunk(0, True)
            with eng.Fori(0, NCH - 2) as i:
                step.enter(i, 1 + 9)
                norm(i)
                chunk(i + 1, True)
                step.leave(NCH - 2)
            norm(NCH - 2)
            chunk(NCH - 1, False)
            norm(NCH - 1)


N = 16


def phase_scan(nc, t):
    with nc.cleanup_on_exit(), ExitStack() as ctx:
        sp = Space(nc, ctx, "ssm")
        hi, lo = sp.sb("hi", [P, KT, NTOK], F32R), sp.sb("lo", [P, KT, NTOK], F32R)
        u, dt, y = sp.sb("u", [P, KT, NTOK]), sp.sb("dt", [P, KT, NTOK]), t.z_sb
        wdt = sp.sb("wdt", [P, KT, D])
        wdt_hi, wdt_lo = sp.sb("wdt_hi", [P, KT, D], F32R), sp.sb("wdt_lo", [P, KT, D], F32R)
        small = sp.sb("small", [P, 4, KT])
        par = sp.sb("par", [P, 5, KT, N])
        cur = sp.sb("cur", [P, KT, 5])
        raw = sp.sb("raw", [P, 2, KT, 2 * P])
        w_hi = [sp.sb(f"w_hi{m}", [P, KT, 2 * P], F32R) for m in range(KT)]
        w_lo = [sp.sb(f"w_lo{m}", [P, KT, 2 * P], F32R) for m in range(KT)]
        RING = 4
        a = sp.sb("a", [P, RING, CH])
        inp = sp.sb("inp", [P, 2, CH])
        h = sp.sb("h", [P, RING, CH])
        cc = sp.sb("cc", [P, RING, CH])
        b_ps, c_ps = sp.psum("b_ps", [P, RING, CH]), sp.psum("c_ps", [P, RING, CH])

        small_loaded = sp.sem("small_loaded")
        u_loaded = [sp.sem(f"u_loaded{m}") for m in range(KT)]
        raw_loaded = [sp.sem(f"raw_loaded{m}") for m in range(KT)]
        hi_ready, lo_ready = sp.sem("hi_ready"), sp.sem("lo_ready")
        dt_ps_ready, dt_ready = sp.sem("dt_ps_ready"), sp.sem("dt_ready")
        soft_ready, soft_done = sp.sem("soft_ready"), sp.sem("soft_done")
        par_ready = sp.sem("par_ready")
        y_ready = sp.sem("y_ready")
        w_ready = sp.sem("w_ready")
        b_ready, c_ready = sp.sem("b_ready"), sp.sem("c_ready")
        b_read = sp.sem("b_read")
        a_ready, cc_ready = sp.sem("a_ready"), sp.sem("cc_ready")
        c_read = sp.sem("c_read")
        a_used = sp.sem("a_used")
        h_ready = sp.sem("h_ready")
        y_added = sp.sem("y_added")
        pool_step, dve_step, act_step = sp.sem("pool_step"), sp.sem("dve_step"), sp.sem("act_step")
        block = ctx.enter_context(nc.Block())
        UNITS = KT * NCH

        def chunk(ch):
            return slice(ch * CH, (ch + 1) * CH)

        @block.sync
        def _(eng):
            eng.dma_start(small[:, 0], t.b_dt).then_inc(small_loaded, 16)
            eng.dma_start(small[:, 1], t.dt_bias).then_inc(small_loaded, 16)
            eng.dma_start(small[:, 3], t.d_skip).then_inc(small_loaded, 16)
            eng.dma_start(par[:, 0], t.log_a).then_inc(small_loaded, 16)
            eng.dma_start(par[:, 3], t.b_b).then_inc(small_loaded, 16)
            eng.dma_start(par[:, 4], t.b_c).then_inc(small_loaded, 16)
            eng.dma_start(wdt[:], t.w_dt).then_inc(small_loaded, 16)
            for m in range(KT):
                eng.dma_start(u[:, m], t.x2T[:, m]).then_inc(u_loaded[m], 16)
            for m in range(KT):
                eng.dma_start(raw[:, m], t.w_bc[0, m]).then_inc(raw_loaded[m], 16)
            with eng.Fori(0, N - 1) as n:
                for m in range(KT):
                    eng.wait_ge(w_ready, KT * n + m + 1)
                    eng.dma_start(raw[:, m], t.w_bc[ds(n + 1, 1), m].rearrange("a p k c -> (a p) k c")).then_inc(raw_loaded[m], 16)

        @block.tensor
        def _(eng):
            def exact(out, w_hi, w_lo, k, tok, first, last):
                nc.tensor.matmul(out, w_hi, hi[:, k, tok], start=first, stop=False)
                nc.tensor.matmul(out, w_hi, lo[:, k, tok], start=False, stop=False)
                return nc.tensor.matmul(out, w_lo, hi[:, k, tok], start=False, stop=last)

            eng.sem_inc(b_read, RING)
            eng.sem_inc(c_read, RING)
            eng.wait_ge(lo_ready, 1 + KT)
            for m in range(KT):
                for ch in range(NCH):
                    n = m * NCH + ch
                    after(eng, dt_ready, n - RING + 1)
                    for k in range(KT):
                        col = slice(m * P, (m + 1) * P)
                        mm = exact(b_ps[:, n % RING], wdt_hi[:, k, col], wdt_lo[:, k, col], k, chunk(ch), k == 0, k == KT - 1)
                    mm.then_inc(dt_ps_ready, 1)
            eng.wait_ge(dt_ready, KT * NCH)
            with eng.Fori(0, N) as n:
                for m in range(KT):
                    eng.wait_ge(w_ready, KT * n + m + 1)
                    for ch in range(NCH):
                        i = m * NCH + ch
                        unit = UNITS * n + i
                        for ps, read, ready, col in ((b_ps, b_read, b_ready, slice(0, P)), (c_ps, c_read, c_ready, slice(P, 2 * P))):
                            eng.wait_ge(read, unit + 1)
                            for k in range(KT):
                                mm = exact(ps[:, i % RING], w_hi[m][:, k, col], w_lo[m][:, k, col], k, chunk(ch), k == 0, k == KT - 1)
                            mm.then_inc(ready, 1)

        @block.scalar
        def _(eng):
            eng.sem_inc(a_used, RING)
            eng.sem_inc(y_added, RING)
            eng.wait_ge(small_loaded, 112)
            nc.scalar.copy(wdt_hi[:], wdt[:]).then_inc(hi_ready, 1)
            for m in range(KT):
                eng.wait_ge(u_loaded[m], 16)
                nc.scalar.copy(hi[:, m], u[:, m]).then_inc(hi_ready, 1)
            nc.scalar.activation(par[:, 1], par[:, 0], ACT.Exp).then_inc(par_ready, 1)
            eng.wait_ge(par_ready, 2)
            for m in range(KT):
                for ch in range(NCH):
                    n = m * NCH + ch
                    eng.wait_ge(dt_ps_ready, n + 1)
                    nc.scalar.activation(dt[:, m, chunk(ch)], b_ps[:, n % RING], ACT.Identity,
                                         bias=small[:, 2, m:m + 1]).then_inc(dt_ready, 1)
            for m in range(KT):
                eng.wait_ge(soft_ready, 3 * m + 1)
                nc.scalar.activation(y[:, 0], y[:, 0], ACT.Exp).then_inc(soft_done, 1)
                eng.wait_ge(soft_ready, 3 * m + 2)
                nc.scalar.activation(y[:, 1], y[:, 1], ACT.Ln).then_inc(soft_done, 1)
            eng.wait_ge(soft_ready, 3 * KT)
            for m in range(KT):
                nc.scalar.activation(y[:, m], u[:, m], ACT.Copy, scale=small[:, 3, m:m + 1]).then_inc(y_ready, 1)
            nc.scalar.activation(small[:, 0], small[:, 0], ACT.Exp).then_inc(act_step, 1)
            with eng.Fori(0, N) as n:
                for m in range(KT):
                    eng.wait_ge(w_ready, KT * n + m + 1)
                    for ch in range(NCH):
                        i = m * NCH + ch
                        unit = UNITS * n + i
                        eng.wait_ge(a_used, unit + 1)
                        nc.scalar.activation(a[:, i % RING], dt[:, m, chunk(ch)], ACT.Exp,
                                             scale=cur[:, m, 1:2]).then_inc(a_ready, 1)
                        eng.wait_ge(c_ready, unit + 1)
                        eng.wait_ge(y_added, unit + 1)
                        nc.scalar.activation(cc[:, i % RING], c_ps[:, i % RING], ACT.Identity, bias=cur[:, m, 4:5],
                                             scale=cur[:, m, 2:3]).then_inc(c_read, 1)

        @block.gpsimd
        def _(eng):
            eng.wait_ge(y_ready, KT)
            step = Steps(eng, pool_step)
            with eng.Fori(0, N) as n:
                step.enter(n, UNITS)
                for m in range(KT):
                    for ch in range(NCH):
                        i = m * NCH + ch
                        unit = UNITS * n + i
                        eng.wait_ge(c_read, unit + 1 + RING)
                        eng.wait_ge(h_ready, unit + 1)
                        step(nc.gpsimd.tensor_tensor(cc[:, i % RING], cc[:, i % RING], h[:, i % RING], ALU.mult))
                        nc.gpsimd.tensor_tensor(y[:, m, chunk(ch)], y[:, m, chunk(ch)], cc[:, i % RING], ALU.add).then_inc(y_added, 1)
                        eng.wait_ge(y_added, unit + 1 + RING)
                step.leave(N)

        @block.vector
        def _(eng):
            step = Steps(eng, dve_step)

            def split(n, m):
                step(nc.vector.tensor_scalar(cur[:, m].unsqueeze(2), par[:, :, m, ds(n, 1)], 1.0, None, ALU.mult))
                step(nc.vector.tensor_copy(w_hi[m][:], raw[:, m]))
                nc.vector.tensor_tensor(w_lo[m][:], raw[:, m], w_hi[m][:].bitcast(F32), ALU.subtract).then_inc(w_ready, 1)

            eng.wait_ge(small_loaded, 112)
            step(nc.vector.tensor_tensor(small[:, 2], small[:, 0], small[:, 1], ALU.add))
            step(nc.vector.tensor_scalar(small[:, 3], small[:, 3], 1.0, None, ALU.add))
            eng.wait_ge(par_ready, 1)
            step(nc.vector.tensor_scalar(par[:, 1], par[:, 1], -1.0, None, ALU.mult))
            nc.vector.reciprocal(par[:, 2], par[:, 1]).then_inc(par_ready, 1)
            eng.wait_ge(par_ready, 2)
            nc.vector.tensor_tensor(par[:, 4], par[:, 4], par[:, 2], ALU.mult).then_inc(par_ready, 1)
            for n in range(1 + KT):
                eng.wait_ge(hi_ready, n + 1)
                if n == 0:
                    nc.vector.tensor_tensor(wdt_lo[:], wdt[:], wdt_hi[:].bitcast(F32), ALU.subtract).then_inc(lo_ready, 1)
                else:
                    nc.vector.tensor_tensor(lo[:, n - 1], u[:, n - 1], hi[:, n - 1].bitcast(F32), ALU.subtract).then_inc(lo_ready, 1)
            eng.wait_ge(par_ready, 3)
            for m in range(KT):
                eng.wait_ge(raw_loaded[m], 16)
                split(0, m)
            for m in range(KT):
                eng.wait_ge(dt_ready, NCH * (m + 1))
                nc.vector.scalar_tensor_tensor(out=y[:, 0], in0=dt[:, m], scalar=-1.0, in1=dt[:, m],
                                               op0=ALU.mult, op1=ALU.min).then_inc(soft_ready, 1)
                eng.wait_ge(soft_done, 2 * m + 1)
                step(nc.vector.tensor_scalar(y[:, 1], y[:, 0], 1.0, None, ALU.add))
                step(nc.vector.scalar_tensor_tensor(out=y[:, 0], in0=y[:, 1], scalar=1.0, in1=y[:, 0],
                                                    op0=ALU.subtract, op1=ALU.subtract))
                nc.vector.scalar_tensor_tensor(out=dt[:, m], in0=dt[:, m], scalar=0.0, in1=y[:, 0],
                                               op0=ALU.max, op1=ALU.subtract).then_inc(soft_ready, 1)
                eng.wait_ge(soft_ready, 3 * m + 2)
                eng.wait_ge(soft_done, 2 * m + 2)
                nc.vector.tensor_tensor(dt[:, m], dt[:, m], y[:, 1], ALU.add).then_inc(soft_ready, 1)
                eng.wait_ge(soft_ready, 3 * m + 3)

            def states(n, last):
                for m in range(KT):
                    for ch in range(NCH):
                        i = m * NCH + ch
                        unit = UNITS * n + i
                        bu = inp[:, i % 2]
                        tok = chunk(ch)
                        eng.wait_ge(b_ready, unit + 1)
                        nc.vector.scalar_tensor_tensor(out=bu, in0=b_ps[:, i % RING], scalar=cur[:, m, 3:4],
                                                       in1=u[:, m, tok], op0=ALU.add, op1=ALU.mult).then_inc(b_read, 1)
                        eng.wait_ge(b_read, unit + 1 + RING)
                        eng.wait_ge(a_ready, unit + 1)
                        step(nc.vector.scalar_tensor_tensor(out=bu, in0=a[:, i % RING], scalar=1.0, in1=bu,
                                                            op0=ALU.subtract, op1=ALU.mult))
                        eng.wait_ge(y_added, unit + 1)
                        first = ch % (S // CH) == 0
                        nc.vector.tensor_tensor_scan(h[:, i % RING], a[:, i % RING], bu,
                                                     0.0 if first else h[:, (i - 1) % RING, CH - 1:CH],
                                                     ALU.mult, ALU.add).then_inc(h_ready, 1)
                        eng.wait_ge(h_ready, unit + 1)
                        eng.sem_inc(a_used, 1)
                    if not last:
                        eng.wait_ge(raw_loaded[m], 16 * n + 32)
                        eng.wait_ge(c_read, UNITS * n + NCH * (m + 1) + RING)
                        split(n + 1, m)

            with eng.Fori(0, N - 1) as n:
                step.enter(n, UNITS + 2 * KT)
                states(n, False)
                step.leave(N - 1)
            states(N - 1, True)


E2 = 20
HG = D // 4
EB = NSP * E2


def phase_mixture(nc, t):
    with nc.cleanup_on_exit(), ExitStack() as ctx:
        sp = Space(nc, ctx, "moe")
        ident, idb = sp.sb("ident", [P, P]), sp.sb("idb", [P, P], BF16)
        eps = sp.sb("eps", [P, 1])
        we_hi, we_lo = sp.sb("we_hi", [P, KT, E2 * D], F32R), sp.sb("we_lo", [P, KT, E2 * D], F32R)
        wraw = sp.sb("wraw", [P, 2, KT, CH])
        g1 = sp.sb("g1", [P, KT, P])
        g1_hi, g1_lo = sp.sb("g1_hi", [P, KT, P], F32R), sp.sb("g1_lo", [P, KT, P], F32R)
        b1 = sp.sb("b1", [HG, 1])
        g2 = sp.sb("g2", [HG, E2])
        b2 = sp.sb("b2", [P, E2])
        iota = sp.sb("iota", [P, E2])
        be = sp.sb("be", [EB, D])
        pick = sp.sb("pick", [EB, 3])
        bepart = sp.sb("bepart", [EB, 3, D], BF16)
        be_stack = sp.sb("be_stack", [EB, D], BF16)
        z = sp.sb("z", [P, KT, CH])
        x3 = [sp.sb(f"x3{s}", [P, TPC, D]) for s in range(2)]
        x_hi = [sp.sb(f"x_hi{s}", [P, KT, CH], F32R) for s in range(2)]
        x_lo = [sp.sb(f"x_lo{s}", [P, KT, CH], F32R) for s in range(2)]
        hT = sp.sb("hT", [HG, CH])
        pr = sp.sb("pr", [P, TPC, E2])
        red = sp.sb("red", [P, TPC])
        inv = sp.sb("inv", [P, TPC])
        top = sp.sb("top", [P, TPC, 8])
        topi = sp.sb("topi", [P, TPC, 8], U32)
        topf = sp.sb("topf", [P, TPC, 8])
        gate = [sp.sb(f"gate{s}", [P, TPC, E2]) for s in range(2)]
        gtmp = sp.sb("gtmp", [P, TPC, E2])
        gst = sp.sb("gst", [P, TPC, NSP, E2], BF16)
        gT = [sp.sb(f"gT{s}", [EB, CH], BF16) for s in range(2)]
        acc = sp.sb("acc", [P, 2, 2, D])
        out = sp.sb("out", [P, 2, D])
        stats, mv = sp.sb("stats", [P, TPC, 6]), sp.sb("mv", [P, TPC, 2])
        std, rstd = sp.sb("std", [P, TPC]), sp.sb("rstd", [P, TPC])
        ostats, omv = sp.sb("ostats", [P, 6]), sp.sb("omv", [P, 2])
        ostd, orstd = sp.sb("ostd", [P, 1]), sp.sb("orstd", [P, 1])
        ex = sp.psum("ex", [P, 4, CH])
        z_ps = sp.psum("z_ps", [P, CH])
        xT_ps = sp.psum("xT_ps", [P, CH])
        rt_ps = sp.psum("rt_ps", [P, CH])
        be_ps = sp.psum("be_ps", [P, CH])

        const_loaded, pool_set = sp.sem("const_loaded"), sp.sem("pool_set")
        wraw_loaded = [sp.sem(f"wraw_loaded{s}") for s in range(2)]
        we_hi_ready, we_lo_ready = sp.sem("we_hi_ready"), sp.sem("we_lo_ready")
        g1_ready, be_ready = sp.sem("g1_ready"), sp.sem("be_ready")
        z_loaded = sp.sem("z_loaded")
        z_ps_ready, z_read = sp.sem("z_ps_ready"), sp.sem("z_read")
        x3_ready = sp.sem("x3_ready")
        xT_ps_ready, x_hi_ready, x_lo_ready = sp.sem("xT_ps_ready"), sp.sem("x_hi_ready"), sp.sem("x_lo_ready")
        rt_ready, hid_ready, lg_read, gT_ready = sp.sem("rt_ready"), sp.sem("hid_ready"), sp.sem("lg_read"), sp.sem("gT_ready")
        shifted, exp_ready, gst_ready = sp.sem("shifted"), sp.sem("exp_ready"), sp.sem("gst_ready")
        be_ps_ready, be_read = sp.sem("be_ps_ready"), sp.sem("be_read")
        ex_ready = sp.sem("ex_ready")
        ex_read = sp.sem("ex_read")
        var_ready, std_ready = sp.sem("var_ready"), sp.sem("std_ready")
        out_ready = sp.sem("out_ready")
        out_stored = [sp.sem(f"out_stored{s}") for s in range(2)]
        idb_ready, dve_step = sp.sem("idb_ready"), sp.sem("dve_step")
        block = ctx.enter_context(nc.Block())
        NW2 = E2 * D // CH

        @block.sync
        def _(eng):
            eng.sem_inc(out_stored[0], START)
            eng.sem_inc(out_stored[1], START)
            loads = ((ident, t.ident), (g1, t.g1), (b1, t.g1b), (g2, t.g2), (b2, t.g2b), (iota, t.iota),
                     (be, t.bmoe), (pick, t.pick20))
            for dst, src in loads:
                eng.dma_start(dst[:], src).then_inc(const_loaded, 16)

            def load(c):
                after(eng, z_ps_ready, 2 * c)
                eng.dma_start(z[:], t.z_sb[:, :, ds(c * CH, CH)]).then_inc(z_loaded, 16)

            load(0)
            for n in range(NW2):
                if n >= 2:
                    eng.wait_ge(we_lo_ready, n - 1)
                eng.dma_start(wraw[:, n % 2], t.we[:, :, n * CH:(n + 1) * CH]).then_inc(wraw_loaded[n % 2], 16)
            load(1)

            def chunks(i, last):
                for s in range(2):
                    c = 2 * i + s
                    if not last:
                        load(c + 2)
                    for j in range(TPC):
                        eng.wait_ge(out_ready, TPC * c + j + 1)
                        eng.dma_start(t.out.rearrange("(n p) d -> p n d", p=P)[:, ds(c * TPC + j, 1), :],
                                      out[:, j % 2].unsqueeze(1)).then_inc(out_stored[j % 2], 16)

            with eng.Fori(0, NCH // 2 - 1) as i:
                chunks(i, False)
            chunks(NCH // 2 - 1, True)
            for s in range(2):
                eng.wait_ge(out_stored[s], 16 * NT // 2 + START)

        @block.gpsimd
        def _(eng):
            nc.gpsimd.memset(eps[:], EPS).then_inc(pool_set, 1)

        @block.tensor
        def _(eng):
            eng.sem_inc(ex_ready, START)
            eng.sem_inc(be_ps_ready, START)
            eng.sem_inc(ex_read, 4)
            eng.wait_ge(const_loaded, 16 * 8)
            eng.wait_ge(idb_ready, 1)

            def turn_z(c):
                eng.wait_ge(z_loaded, 16 * c + 16)
                for half in range(2):
                    after(eng, z_read, 2 * c + half)
                    for j in range(2):
                        for k in range(KT):
                            tok = slice((2 * half + j) * P, (2 * half + j + 1) * P)
                            mm = nc.tensor.transpose(z_ps[:, (j * KT + k) * P:(j * KT + k + 1) * P], z[:, k, tok], ident[:])
                    mm.then_inc(z_ps_ready, 1)

            def turn_x(c, s):
                eng.wait_ge(x3_ready, c + 1)
                for k in range(KT):
                    after(eng, x_lo_ready, KT * c + k)
                    for j in range(TPC):
                        mm = nc.tensor.transpose(xT_ps[:, j * P:(j + 1) * P], x3[s][:, j, k * P:(k + 1) * P], ident[:])
                    mm.then_inc(xT_ps_ready, 1)

            def hidden(c, s):
                eng.wait_ge(g1_ready, 1)
                eng.wait_ge(x_lo_ready, KT * (c + 1))
                after(eng, gT_ready, c)
                for k in range(KT):
                    nc.tensor.matmul(rt_ps[:], g1_hi[:, k], x_hi[s][:, k], start=k == 0, stop=False)
                    nc.tensor.matmul(rt_ps[:], g1_hi[:, k], x_lo[s][:, k], start=False, stop=False)
                    mm = nc.tensor.matmul(rt_ps[:], g1_lo[:, k], x_hi[s][:, k], start=False, stop=k == KT - 1)
                mm.then_inc(rt_ready, 1)

            def logits(c):
                eng.wait_ge(hid_ready, c + 1)
                for j in range(TPC):
                    mm = nc.tensor.matmul(rt_ps[:, j * E2:(j + 1) * E2], hT[:, j * P:(j + 1) * P], g2[:], start=True, stop=True)
                mm.then_inc(rt_ready, 1)

            def turn_gates(c):
                eng.wait_ge(gst_ready, c + 1)
                for j in range(TPC):
                    mm = nc.tensor.transpose(rt_ps[0:EB, j * P // 2:(j + 1) * P // 2].bitcast(BF16),
                                             gst[:, j].rearrange("p a e -> p (a e)"), idb[:])
                mm.then_inc(rt_ready, 1)

            def experts(c, s, j):
                tok = slice(j * P, (j + 1) * P)
                if j == 0:
                    eng.wait_ge(gT_ready, c + 1)
                eng.wait_ge(be_ready, 1)
                after(eng, be_read, TPC * c + j + START)
                nc.tensor.matmul(be_ps[:, 0:D], gT[s][:, tok], be_stack[:], start=True, stop=True).then_inc(be_ps_ready, 1)
                for n in range(NW2):
                    if isinstance(c, int) and c == 0 and j == 0:
                        eng.wait_ge(we_lo_ready, n + 1)
                    eng.wait_ge(ex_read, (TPC * c + j) * NW2 + n + 1)
                    bank = (j * NW2 + n) % 4
                    cols = slice(n * CH, (n + 1) * CH)
                    for k in range(KT):
                        nc.tensor.matmul(ex[:, bank], x_hi[s][:, k, tok], we_hi[:, k, cols], start=k == 0, stop=False)
                        nc.tensor.matmul(ex[:, bank], x_hi[s][:, k, tok], we_lo[:, k, cols], start=False, stop=False)
                        mm = nc.tensor.matmul(ex[:, bank], x_lo[s][:, k, tok], we_hi[:, k, cols], start=False, stop=k == KT - 1)
                    mm.then_inc(ex_ready, 1)

            turn_z(0)
            turn_x(0, 0)
            hidden(0, 0)
            logits(0)
            turn_gates(0)
            eng.wait_ge(we_lo_ready, NW2)

            def chunks(i, last):
                for s in range(2):
                    c = 2 * i + s
                    more = not (last and s == 1)
                    if more:
                        turn_z(c + 1)
                    experts(c, s, 0)
                    if more:
                        turn_x(c + 1, 1 - s)
                        hidden(c + 1, 1 - s)
                    experts(c, s, 1)
                    if more:
                        logits(c + 1)
                    experts(c, s, 2)
                    if more:
                        turn_gates(c + 1)
                    experts(c, s, 3)

            with eng.Fori(0, NCH // 2 - 1) as i:
                chunks(i, False)
            chunks(NCH // 2 - 1, True)

        @block.scalar
        def _(eng):
            eng.wait_ge(const_loaded, 16 * 8)
            eng.wait_ge(pool_set, 1)

            def round_x(c, s):
                for k in range(KT):
                    eng.wait_ge(xT_ps_ready, KT * c + k + 1)
                    after(eng, ex_ready, TPC * NW2 * (c - 1) + START)
                    nc.scalar.copy(x_hi[s][:, k], xT_ps[:]).then_inc(x_hi_ready, 1)

            def gelu(c):
                eng.wait_ge(rt_ready, 3 * c + 1)
                nc.scalar.activation(hT[:], rt_ps[0:HG], ACT.Gelu, bias=b1[:]).then_inc(hid_ready, 1)

            def exponentials(c):
                eng.wait_ge(shifted, c + 1)
                nc.scalar.activation(pr[:], pr[:], ACT.Exp).then_inc(exp_ready, 1)

            def turned(c, s):
                eng.wait_ge(rt_ready, 3 * c + 3)
                after(eng, be_ps_ready, TPC * (c - 1) + START)
                nc.scalar.copy(gT[s][:], rt_ps[0:EB, 0:CH // 2].bitcast(BF16)).then_inc(gT_ready, 1)

            for n in range(NW2):
                eng.wait_ge(wraw_loaded[n % 2], 16 * (n // 2 + 1))
                nc.scalar.copy(we_hi[:, :, n * CH:(n + 1) * CH], wraw[:, n % 2]).then_inc(we_hi_ready, 1)
            eng.wait_ge(var_ready, 1)
            nc.scalar.activation(std[:], mv[:, :, 1], ACT.Sqrt, bias=eps[:]).then_inc(std_ready, 1)
            round_x(0, 0)
            gelu(0)
            exponentials(0)
            turned(0, 0)

            def chunks(i, last):
                for s in range(2):
                    c = 2 * i + s
                    more = not (last and s == 1)
                    base = 5 * c + 1
                    if more:
                        eng.wait_ge(var_ready, base + 1)
                        nc.scalar.activation(std[:], mv[:, :, 1], ACT.Sqrt, bias=eps[:]).then_inc(std_ready, 1)
                        base = base + 1
                    for j in range(TPC):
                        if j == 1 and more:
                            round_x(c + 1, 1 - s)
                            gelu(c + 1)
                        if j == 2 and more:
                            exponentials(c + 1)
                        eng.wait_ge(var_ready, base + j + 1)
                        nc.scalar.activation(ostd[:], omv[:, 1:2], ACT.Sqrt, bias=eps[:]).then_inc(std_ready, 1)
                        if j == 2 and more:
                            turned(c + 1, 1 - s)

            with eng.Fori(0, NCH // 2 - 1) as i:
                chunks(i, False)
            chunks(NCH // 2 - 1, True)

        @block.vector
        def _(eng):
            eng.sem_inc(be_read, START)
            step = Steps(eng, dve_step)
            eng.wait_ge(const_loaded, 16 * 8)
            eng.wait_ge(pool_set, 1)

            def moments(c, s, count):
                for half in range(2):
                    eng.wait_ge(z_ps_ready, 2 * c + half + 1)
                    for j in range(2):
                        ins = nc.vector.bn_stats(stats[:, 2 * half + j], z_ps[:, j * D:(j + 1) * D])
                    step(ins)
                    nc.vector.tensor_copy(x3[s][:, 2 * half:2 * half + 2], z_ps[:].rearrange("p (j d) -> p j d", j=2)).then_inc(z_read, 1)
                eng.drain()
                for j in range(TPC):
                    ins = nc.vector.bn_aggr(mv[:, j], stats[:, j])
                ins.then_inc(var_ready, 1)
                eng.wait_ge(std_ready, count)
                step(nc.vector.reciprocal(rstd[:], std[:]))
                for j in range(TPC):
                    ins = nc.vector.tensor_scalar(x3[s][:, j], x3[s][:, j], mv[:, j, 0:1], rstd[:, j:j + 1], ALU.subtract, ALU.mult)
                ins.then_inc(x3_ready, 1)

            def round_x(c, s):
                for k in range(KT):
                    eng.wait_ge(x_hi_ready, KT * c + k + 1)
                    nc.vector.tensor_tensor(x_lo[s][:, k], xT_ps[:], x_hi[s][:, k].bitcast(F32), ALU.subtract).then_inc(x_lo_ready, 1)

            def shift(c):
                eng.wait_ge(rt_ready, 3 * c + 2)
                step(nc.vector.tensor_tensor(pr[:], rt_ps[:, 0:TPC * E2].rearrange("p (j e) -> p j e", j=TPC),
                                             b2[:].unsqueeze(1).to_broadcast([P, TPC, E2]), ALU.add))
                step(nc.vector.tensor_reduce(red[:], pr[:], AX, ALU.max))
                nc.vector.tensor_tensor(pr[:], pr[:], red[:].unsqueeze(2).to_broadcast([P, TPC, E2]), ALU.subtract).then_inc(shifted, 1)

            def gates(c, s):
                over = lambda x: x.unsqueeze(2).to_broadcast([P, TPC, E2])
                eng.wait_ge(exp_ready, c + 1)
                step(nc.vector.tensor_reduce(red[:], pr[:], AX, ALU.add))
                step(nc.vector.reciprocal(inv[:], red[:]))
                nc.vector.tensor_tensor(pr[:], pr[:], over(inv[:]), ALU.mult)
                eng.drain()
                for j in range(TPC):
                    nc.vector.max(top[:, j], pr[:, j])
                eng.drain()
                for j in range(TPC):
                    ins = nc.vector.max_index(topi[:, j], top[:, j], pr[:, j])
                step(ins)
                step(nc.vector.tensor_copy(topf[:], topi[:]))
                places = iota[:].unsqueeze(1).to_broadcast([P, TPC, E2])
                step(nc.vector.tensor_tensor(gate[s][:], places, over(topf[:, :, 0]), ALU.is_equal))
                step(nc.vector.tensor_tensor(gate[s][:], gate[s][:], over(top[:, :, 0]), ALU.mult))
                step(nc.vector.tensor_tensor(gtmp[:], places, over(topf[:, :, 1]), ALU.is_equal))
                step(nc.vector.tensor_tensor(gtmp[:], gtmp[:], over(top[:, :, 1]), ALU.mult))
                step(nc.vector.tensor_tensor(gate[s][:], gate[s][:], gtmp[:], ALU.add))
                several = lambda x, n: x.unsqueeze(2).to_broadcast([P, TPC, n, E2])
                step(nc.vector.tensor_copy(gst[:, :, 0:3], several(gate[s][:], 3)))
                step(nc.vector.tensor_tensor(gtmp[:], gate[s][:], gst[:, :, 0], ALU.subtract))
                step(nc.vector.tensor_copy(gst[:, :, 3:5], several(gtmp[:], 2)))
                nc.vector.tensor_tensor(gst[:, :, 5], gtmp[:], gst[:, :, 3], ALU.subtract).then_inc(gst_ready, 1)
                eng.wait_ge(gst_ready, c + 1)

            def mix(c, s, j):
                tile = TPC * c + j
                eng.wait_ge(be_ps_ready, tile + 1 + START)
                even, odd = acc[:, j % 2, 0], acc[:, j % 2, 1]
                nc.vector.tensor_tensor(even, be_ps[:, 0:D], x3[s][:, j], ALU.add).then_inc(be_read, 1)
                eng.wait_ge(be_read, tile + 1 + START)
                for n in range(NW2):
                    eng.wait_ge(ex_ready, tile * NW2 + n + 1 + START)
                    bank = (j * NW2 + n) % 4
                    step(nc.vector.scalar_tensor_tensor(out=even, in0=ex[:, bank, 0:D], scalar=gate[s][:, j, 2 * n:2 * n + 1],
                                                        in1=even, op0=ALU.mult, op1=ALU.add))
                    if n == 0:
                        nc.vector.tensor_scalar(odd, ex[:, bank, D:], gate[s][:, j, 1:2], None, ALU.mult).then_inc(ex_read, 1)
                    else:
                        nc.vector.scalar_tensor_tensor(out=odd, in0=ex[:, bank, D:], scalar=gate[s][:, j, 2 * n + 1:2 * n + 2],
                                                       in1=odd, op0=ALU.mult, op1=ALU.add).then_inc(ex_read, 1)
                    eng.wait_ge(ex_read, tile * NW2 + n + 1 + 4)
                step(nc.vector.tensor_tensor(even, even, odd, ALU.add))

            def last_norm(c, s, j, i, count):
                res = acc[:, j % 2, 0]
                nc.vector.bn_stats(ostats[:], res)
                eng.drain()
                nc.vector.bn_aggr(omv[:], ostats[:]).then_inc(var_ready, 1)
                eng.wait_ge(std_ready, count)
                step(nc.vector.reciprocal(orstd[:], ostd[:]))
                eng.wait_ge(out_stored[j % 2], 16 * (2 * c + j // 2) + START)
                nc.vector.tensor_scalar(out[:, j % 2], res, omv[:, 0:1], orstd[:], ALU.subtract, ALU.mult).then_inc(out_ready, 1)
                eng.wait_ge(out_ready, TPC * c + j + 1)

            nc.vector.tensor_copy(idb[:], ident[:]).then_inc(idb_ready, 1)
            step(nc.vector.tensor_copy(g1_hi[:], g1[:]))
            nc.vector.tensor_tensor(g1_lo[:], g1[:], g1_hi[:].bitcast(F32), ALU.subtract).then_inc(g1_ready, 1)
            step(nc.vector.tensor_copy(bepart[:, 0], be[:]))
            step(nc.vector.tensor_tensor(be[:], be[:], bepart[:, 0], ALU.subtract))
            step(nc.vector.tensor_copy(bepart[:, 1], be[:]))
            step(nc.vector.tensor_tensor(bepart[:, 2], be[:], bepart[:, 1], ALU.subtract))
            step(nc.vector.tensor_scalar(be[:], bepart[:, 0], pick[:, 0:1], None, ALU.mult))
            step(nc.vector.scalar_tensor_tensor(out=be[:], in0=bepart[:, 1], scalar=pick[:, 1:2], in1=be[:], op0=ALU.mult, op1=ALU.add))
            nc.vector.scalar_tensor_tensor(out=be_stack[:], in0=bepart[:, 2], scalar=pick[:, 2:3], in1=be[:],
                                           op0=ALU.mult, op1=ALU.add).then_inc(be_ready, 1)
            for n in range(NW2):
                eng.wait_ge(we_hi_ready, n + 1)
                cols = slice(n * CH, (n + 1) * CH)
                nc.vector.tensor_tensor(we_lo[:, :, cols], wraw[:, n % 2], we_hi[:, :, cols].bitcast(F32), ALU.subtract).then_inc(we_lo_ready, 1)
            moments(0, 0, 1)
            round_x(0, 0)
            shift(0)
            gates(0, 0)

            def chunks(i, last):
                for s in range(2):
                    c = 2 * i + s
                    more = not (last and s == 1)
                    base = 5 * c + 1
                    if more:
                        moments(c + 1, 1 - s, base + 1)
                        base = base + 1
                    for j in range(TPC):
                        if j == 1 and more:
                            round_x(c + 1, 1 - s)
                        mix(c, s, j)
                        if j == 1 and more:
                            shift(c + 1)
                        if j == 2 and more:
                            gates(c + 1, 1 - s)
                        last_norm(c, s, j, i, base + j + 1)

            with eng.Fori(0, NCH // 2 - 1) as i:
                step.enter(i, 2 * (3 + 2 + 12 + TPC * (NW2 + 2)))
                chunks(i, False)
                step.leave(NCH // 2 - 1)
            chunks(NCH // 2 - 1, True)


def host_layout(v):
    import numpy as np

    v = {k: np.asarray(a) for k, a in v.items()}
    f = np.float32

    def cols(w):
        return np.ascontiguousarray(w.reshape(-1, P, w.shape[1]).transpose(1, 0, 2))

    def rows(b):
        return np.ascontiguousarray(b.reshape(-1, P).T)

    def every(b):
        return np.ascontiguousarray(np.broadcast_to(b.reshape(1, -1), (P, b.size)))

    x = v["L0_attn_x"].reshape(NTOK, D)
    a = {}
    a["x"] = x
    a["xT"] = cols(x.T)
    a["wqkv"] = cols(v["L0_attn_W_w"].T)
    a["bqk"] = rows(v["L0_attn_W_b"][:2 * D])
    a["bv"] = every(v["L0_attn_W_b"][2 * D:])
    a["rpb"] = v["L0_attn_rpb"].T
    a["rpb_back"] = v["L0_attn_rpb"].T[:, ::-1]
    eye = np.eye(P, dtype=f)
    a["ident"] = eye
    hidden = np.where(np.arange(P)[None, :] > np.arange(P)[:, None], f(-1e30), f(0))
    a["squares"] = np.stack([eye, eye[::-1], hidden, hidden.T], axis=1)
    a["wproj"] = cols(v["L0_attn_proj_w"].T)
    a["bproj"] = every(v["L0_attn_proj_b"])
    a["ln_g"] = every(v["L0_attn_ln_g"])
    a["ln_b"] = every(v["L0_attn_ln_b"])
    a["keep"] = every(np.array([float((c + 1) % (S // CH) != 0) for c in range(NCH)], f))
    stack = lambda w: w.transpose(1, 0, 2).reshape(D, KR)
    router = v["L0_ffn_router_w1"].T
    a["wq"], a["wk"], a["winv"] = cols(v["L0_ffn_W_Q"]), cols(v["L0_ffn_W_K"]), cols(v["L0_ffn_W_inv"])
    two = lambda f0, f1: np.stack([cols(f0), cols(f1)], axis=1)
    a["vq"] = two(np.concatenate([stack(v["L0_ffn_V_fwd"]), router], 1), np.concatenate([stack(v["L0_ffn_W_inv_exp"]), router], 1))
    a["vk"] = two(stack(v["L0_ffn_W_fwd"]), stack(v["L0_ffn_V_inv"]))
    a["u"] = two(stack(v["L0_ffn_U_fwd"]), stack(v["L0_ffn_U_inv"]))
    a["wo"] = cols(v["L0_ffn_W_O"].T)
    a["bffn"] = cols(np.tile(np.concatenate([v["L0_ffn_b_fwd"], v["L0_ffn_b_inv"]]).T, (1, NSP)))
    a["alpha"] = np.broadcast_to(v["L0_ffn_alpha_bi"].reshape(1, 1), (P, 1))
    a["alphas"] = np.tile(np.concatenate([np.ones(KE, f), np.broadcast_to(v["L0_ffn_alpha_bi"].reshape(1), (KE,))]), NSP)[:, None]
    left, right = (0, 0, 0, 1, 1, 2), (0, 1, 2, 0, 1, 0)

    def picked(width):
        return np.repeat(np.eye(3, dtype=f)[list(right)], width, axis=0)

    a["pick"] = picked(NW)
    a["w2"] = cols(v["L0_ffn_router_w2"].T)
    a["b1"] = rows(v["L0_ffn_router_b1"])
    a["b2"] = every(v["L0_ffn_router_b2"])
    a["be"] = every(v["L0_ffn_expert_bias"])
    sel = np.zeros((NSP, 2, KE, NG, P), f)
    for g in range(NG):
        for p in range(P):
            sel[[0, 3, 5], g // GB, g % GB * (P // R) + p // R, g, p] = 1
    a["sel"] = sel.reshape(NSP * NW, NG, P)
    a["count"] = np.ascontiguousarray(np.tile(np.arange(1, S + 1, dtype=f), B).reshape(NT, P).T)
    a["w_dt"] = cols(v["L1_attn_W_dt"].T)
    a["b_dt"], a["dt_bias"], a["d_skip"] = rows(v["L1_attn_b_dt"]), rows(v["L1_attn_dt_bias"]), rows(v["L1_attn_D_skip"])
    blocks = lambda b: b.reshape(KT, P, N).transpose(1, 0, 2)
    a["log_a"] = blocks(v["L1_attn_log_A"])
    a["b_b"], a["b_c"] = blocks(v["L1_attn_b_B"]), blocks(v["L1_attn_b_C"])
    wbc = np.stack([w.reshape(KT, P, N, KT, P) for w in (v["L1_attn_W_B"], v["L1_attn_W_C"])])
    a["w_bc"] = wbc.transpose(3, 1, 5, 4, 0, 2).reshape(N, KT, P, KT, 2 * P)
    a["g1"] = cols(np.concatenate([v["L1_ffn_wg1"], np.zeros((D, P - HG), f)], 1))
    a["g1b"] = v["L1_ffn_bg1"][:, None]
    a["g2"] = v["L1_ffn_wg2"][:, :E2]
    a["g2b"] = every(v["L1_ffn_bg2"][:E2])
    a["iota"] = every(np.arange(E2, dtype=f))
    a["bmoe"] = np.tile(v["L1_ffn_be"], (NSP, 1))
    a["pick20"] = picked(E2)
    a["we"] = v["L1_ffn_We"].transpose(1, 0, 2).reshape(KT, P, E2 * D).transpose(1, 0, 2)
    return {k: np.ascontiguousarray(w) for k, w in a.items()}


def open_fused(nc, ctx, t):
    sp = Space(nc, ctx, "fus")
    t.aq_hi, t.aq_lo = sp.sb("aq_hi", [P, 2, KT, WF], F32R), sp.sb("aq_lo", [P, 2, KT, WF], F32R)
    t.ak_hi, t.ak_lo = sp.sb("ak_hi", [P, 2, KT, KR], F32R), sp.sb("ak_lo", [P, 2, KT, KR], F32R)
    t.uo = sp.sb("uo", [P, NG, D])
    t.bo_stack = sp.sb("bo_stack", [NSP * NW, D], BF16)
    t.router2, t.routerb = sp.sb("router2", [P, KT, KE]), sp.sb("routerb", [P, KT])
    t.logitb = sp.sb("logitb", [P, KE])
    t.sel_sb = sp.sb("sel", [NSP * NW, NG, P], BF16)
    t.count_sb = sp.sb("count", [P, NT])


class Tensors:
    pass


def declare(nc, arrays):
    def array(name):
        a = arrays[name]
        return nc.dram_tensor(f"in_{name}", a.shape, mybir.dt.from_np(a.dtype), kind="ExternalInput").ap()

    t = Tensors()
    t.x = array("x")
    t.xT = array("xT")
    t.wqkv = array("wqkv")
    t.bqk = array("bqk")
    t.bv = array("bv")
    t.rpb = array("rpb")
    t.rpb_back = array("rpb_back")
    t.ident = array("ident")
    t.squares = array("squares")
    t.wproj = array("wproj")
    t.bproj = array("bproj")
    t.ln_g = array("ln_g")
    t.ln_b = array("ln_b")
    t.keep = array("keep")
    t.wq = array("wq")
    t.wk = array("wk")
    t.winv = array("winv")
    t.vq = array("vq")
    t.vk = array("vk")
    t.u = array("u")
    t.wo = array("wo")
    t.bffn = array("bffn")
    t.alpha = array("alpha")
    t.alphas = array("alphas")
    t.pick = array("pick")
    t.w2 = array("w2")
    t.b1 = array("b1")
    t.b2 = array("b2")
    t.be = array("be")
    t.sel = array("sel")
    t.count = array("count")
    t.w_dt = array("w_dt")
    t.b_dt = array("b_dt")
    t.dt_bias = array("dt_bias")
    t.d_skip = array("d_skip")
    t.log_a = array("log_a")
    t.b_b = array("b_b")
    t.b_c = array("b_c")
    t.w_bc = array("w_bc")
    t.g1 = array("g1")
    t.g1b = array("g1b")
    t.g2 = array("g2")
    t.g2b = array("g2b")
    t.iota = array("iota")
    t.bmoe = array("bmoe")
    t.pick20 = array("pick20")
    t.we = array("we")
    return t


def program(nc, t):
    t.qk = nc.dram_tensor("qk_parts", (2, 3, D, NTOK), BF16).ap()
    t.qk4 = t.qk.rearrange("s a (h r) n -> s a h r n", r=HD)
    t.tables = nc.dram_tensor("bias_tables", (4, H, EW), BF16).ap()
    t.x1 = nc.dram_tensor("x1", (NTOK, D), F32).ap()
    t.x1T = nc.dram_tensor("x1T", (P, KT, NTOK), F32).ap()
    t.cumT = nc.dram_tensor("x1T_sums", (P, KT, NTOK), F32).ap()
    t.x2T = nc.dram_tensor("x2T", (P, KT, NTOK), F32).ap()
    with ExitStack() as ctx:
        sp = Space(nc, ctx, "att_io")
        t.v_sb, t.o_sb = sp.sb("v", [P, NT, D]), sp.sb("o", [P, NT, D])
        phase_qkv(nc, t)
        phase_attention(nc, t)
        phase_project(nc, t)
    with ExitStack() as ctx:
        open_fused(nc, ctx, t)
        phase_combine(nc, t)
        phase_fused(nc, t)
    with ExitStack() as ctx:
        t.z_sb = Space(nc, ctx, "ssm_io").sb("z", [P, KT, NTOK])
        phase_scan(nc, t)
        phase_mixture(nc, t)


def kernel(**inputs):
    import numpy as np
    import concourse.bacc as bacc
    from concourse.bass_utils import run_bass_kernel_spmd

    arrays = host_layout(inputs)
    nc = bacc.Bacc("TRN2", target_bir_lowering=False, num_devices=1)
    t = declare(nc, arrays)
    t.out = nc.dram_tensor("out", (NTOK, D), F32, kind="ExternalOutput").ap()
    program(nc, t)
    r = run_bass_kernel_spmd(nc, [{f"in_{k}": a for k, a in arrays.items()}], core_ids=[0])
    return np.asarray(r.results[0]["out"]).reshape(B, S, D)
```

```python
from contextlib import ExitStack

import concourse.bass as bass
import concourse.mybir as mybir

ALU = mybir.AluOpType
ACT = mybir.ActivationFunctionType
AX = mybir.AxisListType.X
F32 = mybir.dt.float32
BF16 = mybir.dt.bfloat16
F32R = mybir.dt.float32r
U32 = mybir.dt.uint32

P = 128
B, S, D = 2, 2048, 256
NTOK = B * S
KT = D // P
CH = 512
NCH = NTOK // CH
TPC = CH // P
NT = NTOK // P
TB = S // P
H = 16
HD = D // H
RPB = 1023
EW = 1152
EPS = 1e-5
START = 1


def ds(start, size):
    return bass.ds(start, size)


class Steps:

    def __init__(self, eng, sem):
        self.eng, self.sem, self.base, self.n = eng, sem, 0, 0

    def __call__(self, ins):
        ins.then_inc(self.sem, 1)
        self.n += 1
        self.eng.wait_ge(self.sem, self.base + self.n)

    def go(self, ins):
        ins.then_inc(self.sem, 1)
        self.n += 1

    def wait(self):
        self.eng.wait_ge(self.sem, self.base + self.n)

    def enter(self, i, per):
        self.start, self.per = self.base + self.n, per
        self.base, self.n = i * per + self.start, 0

    def leave(self, times):
        assert self.n == self.per, f"{self.n} steps in the body, {self.per} stated"
        self.base, self.n = self.start + times * self.per, 0


def after(eng, sem, value):
    if not isinstance(value, int) or value > 0:
        eng.wait_ge(sem, value)


class Space:

    def __init__(self, nc, ctx, prefix):
        self.nc, self.ctx, self.prefix = nc, ctx, prefix

    def sb(self, name, shape, dt=F32):
        return self.ctx.enter_context(self.nc.sbuf_tensor(f"{self.prefix}_{name}", shape, dt))

    def psum(self, name, shape, dt=F32):
        return self.ctx.enter_context(self.nc.psum_tensor(f"{self.prefix}_{name}", shape, dt))

    def sem(self, name):
        return self.nc.alloc_semaphore(f"{self.prefix}_{name}")


class Region:

    def __init__(self, whole):
        self.whole, self.at = whole[:].rearrange("p k n -> p (k n)"), 0

    def __call__(self, *shape):
        size = 1
        for n in shape:
            size *= n
        flat = self.whole[:, self.at:self.at + size]
        self.at += size
        names = "abc"[:len(shape)]
        return flat.rearrange(f"p ({' '.join(names)}) -> p {' '.join(names)}", **dict(zip(names, shape)))


def phase_qkv(nc, t):
    with nc.cleanup_on_exit(), ExitStack() as ctx:
        sp = Space(nc, ctx, "qkv")
        w = sp.sb("w", [P, KT, 3 * D])
        bqk = sp.sb("bqk", [P, 4])
        bqs = sp.sb("bqs", [P, 2])
        bv = sp.sb("bv", [P, D])
        x = [sp.sb(f"x{s}", [P, KT, CH]) for s in range(2)]
        whole = sp.sb("whole", [P, 4, CH])
        rest = sp.sb("rest", [P, 2, CH])
        parts = [sp.sb(f"parts{s}", [P, 4, 3, CH], BF16) for s in range(2)]
        tab = sp.sb("tab", [H, 2, EW])
        clamped = sp.sb("clamped", [H, 1])
        tabrest = sp.sb("tabrest", [H, EW])
        tabparts = sp.sb("tabparts", [H, 4, EW], BF16)
        qk_ps = sp.psum("qk_ps", [P, 4, CH])
        v_ps = sp.psum("v_ps", [P, 4, CH])

        w_loaded, tab_loaded = sp.sem("w_loaded"), sp.sem("tab_loaded")
        x_loaded = [sp.sem(f"x_loaded{s}") for s in range(2)]
        qk_ready, qk_turns = sp.sem("qk_ready"), sp.sem("qk_turns")
        v_ready, v_turns = sp.sem("v_ready"), sp.sem("v_turns")
        whole_turns = sp.sem("whole_turns")
        parts_ready = sp.sem("parts_ready")
        stored = [sp.sem(f"stored{s}") for s in range(2)]
        tab_ready, tab_stored = sp.sem("tab_ready"), sp.sem("tab_stored")
        dve_step, act_step, tab_zeroed = sp.sem("dve_step"), sp.sem("act_step"), sp.sem("tab_zeroed")
        block = ctx.enter_context(nc.Block())

        @block.sync
        def _(eng):
            for sem in stored:
                eng.sem_inc(sem, START)
            for dst, src in ((w, t.wqkv), (bqk, t.bqk), (bv, t.bv)):
                eng.dma_start(dst[:], src).then_inc(w_loaded, 16)
            eng.wait_ge(tab_zeroed, 1)
            eng.dma_start(tab[:, 0, 0:RPB], t.rpb).then_inc(tab_loaded, 16)
            eng.dma_start(tab[:, 1, P:P + RPB], t.rpb_back).then_inc(tab_loaded, 16)

            def load(c, s):
                eng.dma_start(x[s][:], t.xT[:, :, ds(c * CH, CH)]).then_inc(x_loaded[s], 16)

            def store(c, s):
                for m in range(4):
                    eng.wait_ge(parts_ready, 4 * c + m + 1)
                    eng.dma_start(t.qk[m // 2, :, (m % 2) * P:(m % 2 + 1) * P, ds(c * CH, CH)].rearrange("a p n -> p a n"),
                                  parts[s][:, m]).then_inc(stored[s], 16)

            for s in range(2):
                load(s, s)
            eng.wait_ge(tab_ready, 1)
            eng.dma_start(t.tables.rearrange("a h e -> h a e"), tabparts[:]).then_inc(tab_stored, 16)
            with eng.Fori(0, NCH // 2 - 1) as i:
                for s in range(2):
                    eng.wait_ge(v_ready, 4 * (2 * i + s) + 4)
                    load(2 * i + s + 2, s)
                for s in range(2):
                    store(2 * i + s, s)
            for s in range(2):
                store(NCH - 2 + s, s)
            for s in range(2):
                eng.wait_ge(stored[s], 64 * (NCH // 2) + START)
            eng.wait_ge(tab_stored, 16)

        @block.gpsimd
        def _(eng):
            nc.gpsimd.memset(tab[:], 0.0).then_inc(tab_zeroed, 1)

        @block.tensor
        def _(eng):
            eng.wait_ge(w_loaded, 48)
            with eng.Fori(0, NCH // 2) as i:
                for s in range(2):
                    c = 2 * i + s
                    eng.wait_ge(x_loaded[s], 16 * i + 16)
                    for m in range(4):
                        eng.wait_ge(qk_turns, 4 * c + m + 1)
                        for k in range(KT):
                            mm = nc.tensor.matmul(qk_ps[:, m], w[:, k, m * P:(m + 1) * P], x[s][:, k],
                                                  start=k == 0, stop=k == KT - 1)
                        mm.then_inc(qk_ready, 1)
                    for j in range(TPC):
                        eng.wait_ge(v_turns, 4 * c + j + 1)
                        for k in range(KT):
                            mm = nc.tensor.matmul(v_ps[:, j, 0:D], x[s][:, k, j * P:(j + 1) * P],
                                                  w[:, k, 2 * D:], start=k == 0, stop=k == KT - 1)
                        mm.then_inc(v_ready, 1)

        @block.scalar
        def _(eng):
            eng.sem_inc(qk_turns, 4)
            eng.wait_ge(w_loaded, 48)
            nc.scalar.mul(bqs[:], bqk[:, 0:2], 1.0 / HD).then_inc(act_step, 1)
            eng.wait_ge(act_step, 1)
            with eng.Fori(0, NCH // 2) as i:
                for s in range(2):
                    c = 2 * i + s
                    for m in range(4):
                        eng.wait_ge(qk_ready, 4 * c + m + 1)
                        eng.wait_ge(whole_turns, 4 * c + m + 1)
                        if m == 0:
                            eng.wait_ge(stored[s], 64 * i + START)
                        for n, dst in enumerate((parts[s][:, m, 0], whole[:, m])):
                            ins = nc.scalar.activation(dst, qk_ps[:, m], ACT.Identity,
                                                       bias=bqs[:, m:m + 1] if m < 2 else bqk[:, m:m + 1],
                                                       scale=1.0 / HD if m < 2 else 1.0)
                        ins.then_inc(qk_turns, 1)

        @block.vector
        def _(eng):
            step = Steps(eng, dve_step)
            eng.sem_inc(whole_turns, 4)
            eng.sem_inc(v_turns, 4)
            eng.wait_ge(w_loaded, 48)
            eng.wait_ge(tab_loaded, 32)
            step(nc.vector.tensor_copy(clamped[:], tab[:, 0, RPB - 1:RPB]))
            step(nc.vector.tensor_scalar(tab[:, 0, 0:RPB], tab[:, 0, 0:RPB], clamped[:, 0:1], None, ALU.subtract))
            step(nc.vector.tensor_scalar(tab[:, 1, P:P + RPB], tab[:, 1, P:P + RPB], clamped[:, 0:1], None, ALU.subtract))
            step(nc.vector.tensor_copy(tabparts[:, 0], tab[:, 0]))
            step(nc.vector.tensor_copy(tabparts[:, 1], tab[:, 1]))
            step(nc.vector.tensor_tensor(tabrest[:], tab[:, 1], tabparts[:, 1], ALU.subtract))
            step(nc.vector.tensor_copy(tabparts[:, 2], tabrest[:]))
            nc.vector.tensor_tensor(tabparts[:, 3], tabrest[:], tabparts[:, 2], ALU.subtract).then_inc(tab_ready, 1)
            with eng.Fori(0, NCH // 2) as i:
                step.enter(i, 2 * 4 * 2)
                for s in range(2):
                    c = 2 * i + s
                    for m in range(4):
                        p = parts[s]
                        eng.wait_ge(qk_turns, 4 * c + m + 5)
                        step(nc.vector.tensor_tensor(rest[:, m % 2], whole[:, m], p[:, m, 0], ALU.subtract))
                        eng.sem_inc(whole_turns, 1)
                        step(nc.vector.tensor_copy(p[:, m, 1], rest[:, m % 2]))
                        nc.vector.tensor_tensor(p[:, m, 2], rest[:, m % 2], p[:, m, 1],
                                                ALU.subtract).then_inc(parts_ready, 1)
                        eng.wait_ge(parts_ready, 4 * c + m + 1)
                    for j in range(TPC):
                        eng.wait_ge(v_ready, 4 * c + j + 1)
                        nc.vector.tensor_tensor(t.v_sb[:, ds(c * TPC + j, 1), :], v_ps[:, j, 0:D].unsqueeze(1),
                                                bv[:].unsqueeze(1), ALU.add).then_inc(v_turns, 1)
                step.leave(NCH // 2)


def attention_pieces(J):
    return [(q, min(q + 2 * CH, S)) for q in range(J * P, S, 2 * CH)]


PIECES = [len(attention_pieces(J)) for J in range(TB)]
GROUPS = [(I * P + P + CH - 1) // CH for I in range(TB)]
NP2, NG1 = sum(PIECES), sum(GROUPS)
FAR = 8
QUAD = 4
EARLY = 10


def score_steps(j):
    if j < EARLY:
        return ((j + 1, 0),), ((j + 1, 1),)
    if j == EARLY:
        return ((j + 1, 0),), ((j + 2, 0),)
    if j < TB - 2:
        return ((j + 2, 0),), ()
    return (((TB, 0),), ()) if j == TB - 2 else ((), ((TB, 1),))


ROWS = 6 * HD


def phase_attention(nc, t):
    with nc.cleanup_on_exit(), ExitStack() as ctx:
        sp = Space(nc, ctx, "att")
        qs = [sp.sb(f"qs{s}", [P, S], BF16) for s in range(QUAD)]
        ks = [sp.sb(f"ks{s}", [P, S], BF16) for s in range(QUAD)]
        near = [sp.sb(f"near{s}", [P, 8 * P], BF16) for s in range(2)]
        far = [sp.sb(f"far{s}", [P, 3, 8 * P], BF16) for s in range(2)]
        prob = sp.sb("prob", [P, 4, S])
        vst = [sp.sb(f"vst{s}", [P, TB, 32]) for s in range(2)]
        partmax = sp.sb("partmax", [P, TB, 4])
        mx = sp.sb("mx", [P, TB])
        negmax = sp.sb("negmax", [P, 2, TB], BF16)
        negmaxT = [sp.sb(f"negmaxT{s}", [2 * TB, P], BF16) for s in range(2)]
        oT = sp.sb("oT", [P, CH])
        rsum = sp.sb("rsum", [P, 4, 4])
        squares = sp.sb("squares", [P, 4, P])
        squares_b = sp.sb("squares_b", [P, 4, P], BF16)
        ident = squares[:, 0]
        idb, flip, maskq, maskk = (squares_b[:, n] for n in range(4))
        s1 = sp.psum("s1", [P, 2, CH])
        s2 = sp.psum("s2", [P, 2, 2 * CH])
        o_ps = sp.psum("o_ps", [P, CH])
        turn = sp.psum("turn", [P, CH])

        const_loaded, const_cast = sp.sem("const_loaded"), sp.sem("const_cast")
        stack_loaded = [sp.sem(f"stack_loaded{s}") for s in range(QUAD)]
        near_loaded = [sp.sem(f"near_loaded{s}") for s in range(2)]
        far_loaded = [sp.sem(f"far_loaded{s}") for s in range(2)]
        max_loaded = [sp.sem(f"max_loaded{s}") for s in range(QUAD)]
        s1_ready = sp.sem("s1_ready")
        s1_turns = sp.sem("s1_turns")
        s2_ready = sp.sem("s2_ready")
        s2_turns = sp.sem("s2_turns")
        prob_turns = sp.sem("prob_turns")
        vst_turns = sp.sem("vst_turns")
        vst_ready = sp.sem("vst_ready")
        negmax_ready = sp.sem("negmax_ready")
        negmaxT_ready = sp.sem("negmaxT_ready")
        turn_ready = sp.sem("turn_ready")
        turn_free = sp.sem("turn_free")
        oT_ready = sp.sem("oT_ready")
        pool_set = sp.sem("pool_set")
        dve_step = sp.sem("dve_step")
        block = ctx.enter_context(nc.Block())
        NQ = B * H // QUAD

        def window(part, h):
            at = t.tables[part, ds(h, 1), 0:1]
            return bass.AP(tensor=at.tensor, offset=at.offset, ap=[[1, P], [1, 8 * P]])

        @block.sync
        def _(eng):
            for sem in max_loaded:
                eng.sem_inc(sem, START)
            eng.dma_start(squares[:], t.squares).then_inc(const_loaded, 16)

            def load_stack(h, b, s):
                tok = slice(b * S, (b + 1) * S)
                for n, (lo, parts) in enumerate(((0, "111"), (3, "22"), (5, "3"))):
                    for r, part in enumerate(parts):
                        eng.dma_start(qs[s][(lo + r) * HD:(lo + r + 1) * HD, :],
                                      t.qk4[0, int(part) - 1, ds(h, 1), :, tok].rearrange("a r n -> (a r) n")).then_inc(stack_loaded[s], 16)
                for lo, num in ((0, 3), (3, 2), (5, 1)):
                    eng.dma_start(ks[s][lo * HD:(lo + num) * HD, :],
                                  t.qk4[1, 0:num, ds(h, 1), :, tok].rearrange("c a r n -> c (a r) n")).then_inc(stack_loaded[s], 16)

            def load_near(h, s):
                eng.dma_start(near[s][:], window(0, h)).then_inc(near_loaded[s], 16)

            def load_far(h, s):
                for part in range(3):
                    eng.dma_start(far[s][:, part], window(1 + part, h)).then_inc(far_loaded[s], 16)

            def store_max(v, i, k):
                eng.wait_ge(negmaxT_ready, v + 1)
                for a in range(2):
                    eng.dma_start(qs[k][ROWS + a:ROWS + a + 1, :],
                                  negmaxT[k % 2][a * TB:(a + 1) * TB, :]).then_inc(max_loaded[k], 16)

            load_near(0, 0)
            load_stack(0, 0, 0)
            load_stack(0, 1, 1)
            load_far(0, 0)
            load_stack(1, 0, 2)
            load_near(1, 1)
            store_max(0, 0, 0)

            def units(i, last):
                for k in range(QUAD):
                    u = QUAD * i + k
                    eng.wait_ge(s2_ready, NP2 * u + START)
                    if k % 2 == 0:
                        h = 2 * i + k // 2
                        if not (last and k == 2):
                            load_far(h + 1, (k // 2 + 1) % 2)
                        if not last:
                            eng.wait_ge(s1_ready, NG1 * (u + 2))
                            load_near(h + 2, k // 2)
                    if not last or k == 0:
                        load_stack(2 * i + (k + 3) // 2, (k + 3) % 2, (k + 3) % QUAD)
                    if not last or k < 3:
                        store_max(u + 1, i, (k + 1) % QUAD)

            with eng.Fori(0, NQ - 1) as i:
                units(i, False)
            units(NQ - 1, True)

        @block.gpsimd
        def _(eng):
            step = Steps(eng, pool_set)
            for s in range(QUAD):
                step(nc.gpsimd.memset(ks[s][ROWS:ROWS + 2, :], 1.0))
            for s in range(2):
                step(nc.gpsimd.memset(vst[s][:, :, 16:17], 1.0))
                step(nc.gpsimd.memset(vst[s][:, :, 17:32], 0.0))
            with eng.Fori(0, NQ) as i:
                for k in range(QUAD):
                    u = QUAD * i + k
                    b = k % 2
                    eng.wait_ge(vst_turns, u + 1)
                    nc.gpsimd.tensor_copy(vst[b][:, :, 0:HD],
                                          t.v_sb[:, b * TB:(b + 1) * TB, ds((2 * i + k // 2) * HD, HD)]).then_inc(vst_ready, 1)

        @block.tensor
        def _(eng):
            eng.sem_inc(s2_ready, START)
            eng.sem_inc(vst_turns, 2)
            eng.sem_inc(prob_turns, 4)
            eng.wait_ge(const_loaded, 16)
            eng.wait_ge(const_cast, 1)
            eng.wait_ge(pool_set, 8)

            def maxima(v, s, hs, I, banks=None):
                before = sum(GROUPS[I + 1:])
                for g in range(GROUPS[I]) if banks is None else banks:
                    n = NG1 * v + before + g
                    lo, hi = g * CH, min(g * CH + CH, (I + 1) * P)
                    bank = s1[:, (before + g) % 2]
                    eng.wait_ge(s1_turns, n + 1)
                    last = hi == (I + 1) * P
                    near_hi = min(hi, (I - FAR + 1) * P)
                    mm = nc.tensor.matmul(bank[:, 0:hi - lo], qs[s][0:ROWS, I * P:(I + 1) * P],
                                          ks[s][0:ROWS, lo:hi], start=True,
                                          stop=not last and near_hi <= lo)
                    if near_hi > lo:
                        at = 15 * P - I * P + lo
                        mm = nc.tensor.matmul(bank[:, 0:near_hi - lo], flip, near[hs][:, at:at + near_hi - lo],
                                              start=False, stop=not last)
                    if last:
                        mm = nc.tensor.matmul(bank[:, I * P - lo:hi - lo], idb, maskq, start=False, stop=True)
                    mm.then_inc(s1_ready, 1)

            def scores(u, s, hs, J, n):
                before = sum(PIECES[:J])
                if n < PIECES[J]:
                    q0, q1 = attention_pieces(J)[n]
                    slot = s2[:, (before + n) % 2]
                    eng.wait_ge(s2_turns, NP2 * u + before + n + 1)
                    for lo in range(q0, q1, CH):
                        hi = min(lo + CH, q1)
                        col = lo - q0
                        far_lo = max(lo, (J + FAR) * P)
                        has_far, has_mask = far_lo < hi, lo == J * P
                        mm = nc.tensor.matmul(slot[:, col:col + hi - lo], ks[s][0:ROWS + 2, J * P:(J + 1) * P],
                                              qs[s][0:ROWS + 2, lo:hi], start=True, stop=not (has_far or has_mask))
                        if has_far:
                            at = far_lo - (J + FAR) * P
                            for part in range(3):
                                mm = nc.tensor.matmul(slot[:, far_lo - q0:hi - q0], flip,
                                                      far[hs][:, part, at:at + hi - far_lo], start=False,
                                                      stop=part == 2 and not has_mask)
                        if has_mask:
                            mm = nc.tensor.matmul(slot[:, 0:P], idb, maskk, start=False, stop=True)
                    mm.then_inc(s2_ready, 1)

            def values(u, s, J):
                eng.wait_ge(s2_turns, NP2 * u + sum(PIECES[:J + 1]) + 2)
                for c in range(J // TPC, S // CH):
                    lo = max(J * P, c * CH)
                    mm = nc.tensor.matmul(o_ps[32 * c:32 * c + 32, lo - c * CH:CH], vst[s % 2][:, J, :],
                                          prob[:, J % 4, lo:(c + 1) * CH], start=J == 0, stop=J == TPC * c + TPC - 1)
                mm.then_inc(prob_turns, 1)

            def turn_max(v, uses):
                eng.wait_ge(negmax_ready, v + 1)
                eng.wait_ge(turn_free, uses)
                nc.tensor.transpose(turn[0:2 * TB, 0:P // 2].bitcast(BF16), negmax[:].rearrange("p a n -> p (a n)"),
                                    idb).then_inc(turn_ready, 1)

            eng.wait_ge(near_loaded[0], 16)
            for v in range(2):
                eng.wait_ge(stack_loaded[v], 144)
                for I in reversed(range(TB)):
                    maxima(v, v, 0, I)
            turn_max(0, 1)

            def stack_ready(i, k):
                eng.wait_ge(max_loaded[k], 32 * i + 32 + START)
                if k % 2 == 0:
                    eng.wait_ge(far_loaded[k // 2], 48 * i + 48)

            def units(i, last):
                for k in range(QUAD):
                    u = QUAD * i + k
                    k2 = (k + 2) % QUAD
                    hs2 = (k // 2 + 1) % 2
                    ahead = not (last and k >= 2)
                    if ahead:
                        again = 1 if k < 2 else 2
                        eng.wait_ge(stack_loaded[k2], 144 * (i + again))
                        if k % 2 == 0:
                            eng.wait_ge(near_loaded[hs2], 16 * (i + again))
                    k1 = (k + 1) % QUAD

                    def some_scores(which, final):
                        for J, n in which:
                            if J < TB:
                                scores(u, k, k // 2, J, n)
                            elif not final:
                                scores(u + 1, k1, k1 // 2, 0, n)

                    for j in range(TB):
                        I = TB - 1 - j
                        banks = range(GROUPS[I]) if ahead else ()
                        if j == TB - 2 and not (last and k == QUAD - 1):
                            stack_ready(i + (k + 1) // QUAD, k1)
                        first, second = score_steps(j)
                        if j < TB // 2:
                            maxima(u + 2, k2, hs2, I, banks[:1])
                        some_scores(first, last and k == QUAD - 1)
                        if j >= TB // 2:
                            maxima(u + 2, k2, hs2, I, banks[:1])
                        maxima(u + 2, k2, hs2, I, banks[1:2])
                        if j == 0:
                            eng.wait_ge(vst_ready, u + 1)
                            eng.wait_ge(oT_ready, u + START)
                        values(u, k, j)
                        maxima(u + 2, k2, hs2, I, banks[2:3])
                        some_scores(second, last and k == QUAD - 1)
                        maxima(u + 2, k2, hs2, I, banks[3:])
                        if j == 5 and not (last and k == 3):
                            turn_max(u + 1, 2 * u + 2)
                    eng.wait_ge(oT_ready, u + 1 + START)
                    eng.wait_ge(turn_free, 2 * u + (2 if last and k == 3 else 3))
                    for n in range(TPC):
                        mm = nc.tensor.transpose(turn[:, n * P:(n + 1) * P], oT[:, n * P:(n + 1) * P], ident)
                        if n == 0:
                            mm.then_inc(vst_turns, 1)
                    mm.then_inc(turn_ready, 1)

            stack_ready(0, 0)
            for n in range(2):
                scores(0, 0, 0, 0, n)
            with eng.Fori(0, NQ - 1) as i:
                units(i, False)
            units(NQ - 1, True)

        @block.scalar
        def _(eng):
            eng.sem_inc(oT_ready, START)
            eng.sem_inc(s2_turns, 2)

            def exponentials(u, J, n):
                if n < PIECES[J]:
                    q0, q1 = attention_pieces(J)[n]
                    if n == 0:
                        eng.wait_ge(prob_turns, TB * u + J + 1)
                    before = sum(PIECES[:J])
                    eng.wait_ge(s2_ready, NP2 * u + before + n + 1 + START)
                    nc.scalar.activation(prob[:, J % 4, q0:q1], s2[:, (before + n) % 2, 0:q1 - q0],
                                         ACT.Exp).then_inc(s2_turns, 1)

            def units(i, last):
                for k in range(QUAD):
                    u = QUAD * i + k
                    more = not (last and k == QUAD - 1)
                    for J in range(1, TB):
                        for n in range(2):
                            exponentials(u, J, n)
                    if more:
                        exponentials(u + 1, 0, 0)
                    eng.wait_ge(prob_turns, TB * (u + 1) + 4)
                    eng.wait_ge(turn_ready, 2 * u + 1)
                    nc.scalar.copy(oT[:], o_ps[:]).then_inc(oT_ready, 1)
                    if more:
                        exponentials(u + 1, 0, 1)

            for n in range(2):
                exponentials(0, 0, n)
            with eng.Fori(0, NQ - 1) as i:
                units(i, False)
            units(NQ - 1, True)

        @block.vector
        def _(eng):
            step = Steps(eng, dve_step)
            eng.sem_inc(s1_turns, 2)
            eng.sem_inc(turn_free, 1)
            step(nc.vector.memset(partmax[:], -3.0e38))
            eng.wait_ge(const_loaded, 16)
            nc.vector.tensor_copy(squares_b[:], squares[:]).then_inc(const_cast, 1)

            def maxima(v, I):
                before = sum(GROUPS[I + 1:])
                for g in range(GROUPS[I]):
                    eng.wait_ge(s1_ready, NG1 * v + before + g + 1)
                    width = min(CH, (I + 1) * P - g * CH)
                    nc.vector.tensor_reduce(partmax[:, I, g:g + 1], s1[:, (before + g) % 2, 0:width],
                                            AX, ALU.max).then_inc(s1_turns, 1)

            def negate(v):
                eng.wait_ge(s1_turns, NG1 * (v + 1) + 2)
                step(nc.vector.tensor_reduce(mx[:], partmax[:], AX, ALU.max))
                step(nc.vector.tensor_scalar(negmax[:, 0], mx[:], -1.0, None, ALU.mult))
                nc.vector.scalar_tensor_tensor(out=negmax[:, 1], in0=mx[:], scalar=-1.0, in1=negmax[:, 0],
                                               op0=ALU.mult, op1=ALU.subtract).then_inc(negmax_ready, 1)

            def turned_max(v, i, k, uses):
                eng.wait_ge(turn_ready, uses)
                if k < 2:
                    eng.wait_ge(max_loaded[(k + 2) % QUAD], 32 * i + START)
                else:
                    eng.wait_ge(max_loaded[(k + 2) % QUAD], 32 * i + 32 + START)
                nc.vector.tensor_copy(negmaxT[k % 2][:], turn[0:2 * TB, 0:P // 2].bitcast(BF16)).then_inc(negmaxT_ready, 1)
                eng.wait_ge(negmaxT_ready, v + 1)
                eng.sem_inc(turn_free, 1)

            def normalise(u, i, k, uses):
                eng.wait_ge(turn_ready, uses)
                view = turn[:].rearrange("p (n c d) -> p c n d", n=TPC, c=4)
                step(nc.vector.reciprocal(rsum[:], view[:, :, :, HD]))
                b = k % 2
                out = t.o_sb[:, b * TB:(b + 1) * TB, ds((2 * i + k // 2) * HD, HD)]
                step(nc.vector.tensor_tensor(out.rearrange("p (c n) d -> p c n d", c=4), view[:, :, :, 0:HD],
                                             rsum[:].unsqueeze(3).to_broadcast([P, 4, TPC, HD]), ALU.mult))
                eng.sem_inc(turn_free, 1)

            for I in reversed(range(TB)):
                maxima(0, I)
            negate(0)
            for I in reversed(range(TB)):
                maxima(1, I)
            turned_max(0, 0, 0, 1)
            negate(1)

            def units(i, last):
                for k in range(QUAD):
                    u = QUAD * i + k
                    ahead = not (last and k >= 2)
                    for j in range(TB):
                        if ahead:
                            maxima(u + 2, TB - 1 - j)
                        if j == 6 and not (last and k == 3):
                            turned_max(u + 1, i + (k + 1) // QUAD, (k + 1) % QUAD, 2 * u + 2)
                    normalise(u, i, k, 2 * u + (2 if last and k == 3 else 3))
                    if ahead:
                        negate(u + 2)

            with eng.Fori(0, NQ - 1) as i:
                step.enter(i, QUAD * 4)
                units(i, False)
                step.leave(NQ - 1)
            units(NQ - 1, True)


def place_folded(t):
    in_z, in_dt = Region(t.z_sb), Region(t.dt_sb)
    t.folded = [in_z(KT, D), in_z(KT, D), in_z(KT, D), in_z(2, KT, WF), in_z(2, KT, KR), in_z(KT, D),
                in_z(KT, NSP * NW), in_dt(2, KT, KR), in_dt(KT, D)]
    t.folded_from = [t.wq, t.wk, t.winv, t.vq, t.vk, t.wo, t.bffn, t.u, t.w_dt]


def phase_project(nc, t):
    with nc.cleanup_on_exit(), ExitStack() as ctx:
        sp = Space(nc, ctx, "prj")
        wp = sp.sb("wp", [P, KT, D])
        pb, gain, shift = sp.sb("pb", [P, D]), sp.sb("gain", [P, D]), sp.sb("shift", [P, D])
        ident = sp.sb("ident", [P, P])
        keep = sp.sb("keep", [P, NCH])
        eps = sp.sb("eps", [P, 1])
        ones = sp.sb("ones", [P, CH])
        o = sp.sb("o", [P, TPC, D])
        x = sp.sb("x", [P, TPC, D])
        xp = sp.sb("xp", [P, TPC, D])
        xl = sp.sb("xl", [P, TPC, D])
        oT = sp.sb("oT", [P, 2, KT, P])
        y = sp.sb("y", [P, TPC, D])
        x1 = sp.sb("x1", [P, TPC, D])
        stats = sp.sb("stats", [P, TPC, 6])
        mv = sp.sb("mv", [P, 2, TPC, 2])
        std = sp.sb("std", [P, 2, TPC])
        rstd = sp.sb("rstd", [P, 2, TPC])
        less = sp.sb("less", [P, TPC])
        xT = sp.sb("xT", [P, KT, CH])
        cum = sp.sb("cum", [P, KT, CH])
        carry = sp.sb("carry", [P, KT])
        oT_ps = sp.psum("oT_ps", [P, 2, CH])
        y_ps = sp.psum("y_ps", [P, TPC, CH])
        xT_ps = sp.psum("xT_ps", [P, KT, CH])

        const_loaded, pool_set = sp.sem("const_loaded"), sp.sem("pool_set")
        o_loaded, x_loaded = sp.sem("o_loaded"), sp.sem("x_loaded")
        o_used = sp.sem("o_used")
        biased = sp.sem("biased")
        oT_ps_ready, oT_ready = sp.sem("oT_ps_ready"), sp.sem("oT_ready")
        y_ready, y_used = sp.sem("y_ready"), sp.sem("y_used")
        xl_used = sp.sem("xl_used")
        var_ready, std_ready = sp.sem("var_ready"), sp.sem("std_ready")
        shift_ready = sp.sem("shift_ready")
        x1_ready, xT_ps_ready = sp.sem("x1_ready"), sp.sem("xT_ps_ready")
        xT_ready, cum_ready = sp.sem("xT_ready"), sp.sem("cum_ready")
        x1_stored, xT_stored, cum_stored = sp.sem("x1_stored"), sp.sem("xT_stored"), sp.sem("cum_stored")
        dve_step, folded_loaded = sp.sem("dve_step"), sp.sem("folded_loaded")
        block = ctx.enter_context(nc.Block())

        @block.sync
        def _(eng):
            eng.sem_inc(x1_stored, START)
            eng.sem_inc(xT_stored, START)
            eng.sem_inc(cum_stored, START)
            for dst, src in ((wp, t.wproj), (pb, t.bproj), (gain, t.ln_g), (shift, t.ln_b), (ident, t.ident), (keep, t.keep)):
                eng.dma_start(dst[:], src).then_inc(const_loaded, 16)

            def load(c):
                after(eng, o_used, c)
                eng.dma_start(o[:], t.o_sb[:, ds(c * TPC, TPC), :]).then_inc(o_loaded, 16)
                after(eng, biased, 2 * c)
                eng.dma_start(x[:], t.x.rearrange("(n p) d -> p n d", p=P)[:, ds(c * TPC, TPC), :]).then_inc(x_loaded, 16)

            def store(c):
                eng.wait_ge(x1_ready, c + 1)
                eng.dma_start(t.x1.rearrange("(n p) d -> p n d", p=P)[:, ds(c * TPC, TPC), :], x1[:]).then_inc(x1_stored, 16)
                eng.wait_ge(xT_ready, KT * (c + 1) + START)
                eng.dma_start(t.x1T[:, :, ds(c * CH, CH)], xT[:]).then_inc(xT_stored, 16)
                eng.wait_ge(cum_ready, c + 1 + START)
                eng.dma_start(t.cumT[:, :, ds(c * CH, CH)], cum[:]).then_inc(cum_stored, 16)

            load(0)
            load(1)
            for dst, src in zip(t.folded, t.folded_from):
                eng.dma_start(dst, src).then_inc(folded_loaded, 16)
            with eng.Fori(0, NCH - 2) as i:
                load(i + 2)
                store(i)
            store(NCH - 2)
            store(NCH - 1)
            after(eng, folded_loaded, 16 * len(t.folded))
            for sem in (x1_stored, xT_stored, cum_stored):
                eng.wait_ge(sem, 16 * NCH + START)

        @block.gpsimd
        def _(eng):
            step = Steps(eng, pool_set)
            step(nc.gpsimd.memset(eps[:], EPS))
            step(nc.gpsimd.memset(ones[:], 1.0))
            step(nc.gpsimd.memset(carry[:], 0.0))
            eng.wait_ge(const_loaded, 96)

            with eng.Fori(0, NCH) as c:
                eng.wait_ge(x_loaded, 16 * c + 16)
                eng.wait_ge(y_ready, TPC * c + START)
                nc.gpsimd.tensor_tensor(xp[:], x[:], pb[:].unsqueeze(1).to_broadcast([P, TPC, D]), ALU.add).then_inc(biased, 1)
                eng.wait_ge(biased, 2 * c + 1)
                eng.wait_ge(xl_used, c + START)
                nc.gpsimd.tensor_tensor(xl[:], x[:], shift[:].unsqueeze(1).to_broadcast([P, TPC, D]), ALU.add).then_inc(biased, 1)
                eng.wait_ge(biased, 2 * c + 2)

        @block.tensor
        def _(eng):
            eng.wait_ge(const_loaded, 96)

            def project(c):
                eng.wait_ge(o_loaded, 16 * c + 16)
                for j in range(TPC + 1):
                    if j < TPC:
                        after(eng, oT_ready, TPC * c + j - 1)
                        for k in range(KT):
                            mm = nc.tensor.transpose(oT_ps[:, j % 2, k * P:(k + 1) * P], o[:, j, k * P:(k + 1) * P], ident[:])
                        mm.then_inc(oT_ps_ready, 1)
                        if j == TPC - 1:
                            eng.wait_ge(oT_ps_ready, TPC * c + TPC)
                            eng.sem_inc(o_used, 1)
                    if j > 0:
                        eng.wait_ge(oT_ready, TPC * c + j)
                        after(eng, y_used, TPC * (c - 1) + j + START)
                        for k in range(KT):
                            nc.tensor.matmul(y_ps[:, j - 1, 0:D], oT[:, (j - 1) % 2, k], wp[:, k], start=k == 0, stop=False)
                        if j == 1:
                            eng.wait_ge(biased, 2 * c + 1)
                        mm = nc.tensor.matmul(y_ps[:, j - 1, 0:D], ident[:], xp[:, j - 1], start=False, stop=True)
                        mm.then_inc(y_ready, 1)

            def turn(c):
                eng.wait_ge(x1_ready, c + 1)
                for k in range(KT):
                    eng.wait_ge(xT_ready, KT * c + START)
                    for j in range(TPC):
                        mm = nc.tensor.transpose(xT_ps[:, k, j * P:(j + 1) * P], x1[:, j, k * P:(k + 1) * P], ident[:])
                    mm.then_inc(xT_ps_ready, 1)

            project(0)
            project(1)
            with eng.Fori(0, NCH - 2) as i:
                turn(i)
                project(i + 2)
            turn(NCH - 2)
            turn(NCH - 1)

        @block.scalar
        def _(eng):
            eng.sem_inc(xT_ready, START)
            eng.wait_ge(pool_set, 3)

            def copy_o(c):
                for j in range(TPC):
                    eng.wait_ge(oT_ps_ready, TPC * c + j + 1)
                    after(eng, y_ready, TPC * c + j - 1 + START)
                    nc.scalar.copy(oT[:, j % 2], oT_ps[:, j % 2, 0:D].rearrange("p (k q) -> p k q", k=KT)).then_inc(oT_ready, 1)

            def deviation(c, n):
                eng.wait_ge(var_ready, 2 * c + n + 1)
                nc.scalar.activation(std[:, n], mv[:, n, :, 1], ACT.Sqrt, bias=eps[:]).then_inc(std_ready, 1)

            def back(c):
                for k in range(KT):
                    eng.wait_ge(xT_ps_ready, KT * c + k + 1)
                    if k == 0:
                        eng.wait_ge(xT_stored, 16 * c + START)
                        eng.wait_ge(cum_ready, c + START)
                    nc.scalar.copy(xT[:, k], xT_ps[:, k]).then_inc(xT_ready, 1)

            def write_x1(c):
                eng.wait_ge(shift_ready, c + 1)
                eng.wait_ge(x1_stored, 16 * c + START)
                after(eng, xT_ps_ready, KT * c)
                for j in range(TPC):
                    ins = nc.scalar.activation(x1[:, j], y[:, j], ACT.Identity, bias=less[:, j:j + 1], scale=rstd[:, 1, j:j + 1])
                ins.then_inc(x1_ready, 1)

            copy_o(0)
            deviation(0, 0)
            copy_o(1)
            deviation(0, 1)
            write_x1(0)
            with eng.Fori(0, NCH - 2) as i:
                deviation(i + 1, 0)
                back(i)
                copy_o(i + 2)
                deviation(i + 1, 1)
                write_x1(i + 1)
            back(NCH - 2)
            for n in range(2):
                deviation(NCH - 1, n)
            write_x1(NCH - 1)
            back(NCH - 1)

        @block.vector
        def _(eng):
            eng.sem_inc(y_used, START)
            eng.sem_inc(y_ready, START)
            eng.sem_inc(xl_used, START)
            eng.sem_inc(cum_ready, START)
            step = Steps(eng, dve_step)
            eng.wait_ge(const_loaded, 96)
            eng.wait_ge(pool_set, 3)

            def moments(n, of):
                for j in range(TPC):
                    of(j)
                eng.drain()
                for j in range(TPC):
                    ins = nc.vector.bn_aggr(mv[:, n, j], stats[:, j])
                ins.then_inc(var_ready, 1)

            def residual(c):
                def of(j):
                    eng.wait_ge(y_ready, TPC * c + j + 1 + START)
                    nc.vector.bn_stats(stats[:, j], y_ps[:, j, 0:D])
                moments(0, of)

            def inner_norm(c):
                eng.wait_ge(std_ready, 2 * c + 1)
                step(nc.vector.reciprocal(rstd[:, 0], std[:, 0]))
                after(eng, x1_ready, c)
                for j in range(TPC):
                    nc.vector.scalar_tensor_tensor(out=y[:, j], in0=y_ps[:, j, 0:D], scalar=mv[:, 0, j, 0:1], in1=gain[:],
                                                   op0=ALU.subtract, op1=ALU.mult).then_inc(y_used, 1)
                eng.wait_ge(y_used, TPC * c + TPC + START)
                eng.wait_ge(biased, 2 * c + 2)
                for j in range(TPC):
                    step.go(nc.vector.scalar_tensor_tensor(out=y[:, j], in0=y[:, j], scalar=rstd[:, 0, j:j + 1], in1=xl[:, j],
                                                           op0=ALU.mult, op1=ALU.add))
                step.wait()
                eng.sem_inc(xl_used, 1)
                moments(1, lambda j: nc.vector.bn_stats(stats[:, j], y[:, j]))

            def outer_norm(c):
                eng.wait_ge(std_ready, 2 * c + 2)
                step(nc.vector.reciprocal(rstd[:, 1], std[:, 1]))
                nc.vector.scalar_tensor_tensor(out=less[:], in0=mv[:, 1, :, 0], scalar=-1.0, in1=rstd[:, 1],
                                               op0=ALU.mult, op1=ALU.mult).then_inc(shift_ready, 1)

            def running_sum(c):
                eng.wait_ge(xT_ready, KT * c + KT + START)
                eng.wait_ge(cum_stored, 16 * c + START)
                for k in range(KT):
                    step.go(nc.vector.tensor_tensor_scan(cum[:, k], ones[:], xT[:, k], carry[:, k:k + 1], ALU.mult, ALU.add))
                step.wait()
                nc.vector.tensor_scalar(carry[:].unsqueeze(2), cum[:, :, CH - 1:CH], keep[:, ds(c, 1)], None,
                                        ALU.mult).then_inc(cum_ready, 1)
                eng.wait_ge(cum_ready, c + 1 + START)

            residual(0)
            inner_norm(0)
            outer_norm(0)
            with eng.Fori(0, NCH - 1) as i:
                step.enter(i, 2 + 1 + TPC + 1)
                residual(i + 1)
                inner_norm(i + 1)
                running_sum(i)
                outer_norm(i + 1)
                step.leave(NCH - 1)
            running_sum(NCH - 1)


KE, R = 8, 64
KR = KE * R
GB = KR // P
NG = 2 * GB
RH = 256
WF = KR + RH
NW = 2 * KE
NSP = 6


def phase_combine(nc, t):
    with nc.cleanup_on_exit(), ExitStack() as ctx:
        sp = Space(nc, ctx, "cmb")
        wq, wk, wi, vq, vk, wo, bias, u, wdt = t.folded
        place = Region(t.u_sb)
        iq = place(KT, WF)
        ik = place(KT, KR)
        small = sp.sb("small", [P, 2, KT])
        alpha = sp.sb("alpha", [P, 1])
        b2, be = sp.sb("b2", [P, KE]), sp.sb("be", [P, KE])
        alphas = sp.sb("alphas", [NSP * NW, 1])
        pick = sp.sb("pick", [NSP * NW, 3])
        sel = sp.sb("sel", [NSP * NW, NG, P])
        bo = sp.sb("bo", [NSP * NW, D])
        bopart = sp.sb("bopart", [NSP * NW, 3, D], BF16)
        borest = sp.sb("borest", [NSP * NW, D])
        bosum = sp.sb("bosum", [NSP * NW, D])
        whole = sp.sb("whole", [P, 2, CH])
        ps = sp.psum("ps", [P, 4, CH])
        loaded = sp.sem("loaded")
        ready = sp.sem("ready")
        evac = sp.sem("evac")
        split = sp.sem("split")
        dve_step = sp.sem("dve_step")
        block = ctx.enter_context(nc.Block())

        jobs = []
        for m in range(KT):
            col = slice(m * P, (m + 1) * P)
            for c0, c1 in ((0, CH), (CH, WF)):
                jobs.append((iq[:, m, c0:c1], P, [wi[:, k, col] for k in range(KT)], [vq[:, 1, k, c0:c1] for k in range(KT)], 1.0, None))
            jobs.append((ik[:, m, :], P, [wi[:, k, col] for k in range(KT)], [vk[:, 1, k, :] for k in range(KT)], 1.0, None))
        n_inner = len(jobs)
        for br in range(2):
            for m in range(KT):
                col = slice(m * P, (m + 1) * P)
                right = (lambda k: vq[:, 0, k]) if br == 0 else (lambda k: iq[:, k])
                for c0, c1 in ((0, CH), (CH, WF)):
                    jobs.append((None, P, [wq[:, k, col] for k in range(KT)], [right(k)[:, c0:c1] for k in range(KT)], 1.0,
                                 (t.aq_hi[:, br, m, c0:c1], t.aq_lo[:, br, m, c0:c1])))
                right = (lambda k: vk[:, 0, k]) if br == 0 else (lambda k: ik[:, k])
                jobs.append((None, P, [wk[:, k, col] for k in range(KT)], [right(k) for k in range(KT)], 1.0,
                             (t.ak_hi[:, br, m], t.ak_lo[:, br, m])))
            for g in range(GB):
                jobs.append((t.uo[:, br * GB + g], P, [u[:, br, k, g * P:(g + 1) * P] for k in range(KT)],
                             [wo[:, k] for k in range(KT)], alpha[:, 0:1] if br else 1.0, None))
        jobs.append((bo[:], NSP * NW, [bias[:, k] for k in range(KT)], [wo[:, k] for k in range(KT)], alphas[:, 0:1], None))
        splits = [n for n, j in enumerate(jobs) if j[5]]
        LOADS = 11

        @block.sync
        def _(eng):
            loads = ((alpha, t.alpha), (alphas, t.alphas), (pick, t.pick), (t.router2, t.w2), (t.routerb, t.b1), (b2, t.b2),
                     (be, t.be), (sel, t.sel), (t.count_sb, t.count), (small[:, 0], t.b_dt), (small[:, 1], t.dt_bias))
            for dst, src in loads:
                eng.dma_start(dst[:], src).then_inc(loaded, 16)
            eng.wait_ge(loaded, 16 * LOADS)

        @block.tensor
        def _(eng):
            for n, (_, rows, left, right, _, _) in enumerate(jobs):
                if n >= 4:
                    eng.wait_ge(evac, n - 3)
                if n == n_inner:
                    eng.wait_ge(evac, n)
                width = right[0].shape[-1]
                for k in range(KT):
                    mm = nc.tensor.matmul(ps[0:rows, n % 4, 0:width], left[k], right[k], start=k == 0, stop=k == KT - 1)
                mm.then_inc(ready, 1)

        @block.scalar
        def _(eng):
            eng.wait_ge(loaded, 16 * LOADS)
            for n, (dst, rows, _, right, scale, parts) in enumerate(jobs):
                width = right[0].shape[-1]
                eng.wait_ge(ready, n + 1)
                if parts:
                    s = splits.index(n)
                    if s >= 2:
                        eng.wait_ge(split, s - 1)
                    dst = whole[:, s % 2, 0:width]
                nc.scalar.activation(dst, ps[0:rows, n % 4, 0:width], ACT.Identity, scale=scale).then_inc(evac, 1)

        @block.vector
        def _(eng):
            step = Steps(eng, dve_step)
            eng.wait_ge(loaded, 16 * LOADS)
            step(nc.vector.tensor_tensor(t.logitb[:], b2[:], be[:], ALU.add))
            step(nc.vector.tensor_copy(t.sel_sb[:], sel[:]))
            step(nc.vector.tensor_tensor(t.dt_bias_sb[:], small[:, 0], small[:, 1], ALU.add))
            step(nc.vector.tensor_copy(t.wdt_hi[:], wdt[:]))
            step(nc.vector.tensor_tensor(t.wdt_lo[:], wdt[:], t.wdt_hi[:].bitcast(F32), ALU.subtract))
            for s, n in enumerate(splits):
                hi, lo = jobs[n][5]
                src = whole[:, s % 2, 0:hi.shape[-1]]
                eng.wait_ge(evac, n + 1)
                step(nc.vector.tensor_copy(hi, src))
                nc.vector.tensor_tensor(lo, src, hi.bitcast(F32), ALU.subtract).then_inc(split, 1)
            eng.wait_ge(evac, len(jobs))
            step(nc.vector.tensor_copy(bopart[:, 0], bo[:]))
            step(nc.vector.tensor_tensor(borest[:], bo[:], bopart[:, 0], ALU.subtract))
            step(nc.vector.tensor_copy(bopart[:, 1], borest[:]))
            step(nc.vector.tensor_tensor(bopart[:, 2], borest[:], bopart[:, 1], ALU.subtract))
            step(nc.vector.tensor_scalar(bosum[:], bopart[:, 0], pick[:, 0:1], None, ALU.mult))
            step(nc.vector.scalar_tensor_tensor(out=bosum[:], in0=bopart[:, 1], scalar=pick[:, 1:2], in1=bosum[:],
                                                op0=ALU.mult, op1=ALU.add))
            step(nc.vector.scalar_tensor_tensor(out=t.bo_stack[:], in0=bopart[:, 2], scalar=pick[:, 2:3], in1=bosum[:],
                                                op0=ALU.mult, op1=ALU.add))


def phase_fused(nc, t):
    with nc.cleanup_on_exit(), ExitStack() as ctx:
        sp = Space(nc, ctx, "ffn")
        ident, idb = sp.sb("ident", [P, P]), sp.sb("idb", [P, P], BF16)
        eps, one = sp.sb("eps", [P, 1]), sp.sb("one", [P, 1])
        place = Region(t.z_sb)
        raw = place(2, KT, CH)
        hT = place(2, KT, CH)
        prod = place(NG, CH)
        hi = sp.sb("hi", [P, 2, KT, CH], F32R)
        lo = sp.sb("lo", [P, 2, KT, CH], F32R)
        res = sp.sb("res", [P, TPC, D])
        ky = sp.sb("ky", [P, 2, CH])
        lg = sp.sb("lg", [P, TPC * 2, KE])
        red = sp.sb("red", [P, TPC * 2])
        den = sp.sb("den", [P, TPC, 2])
        inv = sp.sb("inv", [P, TPC * 2])
        wts = sp.sb("wts", [P, TPC, NW])
        wrest = sp.sb("wrest", [P, TPC, NW])
        wst = sp.sb("wst", [P, TPC, NSP, NW], BF16)
        wT = sp.sb("wT", [NSP * NW, CH], BF16)
        y = sp.sb("y", [P, TPC, D])
        stats = sp.sb("stats", [P, TPC, 6])
        mv = sp.sb("mv", [P, TPC, 2])
        std = sp.sb("std", [P, TPC])
        rstd = sp.sb("rstd", [P, TPC])
        xT = sp.sb("xT", [P, KT, CH])
        x_hi, x_lo = sp.sb("x_hi", [P, KT, CH], F32R), sp.sb("x_lo", [P, KT, CH], F32R)
        pre = sp.sb("pre", [P, KT, CH])
        expn = sp.sb("expn", [P, KT, CH])
        corr = sp.sb("corr", [P, KT, CH])
        work = sp.psum("work", [P, 4, CH])
        o_ps = sp.psum("o_ps", [P, 2, CH])
        lg_ps = sp.psum("lg_ps", [P, CH])
        xT_ps = sp.psum("xT_ps", [P, CH])

        const_loaded, pool_set = sp.sem("const_loaded"), sp.sem("pool_set")
        raw_loaded, res_loaded = sp.sem("raw_loaded"), sp.sem("res_loaded")
        hi_ready, lo_ready = sp.sem("hi_ready"), sp.sem("lo_ready")
        work_ready = sp.sem("work_ready")
        act_read, dve_read = sp.sem("act_read"), sp.sem("dve_read")
        lg_ready, exp_ready = sp.sem("lg_ready"), sp.sem("exp_ready")
        shifted = sp.sem("shifted")
        wst_ready, wT_ps_ready, wT_ready = sp.sem("wst_ready"), sp.sem("wT_ps_ready"), sp.sem("wT_ready")
        ky_used = sp.sem("ky_used")
        o_ready, o_read = sp.sem("o_ready"), sp.sem("o_read")
        var_ready, std_ready = sp.sem("var_ready"), sp.sem("std_ready")
        x2_ready, xT_ps_ready = sp.sem("x2_ready"), sp.sem("xT_ps_ready")
        xT_ready, xT_stored = sp.sem("xT_ready"), sp.sem("xT_stored")
        x_lo_ready = sp.sem("x_lo_ready")
        abs_ready, expn_ready, corr_ready, log_ready = (sp.sem("abs_ready"), sp.sem("expn_ready"), sp.sem("corr_ready"),
                                                        sp.sem("log_ready"))
        idb_ready, dve_step = sp.sem("idb_ready"), sp.sem("dve_step")
        block = ctx.enter_context(nc.Block())

        WEIGHED = {5: (0,), 6: (1, 2, 3), 7: (4, 5, 6, 7)}
        ORDER = [("hidden", n) for n in range(4)]
        for g in range(NG):
            ORDER += [("v", g), ("w", g)]
            if g == 4:
                ORDER += [("dt", m) for m in range(KT)]
            ORDER += [("weight", n) for n in WEIGHED.get(g, ())]
        AT = {use: n for n, use in enumerate(ORDER)}
        USES = len(ORDER)
        READER = {"hidden": "act", "v": "dve", "w": "act", "dt": "act", "weight": "dve"}

        def count(c, use, who=None):
            mine = lambda u: who is None or READER[u[0]] == who
            upto = [u for u in ORDER[:AT[use] + 1] if mine(u)]
            if isinstance(c, int) and c == 0:
                return sum(u[0] != "dt" for u in upto)
            skipped = 0 if who == "dve" else KT
            return sum(mine(u) for u in ORDER) * c + len(upto) - skipped

        def filled(eng, c, use):
            eng.wait_ge(work_ready, count(c, use))

        def emptied(eng, c, use):
            if READER[use[0]] == "act":
                eng.wait_ge(act_read, count(c, use, "act"))
            else:
                eng.wait_ge(dve_read, count(c, use, "dve"))

        def bank_free(eng, c, use):
            first = isinstance(c, int) and c == 0
            m = AT[use] - 4
            if first and m >= 0 and ORDER[m][0] == "dt":
                m -= 4
            if m >= 0:
                emptied(eng, c, ORDER[m])
            elif not first:
                emptied(eng, c - 1, ORDER[m])

        @block.sync
        def _(eng):
            eng.sem_inc(xT_stored, START)
            eng.dma_start(ident[:], t.ident).then_inc(const_loaded, 16)

            def load(c):
                after(eng, lo_ready, 2 * c)
                eng.dma_start(raw[:, 0], t.x1T[:, :, ds(c * CH, CH)]).then_inc(raw_loaded, 16)
                eng.dma_start(raw[:, 1], t.cumT[:, :, ds(c * CH, CH)]).then_inc(raw_loaded, 16)

            def load_res(c):
                after(eng, o_read, TPC * c)
                eng.dma_start(res[:], t.x1.rearrange("(n p) d -> p n d", p=P)[:, ds(c * TPC, TPC), :]).then_inc(res_loaded, 16)

            def store(c):
                eng.wait_ge(xT_ready, KT * (c + 1) + START)
                eng.dma_start(t.u_sb[:, :, ds(c * CH, CH)], xT[:]).then_inc(xT_stored, 16)

            load(0)
            load_res(0)
            load(1)
            load_res(1)
            with eng.Fori(0, NCH - 2) as i:
                store(i)
                load(i + 2)
                load_res(i + 2)
            store(NCH - 2)
            store(NCH - 1)
            eng.wait_ge(xT_stored, 16 * NCH + START)

        @block.gpsimd
        def _(eng):
            nc.gpsimd.memset(eps[:], EPS).then_inc(pool_set, 1)
            nc.gpsimd.memset(one[:], 1.0).then_inc(pool_set, 1)

        @block.tensor
        def _(eng):
            eng.sem_inc(xT_ps_ready, START)
            eng.wait_ge(const_loaded, 16)
            eng.wait_ge(idb_ready, 1)

            def exact(out, w_hi, w_lo, x_hi, x_lo, first, last):
                nc.tensor.matmul(out, w_hi, x_hi, start=first, stop=False)
                nc.tensor.matmul(out, w_hi, x_lo, start=False, stop=False)
                return nc.tensor.matmul(out, w_lo, x_hi, start=False, stop=last)

            def product(c, use, a_hi, a_lo, br, src, col):
                bank_free(eng, c, use)
                for k in range(KT):
                    mm = exact(work[:, AT[use] % 4], a_hi[:, br, k, col], a_lo[:, br, k, col], hi[:, src, k], lo[:, src, k],
                               k == 0, k == KT - 1)
                mm.then_inc(work_ready, 1)

            def logits(c):
                emptied(eng, c, ("hidden", 3))
                after(eng, wT_ready, c)
                for j in range(TPC):
                    for br in range(2):
                        at = (j * 2 + br) * KE
                        for k in range(KT):
                            mm = nc.tensor.matmul(lg_ps[:, at:at + KE], hT[:, br, k, j * P:(j + 1) * P], t.router2[:, k],
                                                  start=k == 0, stop=k == KT - 1)
                mm.then_inc(lg_ready, 1)

            def turn_x2(c, k):
                if k == 0:
                    eng.wait_ge(x2_ready, c + 1)
                eng.wait_ge(xT_ready, KT * c + k + START)
                for j in range(TPC):
                    mm = nc.tensor.transpose(xT_ps[:, j * P:(j + 1) * P], y[:, j, k * P:(k + 1) * P], ident[:])
                mm.then_inc(xT_ps_ready, 1)

            def step_size(c, m, bank):
                eng.wait_ge(x_lo_ready, KT * (c + 1))
                col = slice(m * P, (m + 1) * P)
                for k in range(KT):
                    mm = exact(work[:, bank], t.wdt_hi[:, k, col], t.wdt_lo[:, k, col], x_hi[:, k], x_lo[:, k], k == 0, k == KT - 1)
                mm.then_inc(work_ready, 1)

            def turn_weights(c):
                eng.wait_ge(wst_ready, c + 1)
                for j in range(TPC):
                    mm = nc.tensor.transpose(lg_ps[0:NSP * NW, j * P // 2:(j + 1) * P // 2].bitcast(BF16),
                                             wst[:, j].rearrange("p a w -> p (a w)"), idb[:])
                mm.then_inc(wT_ps_ready, 1)

            def outputs(c):
                for j in range(TPC):
                    after(eng, o_read, TPC * c + j - 1)
                    tok = slice(j * P, (j + 1) * P)
                    nc.tensor.matmul(o_ps[:, j % 2, 0:D], wT[:, tok], t.bo_stack[:], start=True, stop=False)
                    for g in range(NG):
                        if j == 0:
                            emptied(eng, c, ("weight", g))
                        mm = nc.tensor.matmul(o_ps[:, j % 2, 0:D], prod[:, g, tok], t.uo[:, g], start=False, stop=g == NG - 1)
                    mm.then_inc(o_ready, 1)

            def chunk(c, first):
                eng.wait_ge(lo_ready, 2 * c + 2)
                eng.wait_ge(hi_ready, 2 * c + 2)
                for use in ORDER:
                    kind, g = use
                    if kind == "hidden":
                        product(c, use, t.aq_hi, t.aq_lo, g // 2, 0, slice(KR + g % 2 * P, KR + (g % 2 + 1) * P))
                    elif kind == "dt":
                        if not first:
                            bank_free(eng, c, use)
                            step_size(c - 1, g, AT[use] % 4)
                    elif kind == "weight":
                        bank_free(eng, c, use)
                        if g == 0:
                            eng.wait_ge(wT_ready, c + 1)
                        nc.tensor.matmul(work[:, AT[use] % 4], t.sel_sb[:, g], wT[:], start=True, stop=True).then_inc(work_ready, 1)
                    else:
                        br, col = g // GB, slice(g % GB * P, (g % GB + 1) * P)
                        if kind == "v":
                            if g == 5:
                                turn_weights(c)
                            product(c, use, t.aq_hi, t.aq_lo, br, 0, col)
                        else:
                            product(c, use, t.ak_hi, t.ak_lo, br, 1, col)
                            if g == 0:
                                logits(c)
                            if not first and g in (1, 2):
                                turn_x2(c - 1, g - 1)
                outputs(c)

            chunk(0, True)
            with eng.Fori(0, NCH - 1) as i:
                chunk(i + 1, False)
            for k in range(KT):
                turn_x2(NCH - 1, k)
            for m in range(KT):
                step_size(NCH - 1, m, m)

        @block.scalar
        def _(eng):
            eng.sem_inc(xT_ready, START)
            eng.wait_ge(pool_set, 2)

            def round_hi(c):
                for a in range(2):
                    eng.wait_ge(raw_loaded, 32 * c + 32)
                    if a == 0 and not (isinstance(c, int) and c == 0):
                        filled(eng, c - 1, ("w", NG - 1))
                    nc.scalar.copy(hi[:, a], raw[:, a]).then_inc(hi_ready, 1)

            def hidden(c):
                for n in range(4):
                    br, m = n // 2, n % 2
                    filled(eng, c, ("hidden", n))
                    if n == 0:
                        after(eng, lg_ready, c)
                    nc.scalar.activation(hT[:, br, m], work[:, n % 4], ACT.Gelu, bias=t.routerb[:, m:m + 1]).then_inc(act_read, 1)

            def sums(c, g):
                filled(eng, c, ("w", g))
                after(eng, ky_used, NG * c + g - 1)
                nc.scalar.copy(ky[:, g % 2], work[:, AT[("w", g)] % 4]).then_inc(act_read, 1)

            def turned(c):
                eng.wait_ge(wT_ps_ready, c + 1)
                after(eng, o_ready, TPC * c)
                nc.scalar.copy(wT[:], lg_ps[0:NSP * NW, 0:CH // 2].bitcast(BF16)).then_inc(wT_ready, 1)

            def deviation(c):
                eng.wait_ge(var_ready, c + 1)
                nc.scalar.activation(std[:], mv[:, :, 1], ACT.Sqrt, bias=eps[:]).then_inc(std_ready, 1)

            def copy_x2(c, k):
                eng.wait_ge(xT_ps_ready, KT * c + k + 1 + START)
                if k == 0:
                    eng.wait_ge(xT_stored, 16 * c + START)
                nc.scalar.copy(x_hi[:, k], xT_ps[:])
                nc.scalar.copy(xT[:, k], xT_ps[:]).then_inc(xT_ready, 1)

            def add_bias(c, m, bank):
                nc.scalar.activation(pre[:, m], work[:, bank], ACT.Identity, bias=t.dt_bias_sb[:, m:m + 1]).then_inc(act_read, 1)

            def expn_of(c):
                eng.wait_ge(abs_ready, c + 1)
                nc.scalar.activation(expn[:], expn[:], ACT.Exp).then_inc(expn_ready, 1)

            def log_of(c):
                eng.wait_ge(corr_ready, c + 1)
                nc.scalar.activation(expn[:], expn[:], ACT.Ln, bias=one[:]).then_inc(log_ready, 1)

            def chunk(c, first, last):
                hidden(c)
                if not first:
                    deviation(c - 1)
                for g in range(NG):
                    sums(c, g)
                    if not first and g in (1, 2):
                        copy_x2(c - 1, g - 1)
                    if g == 2:
                        eng.wait_ge(shifted, c + 1)
                        nc.scalar.activation(lg[:], lg[:], ACT.Exp).then_inc(exp_ready, 1)
                    if not first and g == 4:
                        for m in range(KT):
                            filled(eng, c, ("dt", m))
                            add_bias(c - 1, m, AT[("dt", m)] % 4)
                    if g == 4:
                        turned(c)
                    if not first and g == 6:
                        expn_of(c - 1)
                if not last:
                    round_hi(c + 1)
                if not first:
                    log_of(c - 1)

            round_hi(0)
            chunk(0, True, False)
            with eng.Fori(0, NCH - 2) as i:
                chunk(i + 1, False, False)
            chunk(NCH - 1, False, True)
            deviation(NCH - 1)
            for k in range(KT):
                copy_x2(NCH - 1, k)
            for m in range(KT):
                eng.wait_ge(work_ready, count(NCH - 1, ORDER[-1]) + m + 1)
                add_bias(NCH - 1, m, m)
            expn_of(NCH - 1)
            log_of(NCH - 1)

        @block.vector
        def _(eng):
            step = Steps(eng, dve_step)
            eng.wait_ge(pool_set, 2)
            eng.wait_ge(const_loaded, 16)
            nc.vector.tensor_copy(idb[:], ident[:]).then_inc(idb_ready, 1)

            def round_lo(c):
                for a in range(2):
                    eng.wait_ge(hi_ready, 2 * c + a + 1)
                    nc.vector.tensor_tensor(lo[:, a], raw[:, a], hi[:, a].bitcast(F32), ALU.subtract).then_inc(lo_ready, 1)

            def multiply(c, g):
                emptied(eng, c, ("w", g))
                if g == 0:
                    after(eng, o_ready, TPC * c)
                nc.vector.tensor_tensor(prod[:, g], work[:, AT[("v", g)] % 4], ky[:, g % 2], ALU.mult).then_inc(dve_read, 1)
                emptied(eng, c, ("v", g))
                eng.sem_inc(ky_used, 1)

            flat = lambda x: x.unsqueeze(2).to_broadcast([P, TPC * 2, KE])
            several = lambda x, n: x.unsqueeze(2).to_broadcast([P, TPC, n, NW])

            def shift(c):
                eng.wait_ge(lg_ready, c + 1)
                step(nc.vector.tensor_tensor(lg[:], lg_ps[:, 0:TPC * NW].rearrange("p (a k) -> p a k", k=KE),
                                             t.logitb[:].unsqueeze(1).to_broadcast([P, TPC * 2, KE]), ALU.add))
                step(nc.vector.tensor_reduce(red[:], lg[:], AX, ALU.max))
                nc.vector.tensor_tensor(lg[:], lg[:], flat(red[:]), ALU.subtract).then_inc(shifted, 1)

            def weights(c):
                eng.wait_ge(exp_ready, c + 1)
                step(nc.vector.tensor_reduce(red[:], lg[:], AX, ALU.add))
                step(nc.vector.tensor_tensor(den[:], red[:].rearrange("p (n b) -> p n b", b=2),
                                             t.count_sb[:, ds(c * TPC, TPC)].unsqueeze(2).to_broadcast([P, TPC, 2]), ALU.mult))
                step(nc.vector.reciprocal(inv[:], den[:].rearrange("p n b -> p (n b)")))
                step(nc.vector.tensor_tensor(wts[:].rearrange("p n (b k) -> p (n b) k", b=2), lg[:], flat(inv[:]), ALU.mult))
                after(eng, wT_ps_ready, c)
                step(nc.vector.tensor_copy(wst[:, :, 0:3], several(wts[:], 3)))
                step(nc.vector.tensor_tensor(wrest[:], wts[:], wst[:, :, 0], ALU.subtract))
                step(nc.vector.tensor_copy(wst[:, :, 3:5], several(wrest[:], 2)))
                nc.vector.tensor_tensor(wst[:, :, 5], wrest[:], wst[:, :, 3], ALU.subtract).then_inc(wst_ready, 1)

            def weigh(c, g):
                filled(eng, c, ("weight", g))
                nc.vector.tensor_tensor(prod[:, g], work[:, AT[("weight", g)] % 4], prod[:, g], ALU.mult).then_inc(dve_read, 1)

            def norm(c):
                eng.wait_ge(res_loaded, 16 * c + 16)
                eng.wait_ge(xT_ps_ready, KT * c + START)
                for j in range(TPC):
                    eng.wait_ge(o_ready, TPC * c + j + 1)
                    nc.vector.tensor_tensor(y[:, j], o_ps[:, j % 2, 0:D], res[:, j], ALU.add).then_inc(o_read, 1)
                eng.wait_ge(o_read, TPC * c + TPC)
                for j in range(TPC):
                    nc.vector.bn_stats(stats[:, j], y[:, j])
                eng.drain()
                for j in range(TPC):
                    ins = nc.vector.bn_aggr(mv[:, j], stats[:, j])
                ins.then_inc(var_ready, 1)
                eng.wait_ge(std_ready, c + 1)
                step(nc.vector.reciprocal(rstd[:], std[:]))
                for j in range(TPC):
                    ins = nc.vector.tensor_scalar(y[:, j], y[:, j], mv[:, j, 0:1], rstd[:, j:j + 1], ALU.subtract, ALU.mult)
                ins.then_inc(x2_ready, 1)
                eng.wait_ge(x2_ready, c + 1)

            def round_x2(c, k):
                eng.wait_ge(xT_ready, KT * c + k + 1 + START)
                nc.vector.tensor_tensor(x_lo[:, k], xT[:, k], x_hi[:, k].bitcast(F32), ALU.subtract).then_inc(x_lo_ready, 1)

            def minus_abs(c):
                nc.vector.scalar_tensor_tensor(out=expn[:], in0=pre[:], scalar=-1.0, in1=pre[:],
                                               op0=ALU.mult, op1=ALU.min).then_inc(abs_ready, 1)

            def correction(c):
                eng.wait_ge(expn_ready, c + 1)
                step(nc.vector.tensor_scalar(corr[:], expn[:], 1.0, 1.0, ALU.add, ALU.subtract))
                nc.vector.tensor_tensor(corr[:], expn[:], corr[:], ALU.subtract).then_inc(corr_ready, 1)
                eng.wait_ge(corr_ready, c + 1)
                step(nc.vector.scalar_tensor_tensor(out=corr[:], in0=pre[:], scalar=0.0, in1=corr[:], op0=ALU.max, op1=ALU.add))

            def softplus(c):
                eng.wait_ge(log_ready, c + 1)
                step(nc.vector.tensor_tensor(t.dt_sb[:, :, ds(c * CH, CH)], corr[:], expn[:], ALU.add))

            def chunk(c, first, last):
                if not first:
                    norm(c - 1)
                for g in range(NG):
                    multiply(c, g)
                    if g == 1:
                        shift(c)
                    if not first and g in (2, 3):
                        round_x2(c - 1, g - 2)
                    if g == 3:
                        weights(c)
                    if g == 5:
                        for n in WEIGHED[g]:
                            weigh(c, n)
                        if not first:
                            emptied(eng, c, ("dt", KT - 1))
                            minus_abs(c - 1)
                    if g > 5:
                        for n in WEIGHED[g]:
                            weigh(c, n)
                if not last:
                    round_lo(c + 1)
                if not first:
                    correction(c - 1)
                    softplus(c - 1)

            round_lo(0)
            chunk(0, True, False)
            with eng.Fori(0, NCH - 2) as i:
                step.enter(i, 1 + 9 + 3)
                chunk(i + 1, False, False)
                step.leave(NCH - 2)
            chunk(NCH - 1, False, True)
            norm(NCH - 1)
            for k in range(KT):
                round_x2(NCH - 1, k)
            eng.wait_ge(act_read, count(NCH - 1, ("w", NG - 1), "act") + KT)
            minus_abs(NCH - 1)
            correction(NCH - 1)
            softplus(NCH - 1)


N = 16


def phase_scan(nc, t):
    with nc.cleanup_on_exit(), ExitStack() as ctx:
        sp = Space(nc, ctx, "ssm")
        hi, lo = sp.sb("hi", [P, KT, NTOK], F32R), sp.sb("lo", [P, KT, NTOK], F32R)
        u, dt, y = t.u_sb, t.dt_sb, t.z_sb
        skip = sp.sb("skip", [P, KT])
        par = sp.sb("par", [P, 5, KT, N])
        cur = sp.sb("cur", [P, KT, 5])
        raw = sp.sb("raw", [P, 2, KT, 2 * P])
        w_hi = [sp.sb(f"w_hi{m}", [P, KT, 2 * P], F32R) for m in range(KT)]
        w_lo = [sp.sb(f"w_lo{m}", [P, KT, 2 * P], F32R) for m in range(KT)]
        RING = 4
        a = sp.sb("a", [P, RING, CH])
        inp = sp.sb("inp", [P, 2, CH])
        h = sp.sb("h", [P, RING, CH])
        cc = sp.sb("cc", [P, RING, CH])
        b_ps, c_ps = sp.psum("b_ps", [P, RING, CH]), sp.psum("c_ps", [P, RING, CH])

        small_loaded = sp.sem("small_loaded")
        raw_loaded = [sp.sem(f"raw_loaded{m}") for m in range(KT)]
        hi_ready, lo_ready = sp.sem("hi_ready"), sp.sem("lo_ready")
        par_ready, skip_ready = sp.sem("par_ready"), sp.sem("skip_ready")
        y_ready = sp.sem("y_ready")
        w_ready = sp.sem("w_ready")
        b_ready, c_ready = sp.sem("b_ready"), sp.sem("c_ready")
        b_read = sp.sem("b_read")
        a_ready = sp.sem("a_ready")
        c_read = sp.sem("c_read")
        a_used = sp.sem("a_used")
        h_ready = sp.sem("h_ready")
        y_added = sp.sem("y_added")
        multiplied, dve_step = sp.sem("multiplied"), sp.sem("dve_step")
        block = ctx.enter_context(nc.Block())
        UNITS = KT * NCH

        def chunk(ch):
            return slice(ch * CH, (ch + 1) * CH)

        @block.sync
        def _(eng):
            for dst, src in ((skip[:], t.d_skip), (par[:, 0], t.log_a), (par[:, 3], t.b_b), (par[:, 4], t.b_c)):
                eng.dma_start(dst, src).then_inc(small_loaded, 16)
            for m in range(KT):
                eng.dma_start(raw[:, m], t.w_bc[0, m]).then_inc(raw_loaded[m], 16)
            with eng.Fori(0, N - 1) as n:
                for m in range(KT):
                    eng.wait_ge(w_ready, KT * n + m + 1)
                    eng.dma_start(raw[:, m], t.w_bc[ds(n + 1, 1), m].rearrange("a p k c -> (a p) k c")).then_inc(raw_loaded[m], 16)

        @block.tensor
        def _(eng):
            def exact(out, w_hi, w_lo, k, tok, first, last):
                nc.tensor.matmul(out, w_hi, hi[:, k, tok], start=first, stop=False)
                nc.tensor.matmul(out, w_hi, lo[:, k, tok], start=False, stop=False)
                return nc.tensor.matmul(out, w_lo, hi[:, k, tok], start=False, stop=last)

            eng.sem_inc(b_read, RING)
            eng.sem_inc(c_read, RING)
            with eng.Fori(0, N) as n:
                for m in range(KT):
                    eng.wait_ge(w_ready, KT * n + m + 1)
                    for ch in range(NCH):
                        i = m * NCH + ch
                        unit = UNITS * n + i
                        if m == 0:
                            eng.wait_ge(lo_ready, ch + 1)
                        for ps, read, ready, col in ((b_ps, b_read, b_ready, slice(0, P)), (c_ps, c_read, c_ready, slice(P, 2 * P))):
                            eng.wait_ge(read, unit + 1)
                            for k in range(KT):
                                mm = exact(ps[:, i % RING], w_hi[m][:, k, col], w_lo[m][:, k, col], k, chunk(ch), k == 0, k == KT - 1)
                            mm.then_inc(ready, 1)

        @block.scalar
        def _(eng):
            eng.sem_inc(a_used, RING)
            eng.sem_inc(y_added, RING)
            for ch in range(NCH):
                nc.scalar.copy(hi[:, :, chunk(ch)], u[:, :, chunk(ch)]).then_inc(hi_ready, 1)
                if ch == 0:
                    eng.wait_ge(small_loaded, 64)
                    nc.scalar.activation(par[:, 1], par[:, 0], ACT.Exp).then_inc(par_ready, 1)
            eng.wait_ge(skip_ready, 1)
            for m in range(KT):
                nc.scalar.activation(y[:, m], u[:, m], ACT.Copy, scale=skip[:, m:m + 1]).then_inc(y_ready, 1)
            with eng.Fori(0, N) as n:
                for m in range(KT):
                    eng.wait_ge(w_ready, KT * n + m + 1)
                    for ch in range(NCH):
                        i = m * NCH + ch
                        unit = UNITS * n + i
                        eng.wait_ge(a_used, unit + 1)
                        nc.scalar.activation(a[:, i % RING], dt[:, m, chunk(ch)], ACT.Exp,
                                             scale=cur[:, m, 1:2]).then_inc(a_ready, 1)
                        eng.wait_ge(c_ready, unit + 1)
                        eng.wait_ge(y_added, unit + 1)
                        nc.scalar.activation(cc[:, i % RING], c_ps[:, i % RING], ACT.Identity, bias=cur[:, m, 4:5],
                                             scale=cur[:, m, 2:3]).then_inc(c_read, 1)

        @block.gpsimd
        def _(eng):
            eng.wait_ge(y_ready, KT)

            def multiply(n, i):
                unit = UNITS * n + i
                eng.wait_ge(c_read, unit + 1 + RING)
                eng.wait_ge(h_ready, unit + 1)
                nc.gpsimd.tensor_tensor(cc[:, i % RING], cc[:, i % RING], h[:, i % RING], ALU.mult).then_inc(multiplied, 1)

            def states(n, last):
                for i in range(UNITS):
                    unit = UNITS * n + i
                    if i < UNITS - 1:
                        multiply(n, i + 1)
                    elif not last:
                        multiply(n + 1, 0)
                    part = y[:, i // NCH, chunk(i % NCH)]
                    eng.wait_ge(multiplied, unit + 1)
                    eng.wait_ge(y_added, unit + RING)
                    nc.gpsimd.tensor_tensor(part, part, cc[:, i % RING], ALU.add).then_inc(y_added, 1)

            multiply(0, 0)
            with eng.Fori(0, N - 1) as n:
                states(n, False)
            states(N - 1, True)

        @block.vector
        def _(eng):
            step = Steps(eng, dve_step)

            def split(n, m):
                step(nc.vector.tensor_scalar(cur[:, m].unsqueeze(2), par[:, :, m, ds(n, 1)], 1.0, None, ALU.mult))
                step(nc.vector.tensor_copy(w_hi[m][:], raw[:, m]))
                nc.vector.tensor_tensor(w_lo[m][:], raw[:, m], w_hi[m][:].bitcast(F32), ALU.subtract).then_inc(w_ready, 1)

            eng.wait_ge(small_loaded, 64)
            nc.vector.tensor_scalar(skip[:], skip[:], 1.0, None, ALU.add).then_inc(skip_ready, 1)
            eng.wait_ge(par_ready, 1)
            step(nc.vector.tensor_scalar(par[:, 1], par[:, 1], -1.0, None, ALU.mult))
            nc.vector.reciprocal(par[:, 2], par[:, 1]).then_inc(par_ready, 1)
            eng.wait_ge(par_ready, 2)
            nc.vector.tensor_tensor(par[:, 4], par[:, 4], par[:, 2], ALU.mult).then_inc(par_ready, 1)
            eng.wait_ge(par_ready, 3)
            eng.wait_ge(raw_loaded[0], 16)
            split(0, 0)
            for ch in range(NCH):
                eng.wait_ge(hi_ready, ch + 1)
                nc.vector.tensor_tensor(lo[:, :, chunk(ch)], u[:, :, chunk(ch)], hi[:, :, chunk(ch)].bitcast(F32),
                                        ALU.subtract).then_inc(lo_ready, 1)

            def states(n, last):
                for m in range(KT):
                    for ch in range(NCH):
                        i = m * NCH + ch
                        unit = UNITS * n + i
                        bu = inp[:, i % 2]
                        tok = chunk(ch)
                        eng.wait_ge(b_ready, unit + 1)
                        nc.vector.scalar_tensor_tensor(out=bu, in0=b_ps[:, i % RING], scalar=cur[:, m, 3:4],
                                                       in1=u[:, m, tok], op0=ALU.add, op1=ALU.mult).then_inc(b_read, 1)
                        eng.wait_ge(b_read, unit + 1 + RING)
                        eng.wait_ge(a_ready, unit + 1)
                        step(nc.vector.scalar_tensor_tensor(out=bu, in0=a[:, i % RING], scalar=1.0, in1=bu,
                                                            op0=ALU.subtract, op1=ALU.mult))
                        eng.wait_ge(y_added, unit + 1)
                        first = ch % (S // CH) == 0
                        nc.vector.tensor_tensor_scan(h[:, i % RING], a[:, i % RING], bu,
                                                     0.0 if first else h[:, (i - 1) % RING, CH - 1:CH],
                                                     ALU.mult, ALU.add).then_inc(h_ready, 1)
                        eng.wait_ge(h_ready, unit + 1)
                        eng.sem_inc(a_used, 1)
                        if ch == 1 and m == 0:
                            eng.wait_ge(raw_loaded[1], 16 * n + 16)
                            eng.wait_ge(c_read, UNITS * n + RING)
                            split(n, 1)
                        if ch == 1 and m == 1 and not last:
                            eng.wait_ge(raw_loaded[0], 16 * n + 32)
                            eng.wait_ge(c_read, UNITS * n + NCH + RING)
                            split(n + 1, 0)

            with eng.Fori(0, N - 1) as n:
                step.enter(n, UNITS + 2 * KT)
                states(n, False)
                step.leave(N - 1)
            states(N - 1, True)


E2 = 20
HG = D // 4
EB = NSP * E2


def phase_mixture(nc, t):
    with nc.cleanup_on_exit(), ExitStack() as ctx:
        sp = Space(nc, ctx, "moe")
        WS = 5
        ident, idb = sp.sb("ident", [P, P]), sp.sb("idb", [P, P], BF16)
        eps = sp.sb("eps", [P, 1])
        we_hi, we_lo = sp.sb("we_hi", [P, KT, E2 * D], F32R), sp.sb("we_lo", [P, KT, E2 * D], F32R)
        wraw = sp.sb("wraw", [P, WS, KT, CH])
        g1 = sp.sb("g1", [P, KT, P])
        g1_hi, g1_lo = sp.sb("g1_hi", [P, KT, P], F32R), sp.sb("g1_lo", [P, KT, P], F32R)
        b1 = sp.sb("b1", [HG, 1])
        g2 = sp.sb("g2", [HG, E2])
        b2 = sp.sb("b2", [P, E2])
        iota = sp.sb("iota", [P, E2])
        be = sp.sb("be", [EB, D])
        pick = sp.sb("pick", [EB, 3])
        bepart = sp.sb("bepart", [EB, 3, D], BF16)
        be_stack = sp.sb("be_stack", [EB, D], BF16)
        z = sp.sb("z", [P, KT, CH])
        x3 = [sp.sb(f"x3{s}", [P, TPC, D]) for s in range(2)]
        x_hi = [sp.sb(f"x_hi{s}", [P, KT, CH], F32R) for s in range(2)]
        x_lo = [sp.sb(f"x_lo{s}", [P, KT, CH], F32R) for s in range(2)]
        hT = sp.sb("hT", [HG, CH])
        pr = sp.sb("pr", [P, TPC, E2])
        red = sp.sb("red", [P, TPC])
        inv = sp.sb("inv", [P, TPC])
        top = sp.sb("top", [P, TPC, 8])
        topi = sp.sb("topi", [P, TPC, 8], U32)
        topf = sp.sb("topf", [P, TPC, 8])
        gate = [sp.sb(f"gate{s}", [P, TPC, E2]) for s in range(2)]
        gtmp = sp.sb("gtmp", [P, TPC, E2])
        gst = sp.sb("gst", [P, TPC, NSP, E2], BF16)
        gT = [sp.sb(f"gT{s}", [EB, CH], BF16) for s in range(2)]
        acc = sp.sb("acc", [P, 2, TPC, D])
        odd = sp.sb("odd", [P, 2, 2, D])
        term = sp.sb("term", [P, 2, 2, D])
        out = sp.sb("out", [P, TPC, D])
        stats, mv = sp.sb("stats", [P, 2, TPC, 6]), sp.sb("mv", [P, 2, TPC, 2])
        std, rstd = sp.sb("std", [P, 2, TPC]), sp.sb("rstd", [P, 2, TPC])
        ex = sp.psum("ex", [P, 4, CH])
        z_ps = sp.psum("z_ps", [P, CH])
        xT_ps = sp.psum("xT_ps", [P, CH])
        rt_ps = sp.psum("rt_ps", [P, CH])
        be_ps = sp.psum("be_ps", [P, CH])

        const_loaded, pool_set = sp.sem("const_loaded"), sp.sem("pool_set")
        wraw_loaded = [sp.sem(f"wraw_loaded{s}") for s in range(WS)]
        we_hi_ready = sp.sem("we_hi_ready")
        we_lo_ready = [sp.sem(f"we_lo_ready{s}") for s in range(2)]
        g1_ready, be_ready = sp.sem("g1_ready"), sp.sem("be_ready")
        z_loaded = sp.sem("z_loaded")
        z_ps_ready, z_read = sp.sem("z_ps_ready"), sp.sem("z_read")
        x3_ready = sp.sem("x3_ready")
        xT_ps_ready, x_hi_ready, x_lo_ready = sp.sem("xT_ps_ready"), sp.sem("x_hi_ready"), sp.sem("x_lo_ready")
        rt_ready, hid_ready, gT_ready = sp.sem("rt_ready"), sp.sem("hid_ready"), sp.sem("gT_ready")
        shifted, exp_ready, gst_ready = sp.sem("shifted"), sp.sem("exp_ready"), sp.sem("gst_ready")
        be_ps_ready, be_read = sp.sem("be_ps_ready"), sp.sem("be_read")
        ex_ready = sp.sem("ex_ready")
        even_read, odd_read = sp.sem("even_read"), sp.sem("odd_read")
        odd_added = sp.sem("odd_added")
        odd_used = sp.sem("odd_used")
        var_ready, std_ready = sp.sem("var_ready"), sp.sem("std_ready")
        out_ready, out_stored = sp.sem("out_ready"), sp.sem("out_stored")
        idb_ready, dve_step = sp.sem("idb_ready"), sp.sem("dve_step")
        block = ctx.enter_context(nc.Block())
        NW2 = E2 * D // CH
        HALF = NW2 // 2
        PAIRS = NCH // 2
        SLOTS = [(j, n) for j in range(TPC) for n in range(NW2)]


        @block.sync
        def _(eng):
            eng.sem_inc(out_stored, START)
            loads = ((ident, t.ident), (g1, t.g1), (b1, t.g1b), (g2, t.g2), (b2, t.g2b), (iota, t.iota),
                     (be, t.bmoe), (pick, t.pick20))

            def load(c):
                after(eng, z_ps_ready, 2 * c)
                eng.dma_start(z[:], t.z_sb[:, :, ds(c * CH, CH)]).then_inc(z_loaded, 16)

            load(0)
            for dst, src in loads:
                eng.dma_start(dst[:], src).then_inc(const_loaded, 16)
            for n in range(NW2):
                if n >= WS:
                    eng.wait_ge(we_lo_ready[(n - WS) % 2], (n - WS) // 2 + 1)
                eng.dma_start(wraw[:, n % WS], t.we[:, :, n * CH:(n + 1) * CH]).then_inc(wraw_loaded[n % WS], 16)
            load(1)

            def store(c):
                eng.wait_ge(out_ready, c + 1)
                eng.dma_start(t.out.rearrange("(n p) d -> p n d", p=P)[:, ds(c * TPC, TPC), :], out[:]).then_inc(out_stored, 16)

            with eng.Fori(0, NCH - 2) as c:
                load(c + 2)
                store(c)
            store(NCH - 2)
            store(NCH - 1)
            eng.wait_ge(out_stored, 16 * NCH + START)

        @block.gpsimd
        def _(eng):
            nc.gpsimd.memset(eps[:], EPS).then_inc(pool_set, 1)
            eng.sem_inc(odd_added, 3)

            for n in range(1, NW2, 2):
                eng.wait_ge(we_hi_ready, n + 1)
                if n > 1:
                    eng.wait_ge(we_lo_ready[1], n // 2)
                cols = slice(n * CH, (n + 1) * CH)
                nc.gpsimd.tensor_tensor(we_lo[:, :, cols], wraw[:, n % WS], we_hi[:, :, cols].bitcast(F32), ALU.subtract).then_inc(we_lo_ready[1], 1)

            with eng.Fori(0, NT // 2) as i:
                for s in range(2):
                    tile = 2 * i + s
                    for m in range(HALF):
                        if m < HALF - 1:
                            eng.wait_ge(odd_read, tile * HALF + m + 2 + 2)
                            if m > 0:
                                eng.wait_ge(odd_added, tile * HALF + m + 3)
                            nc.gpsimd.tensor_tensor(odd[:, s], odd[:, s], term[:, m % 2], ALU.add).then_inc(odd_added, 1)
                        else:
                            eng.wait_ge(odd_added, tile * HALF + m + 3)
                            nc.gpsimd.tensor_tensor(odd[:, s, 0], odd[:, s, 0], odd[:, s, 1], ALU.add).then_inc(odd_added, 1)

        @block.tensor
        def _(eng):
            eng.wait_ge(const_loaded, 16 * 8)
            eng.wait_ge(idb_ready, 1)

            def turn_z(c, half):
                if half == 0:
                    eng.wait_ge(z_loaded, 16 * c + 16)
                after(eng, z_read, 2 * c + half)
                for j in range(2):
                    for k in range(KT):
                        tok = slice((2 * half + j) * P, (2 * half + j + 1) * P)
                        mm = nc.tensor.transpose(z_ps[:, (j * KT + k) * P:(j * KT + k + 1) * P], z[:, k, tok], ident[:])
                mm.then_inc(z_ps_ready, 1)

            def turn_x(c, s, k):
                if k == 0:
                    eng.wait_ge(x3_ready, c + 1)
                after(eng, x_lo_ready, KT * c + k)
                for j in range(TPC):
                    mm = nc.tensor.transpose(xT_ps[:, j * P:(j + 1) * P], x3[s][:, j, k * P:(k + 1) * P], ident[:])
                mm.then_inc(xT_ps_ready, 1)

            def hidden(c, s):
                eng.wait_ge(g1_ready, 1)
                eng.wait_ge(x_lo_ready, KT * (c + 1))
                after(eng, gT_ready, c)
                for k in range(KT):
                    nc.tensor.matmul(rt_ps[:], g1_hi[:, k], x_hi[s][:, k], start=k == 0, stop=False)
                    nc.tensor.matmul(rt_ps[:], g1_hi[:, k], x_lo[s][:, k], start=False, stop=False)
                    mm = nc.tensor.matmul(rt_ps[:], g1_lo[:, k], x_hi[s][:, k], start=False, stop=k == KT - 1)
                mm.then_inc(rt_ready, 1)

            def logits(c):
                eng.wait_ge(hid_ready, c + 1)
                for j in range(TPC):
                    mm = nc.tensor.matmul(rt_ps[:, j * E2:(j + 1) * E2], hT[:, j * P:(j + 1) * P], g2[:], start=True, stop=True)
                mm.then_inc(rt_ready, 1)

            def turn_gates(c):
                eng.wait_ge(gst_ready, c + 1)
                for j in range(TPC):
                    mm = nc.tensor.transpose(rt_ps[0:EB, j * P // 2:(j + 1) * P // 2].bitcast(BF16),
                                             gst[:, j].rearrange("p a e -> p (a e)"), idb[:])
                mm.then_inc(rt_ready, 1)

            def experts(c, s, j, n):
                tok = slice(j * P, (j + 1) * P)
                if n == 0:
                    if j == 0:
                        eng.wait_ge(gT_ready, c + 1)
                        eng.wait_ge(be_ready, 1)
                    after(eng, be_read, TPC * c + j)
                    nc.tensor.matmul(be_ps[:, 0:D], gT[s][:, tok], be_stack[:], start=True, stop=True).then_inc(be_ps_ready, 1)
                if isinstance(c, int) and c == 0 and j == 0:
                    eng.wait_ge(we_lo_ready[n % 2], n // 2 + 1)
                eng.wait_ge(odd_read if n % 2 else even_read, (TPC * c + j) * HALF + n // 2 + 1)
                bank = (j * NW2 + n) % 4
                cols = slice(n * CH, (n + 1) * CH)
                for k in range(KT):
                    nc.tensor.matmul(ex[:, bank], x_hi[s][:, k, tok], we_hi[:, k, cols], start=k == 0, stop=False)
                    nc.tensor.matmul(ex[:, bank], x_hi[s][:, k, tok], we_lo[:, k, cols], start=False, stop=False)
                    mm = nc.tensor.matmul(ex[:, bank], x_lo[s][:, k, tok], we_hi[:, k, cols], start=False, stop=k == KT - 1)
                mm.then_inc(ex_ready, 1)

            for half in range(2):
                turn_z(0, half)
            for k in range(KT):
                turn_x(0, 0, k)
            hidden(0, 0)
            logits(0)
            turn_gates(0)

            def chunks(i, last):
                for s in range(2):
                    c = 2 * i + s
                    more = not (last and s == 1)
                    for at in SLOTS:
                        if more and at in ((0, 0), (0, 2)):
                            turn_z(c + 1, at[1] // 2)
                        if more and at in ((1, 2), (1, 6)):
                            turn_x(c + 1, 1 - s, at[1] // 4)
                        if more and at == (2, 0):
                            hidden(c + 1, 1 - s)
                        if more and at == (2, 4):
                            logits(c + 1)
                        if more and at == (3, 4):
                            turn_gates(c + 1)
                        experts(c, s, *at)

            chunks(0, False)
            with eng.Fori(0, PAIRS - 2) as i:
                chunks(i + 1, False)
            chunks(PAIRS - 1, True)

        @block.scalar
        def _(eng):
            eng.sem_inc(odd_read, 2)

            def split_weights(n):
                eng.wait_ge(wraw_loaded[n % WS], 16 * (n // WS + 1))
                nc.scalar.copy(we_hi[:, :, n * CH:(n + 1) * CH], wraw[:, n % WS]).then_inc(we_hi_ready, 1)

            def deviation(count, which):
                eng.wait_ge(var_ready, count)
                nc.scalar.activation(std[:, which], mv[:, which, :, 1], ACT.Sqrt, bias=eps[:]).then_inc(std_ready, 1)

            def round_x(c, s, k):
                eng.wait_ge(xT_ps_ready, KT * c + k + 1)
                nc.scalar.copy(x_hi[s][:, k], xT_ps[:]).then_inc(x_hi_ready, 1)

            def gelu(c):
                eng.wait_ge(rt_ready, 3 * c + 1)
                nc.scalar.activation(hT[:], rt_ps[0:HG], ACT.Gelu, bias=b1[:]).then_inc(hid_ready, 1)

            def exponentials(c):
                eng.wait_ge(shifted, c + 1)
                nc.scalar.activation(pr[:], pr[:], ACT.Exp).then_inc(exp_ready, 1)

            def turned(c, s):
                eng.wait_ge(rt_ready, 3 * c + 3)
                nc.scalar.copy(gT[s][:], rt_ps[0:EB, 0:CH // 2].bitcast(BF16)).then_inc(gT_ready, 1)

            def scale(c, s, j, n):
                tile = TPC * c + j
                m = (n - 3) // 2
                if n == 1:
                    eng.wait_ge(odd_used, tile + 1)
                    dst = odd[:, j % 2]
                else:
                    eng.wait_ge(odd_added, tile * HALF + m + (1 if m < 2 else 2))
                    dst = term[:, m % 2]
                eng.wait_ge(ex_ready, tile * NW2 + n + 1)
                for a in range(2):
                    ins = nc.scalar.activation(dst[:, a], ex[:, (j * NW2 + n) % 4, a * D:(a + 1) * D], ACT.Copy,
                                               scale=gate[s][:, j, 2 * n + a:2 * n + a + 1])
                ins.then_inc(odd_read, 1)

            eng.wait_ge(pool_set, 1)
            split_weights(0)
            deviation(1, slice(0, 1))
            split_weights(1)
            split_weights(2)
            for k in range(KT):
                round_x(0, 0, k)
            split_weights(3)
            split_weights(4)
            gelu(0)
            split_weights(5)
            exponentials(0)
            for n in range(6, NW2):
                split_weights(n)
            turned(0, 0)

            def chunks(i, first, last):
                for s in range(2):
                    c = 2 * i + s
                    more, before = not (last and s == 1), not (first and s == 0)
                    for at in SLOTS:
                        if at[1] % 2:
                            scale(c, s, *at)
                        if at == (0, 4):
                            deviation(c + 2, slice(0 if more else 1, 2 if before else 1))
                        if more and at in ((1, 3), (1, 6)):
                            round_x(c + 1, 1 - s, at[1] // 3 - 1)
                        if more and at == (2, 1):
                            gelu(c + 1)
                        if more and at == (2, 6):
                            exponentials(c + 1)
                        if more and at == (3, 5):
                            turned(c + 1, 1 - s)

            chunks(0, True, False)
            with eng.Fori(0, PAIRS - 2) as i:
                chunks(i + 1, False, False)
            chunks(PAIRS - 1, False, True)
            deviation(NCH + 2, slice(1, 2))

        @block.vector
        def _(eng):
            step = Steps(eng, dve_step)
            eng.sem_inc(even_read, 2)
            eng.sem_inc(odd_used, 2)

            def read_z(c, s, half):
                eng.wait_ge(z_ps_ready, 2 * c + half + 1)
                for j in range(2):
                    ins = nc.vector.bn_stats(stats[:, 0, 2 * half + j], z_ps[:, j * D:(j + 1) * D])
                step(ins)
                nc.vector.tensor_copy(x3[s][:, 2 * half:2 * half + 2], z_ps[:].rearrange("p (j d) -> p j d", j=2)).then_inc(z_read, 1)

            def variances(which):
                eng.drain()
                for a in which:
                    for j in range(TPC):
                        ins = nc.vector.bn_aggr(mv[:, a, j], stats[:, a, j])
                ins.then_inc(var_ready, 1)

            def deviations(count, which):
                eng.wait_ge(std_ready, count)
                step(nc.vector.reciprocal(rstd[:, which], std[:, which]))

            def normalise(c, s, j):
                for n in range(j, j + 2):
                    ins = nc.vector.tensor_scalar(x3[s][:, n], x3[s][:, n], mv[:, 0, n, 0:1], rstd[:, 0, n:n + 1], ALU.subtract, ALU.mult)
                if j == 2:
                    ins.then_inc(x3_ready, 1)
                else:
                    step(ins)

            def round_x(c, s, k):
                eng.wait_ge(x_hi_ready, KT * c + k + 1)
                nc.vector.tensor_tensor(x_lo[s][:, k], xT_ps[:], x_hi[s][:, k].bitcast(F32), ALU.subtract).then_inc(x_lo_ready, 1)

            def shift(c):
                eng.wait_ge(rt_ready, 3 * c + 2)
                step(nc.vector.tensor_tensor(pr[:], rt_ps[:, 0:TPC * E2].rearrange("p (j e) -> p j e", j=TPC),
                                             b2[:].unsqueeze(1).to_broadcast([P, TPC, E2]), ALU.add))
                step(nc.vector.tensor_reduce(red[:], pr[:], AX, ALU.max))
                nc.vector.tensor_tensor(pr[:], pr[:], red[:].unsqueeze(2).to_broadcast([P, TPC, E2]), ALU.subtract).then_inc(shifted, 1)

            over = lambda x: x.unsqueeze(2).to_broadcast([P, TPC, E2])
            several = lambda x, n: x.unsqueeze(2).to_broadcast([P, TPC, n, E2])
            places = iota[:].unsqueeze(1).to_broadcast([P, TPC, E2])

            def largest(c):
                eng.wait_ge(exp_ready, c + 1)
                step(nc.vector.tensor_reduce(red[:], pr[:], AX, ALU.add))
                step(nc.vector.reciprocal(inv[:], red[:]))
                nc.vector.tensor_tensor(pr[:], pr[:], over(inv[:]), ALU.mult)
                eng.drain()
                for j in range(TPC):
                    nc.vector.max(top[:, j], pr[:, j])
                eng.drain()
                for j in range(TPC):
                    ins = nc.vector.max_index(topi[:, j], top[:, j], pr[:, j])
                step(ins)

            def gates(c, s):
                step(nc.vector.tensor_copy(topf[:], topi[:]))
                step.go(nc.vector.tensor_tensor(gate[s][:], places, over(topf[:, :, 0]), ALU.is_equal))
                step(nc.vector.tensor_tensor(gtmp[:], places, over(topf[:, :, 1]), ALU.is_equal))
                step.go(nc.vector.tensor_tensor(gate[s][:], gate[s][:], over(top[:, :, 0]), ALU.mult))
                step(nc.vector.tensor_tensor(gtmp[:], gtmp[:], over(top[:, :, 1]), ALU.mult))
                step(nc.vector.tensor_tensor(gate[s][:], gate[s][:], gtmp[:], ALU.add))

            def gate_parts(c, s):
                step(nc.vector.tensor_copy(gst[:, :, 0:3], several(gate[s][:], 3)))
                step(nc.vector.tensor_tensor(gtmp[:], gate[s][:], gst[:, :, 0], ALU.subtract))
                step(nc.vector.tensor_copy(gst[:, :, 3:5], several(gtmp[:], 2)))
                nc.vector.tensor_tensor(gst[:, :, 5], gtmp[:], gst[:, :, 3], ALU.subtract).then_inc(gst_ready, 1)
                eng.wait_ge(gst_ready, c + 1)

            def even(c, s, j, n):
                tile = TPC * c + j
                total = acc[:, s, j]
                if n == 0:
                    eng.wait_ge(be_ps_ready, tile + 1)
                    nc.vector.tensor_tensor(total, be_ps[:, 0:D], x3[s][:, j], ALU.add).then_inc(be_read, 1)
                    eng.wait_ge(be_read, tile + 1)
                eng.wait_ge(ex_ready, tile * NW2 + n + 1)
                if n > 0:
                    eng.wait_ge(even_read, tile * HALF + n // 2 + 2)
                for a in range(2):
                    ins = nc.vector.scalar_tensor_tensor(out=total, in0=ex[:, (j * NW2 + n) % 4, a * D:(a + 1) * D],
                                                         scalar=gate[s][:, j, 2 * n + a:2 * n + a + 1],
                                                         in1=total, op0=ALU.mult, op1=ALU.add)
                    if a == 0:
                        step(ins)
                ins.then_inc(even_read, 1)

            def finish(c, s, j):
                tile = TPC * c + j
                total = acc[:, s, j]
                eng.wait_ge(even_read, (tile + 1) * HALF + 2)
                eng.wait_ge(odd_added, (tile + 1) * HALF + 3)
                step(nc.vector.tensor_tensor(total, total, odd[:, j % 2, 0], ALU.add))
                eng.sem_inc(odd_used, 1)
                nc.vector.bn_stats(stats[:, 1, j], total)

            def write_out(c, s, j):
                if j == 0:
                    eng.wait_ge(out_stored, 16 * c + START)
                ins = nc.vector.tensor_scalar(out[:, j], acc[:, s, j], mv[:, 1, j, 0:1], rstd[:, 1, j:j + 1], ALU.subtract, ALU.mult)
                if j == TPC - 1:
                    ins.then_inc(out_ready, 1)
                else:
                    step(ins)

            def split_weights(n):
                eng.wait_ge(we_hi_ready, n + 1)
                cols = slice(n * CH, (n + 1) * CH)
                nc.vector.tensor_tensor(we_lo[:, :, cols], wraw[:, n % WS], we_hi[:, :, cols].bitcast(F32), ALU.subtract).then_inc(we_lo_ready[0], 1)

            eng.wait_ge(const_loaded, 16 * 8)
            nc.vector.tensor_copy(idb[:], ident[:]).then_inc(idb_ready, 1)
            step(nc.vector.tensor_copy(g1_hi[:], g1[:]))
            nc.vector.tensor_tensor(g1_lo[:], g1[:], g1_hi[:].bitcast(F32), ALU.subtract).then_inc(g1_ready, 1)
            for half in range(2):
                read_z(0, 0, half)
            variances((0,))
            split_weights(0)
            deviations(1, 0)
            for j in (0, 2):
                normalise(0, 0, j)
            split_weights(2)
            for k in range(KT):
                round_x(0, 0, k)
            split_weights(4)
            step(nc.vector.tensor_copy(bepart[:, 0], be[:]))
            step(nc.vector.tensor_tensor(be[:], be[:], bepart[:, 0], ALU.subtract))
            step(nc.vector.tensor_copy(bepart[:, 1], be[:]))
            step(nc.vector.tensor_tensor(bepart[:, 2], be[:], bepart[:, 1], ALU.subtract))
            step(nc.vector.tensor_scalar(be[:], bepart[:, 0], pick[:, 0:1], None, ALU.mult))
            step(nc.vector.scalar_tensor_tensor(out=be[:], in0=bepart[:, 1], scalar=pick[:, 1:2], in1=be[:], op0=ALU.mult, op1=ALU.add))
            nc.vector.scalar_tensor_tensor(out=be_stack[:], in0=bepart[:, 2], scalar=pick[:, 2:3], in1=be[:],
                                           op0=ALU.mult, op1=ALU.add).then_inc(be_ready, 1)
            shift(0)
            largest(0)
            gates(0, 0)
            gate_parts(0, 0)
            split_weights(6)
            split_weights(8)

            def chunks(i, first, last):
                for s in range(2):
                    c = 2 * i + s
                    more, before = not (last and s == 1), not (first and s == 0)
                    which = range(0 if more else 1, 2 if before else 1)
                    for at in SLOTS:
                        j, n = at
                        if n % 2 == 0:
                            even(c, s, j, n)
                        if n == 1 and j > 0:
                            finish(c, s, j - 1)
                        if n == 1 and j == 0 and before:
                            finish(c - 1, 1 - s, TPC - 1)
                        if more and at in ((0, 0), (0, 2)):
                            read_z(c + 1, 1 - s, n // 2)
                        if at == (0, 4):
                            variances(which)
                        if at == (0, 6):
                            deviations(c + 2, slice(which[0], which[-1] + 1))
                        if more and at in ((0, 6), (0, 7)):
                            normalise(c + 1, 1 - s, 2 * n - 12)
                        if before and at in ((0, 8), (0, 9), (1, 0), (1, 2)):
                            write_out(c - 1, 1 - s, ((0, 8), (0, 9), (1, 0), (1, 2)).index(at))
                        if more and at in ((1, 4), (1, 7)):
                            round_x(c + 1, 1 - s, n // 3 - 1)
                        if more and at == (2, 5):
                            shift(c + 1)
                        if more and at == (2, 8):
                            largest(c + 1)
                        if more and at == (2, 9):
                            gates(c + 1, 1 - s)
                        if more and at == (3, 0):
                            gate_parts(c + 1, 1 - s)

            chunks(0, True, False)
            with eng.Fori(0, PAIRS - 2) as i:
                step.enter(i, 2 * (TPC * HALF + 2 + 1 + 1 + 3 + 2 + 3 + 6 + 3 + TPC))
                chunks(i + 1, False, False)
                step.leave(PAIRS - 2)
            chunks(PAIRS - 1, False, True)
            finish(NCH - 1, 1, TPC - 1)
            variances((1,))
            deviations(NCH + 2, slice(1, 2))
            for j in range(TPC):
                write_out(NCH - 1, 1, j)


def host_layout(v):
    import numpy as np

    v = {k: np.asarray(a) for k, a in v.items()}
    f = np.float32

    def cols(w):
        return np.ascontiguousarray(w.reshape(-1, P, w.shape[1]).transpose(1, 0, 2))

    def rows(b):
        return np.ascontiguousarray(b.reshape(-1, P).T)

    def every(b):
        return np.ascontiguousarray(np.broadcast_to(b.reshape(1, -1), (P, b.size)))

    x = v["L0_attn_x"].reshape(NTOK, D)
    a = {}
    a["x"] = x
    a["xT"] = cols(x.T)
    a["wqkv"] = cols(v["L0_attn_W_w"].T)
    a["bqk"] = rows(v["L0_attn_W_b"][:2 * D])
    a["bv"] = every(v["L0_attn_W_b"][2 * D:])
    a["rpb"] = v["L0_attn_rpb"].T
    a["rpb_back"] = v["L0_attn_rpb"].T[:, ::-1]
    eye = np.eye(P, dtype=f)
    a["ident"] = eye
    hidden = np.where(np.arange(P)[None, :] > np.arange(P)[:, None], f(-1e30), f(0))
    a["squares"] = np.stack([eye, eye[::-1], hidden, hidden.T], axis=1)
    a["wproj"] = cols(v["L0_attn_proj_w"].T)
    a["bproj"] = every(v["L0_attn_proj_b"])
    a["ln_g"] = every(v["L0_attn_ln_g"])
    a["ln_b"] = every(v["L0_attn_ln_b"])
    a["keep"] = every(np.array([float((c + 1) % (S // CH) != 0) for c in range(NCH)], f))
    stack = lambda w: w.transpose(1, 0, 2).reshape(D, KR)
    router = v["L0_ffn_router_w1"].T
    a["wq"], a["wk"], a["winv"] = cols(v["L0_ffn_W_Q"]), cols(v["L0_ffn_W_K"]), cols(v["L0_ffn_W_inv"])
    two = lambda f0, f1: np.stack([cols(f0), cols(f1)], axis=1)
    a["vq"] = two(np.concatenate([stack(v["L0_ffn_V_fwd"]), router], 1), np.concatenate([stack(v["L0_ffn_W_inv_exp"]), router], 1))
    a["vk"] = two(stack(v["L0_ffn_W_fwd"]), stack(v["L0_ffn_V_inv"]))
    a["u"] = two(stack(v["L0_ffn_U_fwd"]), stack(v["L0_ffn_U_inv"]))
    a["wo"] = cols(v["L0_ffn_W_O"].T)
    a["bffn"] = cols(np.tile(np.concatenate([v["L0_ffn_b_fwd"], v["L0_ffn_b_inv"]]).T, (1, NSP)))
    a["alpha"] = np.broadcast_to(v["L0_ffn_alpha_bi"].reshape(1, 1), (P, 1))
    a["alphas"] = np.tile(np.concatenate([np.ones(KE, f), np.broadcast_to(v["L0_ffn_alpha_bi"].reshape(1), (KE,))]), NSP)[:, None]
    left, right = (0, 0, 0, 1, 1, 2), (0, 1, 2, 0, 1, 0)

    def picked(width):
        return np.repeat(np.eye(3, dtype=f)[list(right)], width, axis=0)

    a["pick"] = picked(NW)
    a["w2"] = cols(v["L0_ffn_router_w2"].T)
    a["b1"] = rows(v["L0_ffn_router_b1"])
    a["b2"] = every(v["L0_ffn_router_b2"])
    a["be"] = every(v["L0_ffn_expert_bias"])
    sel = np.zeros((NSP, 2, KE, NG, P), f)
    for g in range(NG):
        for p in range(P):
            sel[[0, 3, 5], g // GB, g % GB * (P // R) + p // R, g, p] = 1
    a["sel"] = sel.reshape(NSP * NW, NG, P)
    a["count"] = np.ascontiguousarray(np.tile(np.arange(1, S + 1, dtype=f), B).reshape(NT, P).T)
    a["w_dt"] = cols(v["L1_attn_W_dt"].T)
    a["b_dt"], a["dt_bias"], a["d_skip"] = rows(v["L1_attn_b_dt"]), rows(v["L1_attn_dt_bias"]), rows(v["L1_attn_D_skip"])
    blocks = lambda b: b.reshape(KT, P, N).transpose(1, 0, 2)
    a["log_a"] = blocks(v["L1_attn_log_A"])
    a["b_b"], a["b_c"] = blocks(v["L1_attn_b_B"]), blocks(v["L1_attn_b_C"])
    wbc = np.stack([w.reshape(KT, P, N, KT, P) for w in (v["L1_attn_W_B"], v["L1_attn_W_C"])])
    a["w_bc"] = wbc.transpose(3, 1, 5, 4, 0, 2).reshape(N, KT, P, KT, 2 * P)
    a["g1"] = cols(np.concatenate([v["L1_ffn_wg1"], np.zeros((D, P - HG), f)], 1))
    a["g1b"] = v["L1_ffn_bg1"][:, None]
    a["g2"] = v["L1_ffn_wg2"][:, :E2]
    a["g2b"] = every(v["L1_ffn_bg2"][:E2])
    a["iota"] = every(np.arange(E2, dtype=f))
    a["bmoe"] = np.tile(v["L1_ffn_be"], (NSP, 1))
    a["pick20"] = picked(E2)
    a["we"] = v["L1_ffn_We"].transpose(1, 0, 2).reshape(KT, P, E2 * D).transpose(1, 0, 2)
    return {k: np.ascontiguousarray(w) for k, w in a.items()}


def open_fused(nc, ctx, t):
    sp = Space(nc, ctx, "fus")
    t.aq_hi, t.aq_lo = sp.sb("aq_hi", [P, 2, KT, WF], F32R), sp.sb("aq_lo", [P, 2, KT, WF], F32R)
    t.ak_hi, t.ak_lo = sp.sb("ak_hi", [P, 2, KT, KR], F32R), sp.sb("ak_lo", [P, 2, KT, KR], F32R)
    t.uo = sp.sb("uo", [P, NG, D])
    t.bo_stack = sp.sb("bo_stack", [NSP * NW, D], BF16)
    t.router2, t.routerb = sp.sb("router2", [P, KT, KE]), sp.sb("routerb", [P, KT])
    t.logitb = sp.sb("logitb", [P, KE])
    t.sel_sb = sp.sb("sel", [NSP * NW, NG, P], BF16)
    t.count_sb = sp.sb("count", [P, NT])
    t.wdt_hi, t.wdt_lo = sp.sb("wdt_hi", [P, KT, D], F32R), sp.sb("wdt_lo", [P, KT, D], F32R)
    t.dt_bias_sb = sp.sb("dt_bias", [P, KT])


class Tensors:
    pass


def declare(nc, arrays):
    def array(name):
        a = arrays[name]
        return nc.dram_tensor(f"in_{name}", a.shape, mybir.dt.from_np(a.dtype), kind="ExternalInput").ap()

    t = Tensors()
    t.x = array("x")
    t.xT = array("xT")
    t.wqkv = array("wqkv")
    t.bqk = array("bqk")
    t.bv = array("bv")
    t.rpb = array("rpb")
    t.rpb_back = array("rpb_back")
    t.ident = array("ident")
    t.squares = array("squares")
    t.wproj = array("wproj")
    t.bproj = array("bproj")
    t.ln_g = array("ln_g")
    t.ln_b = array("ln_b")
    t.keep = array("keep")
    t.wq = array("wq")
    t.wk = array("wk")
    t.winv = array("winv")
    t.vq = array("vq")
    t.vk = array("vk")
    t.u = array("u")
    t.wo = array("wo")
    t.bffn = array("bffn")
    t.alpha = array("alpha")
    t.alphas = array("alphas")
    t.pick = array("pick")
    t.w2 = array("w2")
    t.b1 = array("b1")
    t.b2 = array("b2")
    t.be = array("be")
    t.sel = array("sel")
    t.count = array("count")
    t.w_dt = array("w_dt")
    t.b_dt = array("b_dt")
    t.dt_bias = array("dt_bias")
    t.d_skip = array("d_skip")
    t.log_a = array("log_a")
    t.b_b = array("b_b")
    t.b_c = array("b_c")
    t.w_bc = array("w_bc")
    t.g1 = array("g1")
    t.g1b = array("g1b")
    t.g2 = array("g2")
    t.g2b = array("g2b")
    t.iota = array("iota")
    t.bmoe = array("bmoe")
    t.pick20 = array("pick20")
    t.we = array("we")
    return t


def program(nc, t):
    t.qk = nc.dram_tensor("qk_parts", (2, 3, D, NTOK), BF16).ap()
    t.qk4 = t.qk.rearrange("s a (h r) n -> s a h r n", r=HD)
    t.tables = nc.dram_tensor("bias_tables", (4, H, EW), BF16).ap()
    t.x1 = nc.dram_tensor("x1", (NTOK, D), F32).ap()
    t.x1T = nc.dram_tensor("x1T", (P, KT, NTOK), F32).ap()
    t.cumT = nc.dram_tensor("x1T_sums", (P, KT, NTOK), F32).ap()
    with ExitStack() as ctx:
        t.z_sb = Space(nc, ctx, "ssm_out").sb("z", [P, KT, NTOK])
        with ExitStack() as ctx_scan:
            sp = Space(nc, ctx_scan, "ssm_in")
            t.u_sb, t.dt_sb = sp.sb("u", [P, KT, NTOK]), sp.sb("dt", [P, KT, NTOK])
            t.v_sb, t.o_sb = Region(t.z_sb)(NT, D), Region(t.u_sb)(NT, D)
            place_folded(t)
            phase_qkv(nc, t)
            phase_attention(nc, t)
            phase_project(nc, t)
            with ExitStack() as ctx_fused:
                open_fused(nc, ctx_fused, t)
                phase_combine(nc, t)
                phase_fused(nc, t)
            phase_scan(nc, t)
        phase_mixture(nc, t)


def kernel(**inputs):
    import numpy as np
    import concourse.bacc as bacc
    from concourse.bass_utils import run_bass_kernel_spmd

    arrays = host_layout(inputs)
    nc = bacc.Bacc("TRN2", target_bir_lowering=False, num_devices=1)
    t = declare(nc, arrays)
    t.out = nc.dram_tensor("out", (NTOK, D), F32, kind="ExternalOutput").ap()
    program(nc, t)
    r = run_bass_kernel_spmd(nc, [{f"in_{k}": a for k, a in arrays.items()}], core_ids=[0])
    return np.asarray(r.results[0]["out"]).reshape(B, S, D)
```
